# Optimizing a Trainium2 kernel written in Bass

```python
import numpy as np
import jax
import jax.numpy as jnp

def _softmax(x, axis=-1):
    return jax.nn.softmax(x, axis=axis)

def _gelu(x):
    return jax.nn.gelu(x, approximate=True)

def _silu(x):
    return jax.nn.silu(x)

def _sigmoid(x):
    return jax.nn.sigmoid(x)

def _layernorm(x, axis=-1, eps=1e-05):
    m = jnp.mean(x, axis=axis, keepdims=True)
    v = jnp.var(x, axis=axis, keepdims=True)
    return (x - m) / jnp.sqrt(v + eps)

def _scatter_add(tgt, idx, src, axis=0):
    return tgt.at[idx].add(src)

def _segment_sum(src, seg, n):
    return jax.ops.segment_sum(src, seg, n)
kernel_name = 'mk_gnn_preln_d4_gnn_r32_b45ae2'

def setup_inputs(seed: int=0):
    np.random.seed(seed)
    _w = jnp.asarray

    def _rec_inputs():
        import jax
        import jax.numpy as jnp
        _gk = jax.random.key(seed)
        x = -0.000202 + 1 * jax.random.normal(jax.random.fold_in(_gk, 1), (3125, 128), jnp.float32)
        _s = jax.random.randint(jax.random.fold_in(_gk, 2), (25000,), 0, 3125, jnp.int32)
        _d = jax.random.randint(jax.random.fold_in(_gk, 3), (25000,), 0, 3125, jnp.int32)
        _loop = jnp.arange(3125, dtype=jnp.int32)
        src = jnp.concatenate([_s, _d, _loop])
        dst = jnp.concatenate([_d, _s, _loop])
        _o = jnp.argsort(dst, stable=True)
        src = src[_o]
        dst = dst[_o]
        edge_attr_128 = -2.25437e-05 + 0.999858 * jax.random.normal(jax.random.fold_in(_gk, 11), (53125, 128), jnp.float32)
        edge_type_8 = jax.random.randint(jax.random.fold_in(_gk, 13), (53125,), 0, 8, jnp.int32)
        return (x, src, dst, edge_attr_128, edge_type_8)
    x, src, dst, edge_attr_128, edge_type_8 = _rec_inputs()

    def _L0_gnn_setup():
        import jax, jax.numpy as jnp
        import numpy as np
        N_NODES = 50000
        key = jax.random.key(seed)
        k1, k2 = jax.random.split(key)
        x = jax.random.normal(k1, (N_NODES, 128), dtype=jnp.float32)
        edge_index = jax.random.randint(k2, (2, 20000), 0, N_NODES, dtype=jnp.int64)
        return {'x': x, 'edge_index': edge_index}
    _L0_gnn_all = _L0_gnn_setup()
    _L0_gnn_in = {k: v for k, v in _L0_gnn_all.items() if k in ()}
    del _L0_gnn_all

    def _L1_gnn_setup():
        import jax, jax.numpy as jnp
        import numpy as np
        N_NODES = 50000
        N_EDGES = 15625
        D = 128
        R = 8
        L = 2
        BN_EPS = 1e-05

        def _rgcn_edge_conv(h, xe, src, dst, etype, w, rt, b):
            m = jax.nn.relu(h[src] + xe)
            n = h.shape[0]
            seg = etype * n + dst
            sums = jax.ops.segment_sum(m, seg, num_segments=R * n)
            cnt = jax.ops.segment_sum(jnp.ones((m.shape[0],), m.dtype), seg, num_segments=R * n)
            mean = sums / jnp.maximum(cnt, 1.0)[:, None]
            hr = mean.reshape(R, n, -1)
            out = jnp.einsum('rnd,rdo->no', hr, w)
            out = out + h @ rt + b
            return out

        def _batch_norm(h, gamma, beta):
            mu = h.mean(axis=0)
            var = jnp.mean((h - mu) ** 2, axis=0)
            return (h - mu) * jax.lax.rsqrt(var + BN_EPS) * gamma + beta
        key = jax.random.key(seed)
        ks = jax.random.split(key, 8)
        x = jax.random.normal(ks[0], (N_NODES, D), dtype=jnp.float32)
        xe = jax.random.normal(ks[1], (N_EDGES, D), dtype=jnp.float32)
        edge_index = jax.random.randint(ks[2], (2, N_EDGES), 0, N_NODES, dtype=jnp.int64)
        edge_type = jax.random.randint(ks[3], (N_EDGES,), 0, R, dtype=jnp.int64)
        w_scale = jnp.sqrt(6.0 / (D + D))
        weight = jax.random.uniform(ks[4], (L, R, D, D), jnp.float32, -w_scale, w_scale)
        root = jax.random.uniform(ks[5], (L, D, D), jnp.float32, -w_scale, w_scale)
        bias = jnp.zeros((L, D), jnp.float32)
        bn_gamma = jnp.ones((L, D), jnp.float32)
        bn_beta = jnp.zeros((L, D), jnp.float32)
        return {'x': x, 'xe': xe, 'edge_index': edge_index, 'edge_type': edge_type, 'weight': weight, 'root': root, 'bias': bias, 'bn_gamma': bn_gamma, 'bn_beta': bn_beta}
    _L1_gnn_all = _L1_gnn_setup()
    _L1_gnn_in = {k: v for k, v in _L1_gnn_all.items() if k in ('weight', 'root', 'bias', 'bn_gamma', 'bn_beta')}
    del _L1_gnn_all

    def _L2_gnn_setup():
        import jax, jax.numpy as jnp
        import numpy as np
        N_NODES = 3125
        N_EDGES = 50000
        D = 128
        EPS = 1e-05
        key = jax.random.key(seed)
        k1, k2, k3 = jax.random.split(key, 3)
        x = jax.random.normal(k1, (N_NODES, D), dtype=jnp.float32)
        edge_index = jax.random.randint(k2, (2, N_EDGES), 0, N_NODES, dtype=jnp.int64)
        W = jax.random.normal(k3, (D, D), dtype=jnp.float32) * (1.0 / np.sqrt(D))
        b = jnp.zeros((D,), dtype=jnp.float32)
        gamma = jnp.ones((D,), dtype=jnp.float32)
        beta = jnp.zeros((D,), dtype=jnp.float32)
        return {'x': x, 'edge_index': edge_index, 'W': W, 'b': b, 'gamma': gamma, 'beta': beta}
    _L2_gnn_all = _L2_gnn_setup()
    _L2_gnn_in = {k: v for k, v in _L2_gnn_all.items() if k in ('W', 'b', 'gamma', 'beta')}
    del _L2_gnn_all

    def _L3_gnn_setup():
        import jax, jax.numpy as jnp
        import numpy as np
        N = 50000
        E = 25000
        IN = 128
        HID = 32
        HEADS = 4
        OUT = 128

        def _glorot(key, shape):
            fan_in, fan_out = (shape[0], shape[1])
            s = jnp.sqrt(6.0 / (fan_in + fan_out))
            return jax.random.uniform(key, shape, jnp.float32, -s, s)

        def _segment_softmax(logits, seg, n):
            m = jax.ops.segment_max(logits, seg, num_segments=n)
            m = jnp.where(jnp.isfinite(m), m, 0.0)
            e = jnp.exp(logits - m[seg])
            s = jax.ops.segment_sum(e, seg, num_segments=n)
            return e / (s[seg] + 1e-16)

        def _transformer_conv(x, src, dst, wq, bq, wk, bk, wv, bv, ws, bs, heads, ch):
            n = x.shape[0]
            q = (x @ wq + bq).reshape(n, heads, ch)
            k = (x @ wk + bk).reshape(n, heads, ch)
            v = (x @ wv + bv).reshape(n, heads, ch)
            alpha = jnp.einsum('ehc,ehc->eh', q[dst], k[src]) / jnp.sqrt(jnp.float32(ch))
            alpha = _segment_softmax(alpha, dst, n)
            msg = v[src] * alpha[:, :, None]
            out = jax.ops.segment_sum(msg, dst, num_segments=n).reshape(n, heads * ch)
            return out + x @ ws + bs
        key = jax.random.key(seed)
        ks = jax.random.split(key, 12)
        x = jax.random.normal(ks[0], (N, IN), jnp.float32)
        edge_index = jax.random.randint(ks[1], (2, E), 0, N, jnp.int64)
        d1 = HID * HEADS
        inp = {'x': x, 'edge_index': edge_index, 'w1_q': _glorot(ks[2], (IN, d1)), 'b1_q': jnp.zeros((d1,), jnp.float32), 'w1_k': _glorot(ks[3], (IN, d1)), 'b1_k': jnp.zeros((d1,), jnp.float32), 'w1_v': _glorot(ks[4], (IN, d1)), 'b1_v': jnp.zeros((d1,), jnp.float32), 'w1_s': _glorot(ks[5], (IN, d1)), 'b1_s': jnp.zeros((d1,), jnp.float32), 'w2_q': _glorot(ks[6], (d1, OUT)), 'b2_q': jnp.zeros((OUT,), jnp.float32), 'w2_k': _glorot(ks[7], (d1, OUT)), 'b2_k': jnp.zeros((OUT,), jnp.float32), 'w2_v': _glorot(ks[8], (d1, OUT)), 'b2_v': jnp.zeros((OUT,), jnp.float32), 'w2_s': _glorot(ks[9], (d1, OUT)), 'b2_s': jnp.zeros((OUT,), jnp.float32)}
        return inp
    _L3_gnn_all = _L3_gnn_setup()
    _L3_gnn_in = {k: v for k, v in _L3_gnn_all.items() if k in ('w1_q', 'b1_q', 'w1_k', 'b1_k', 'w1_v', 'b1_v', 'w1_s', 'b1_s', 'w2_q', 'b2_q', 'w2_k', 'b2_k', 'w2_v', 'b2_v', 'w2_s', 'b2_s')}
    del _L3_gnn_all
    return {'x': x, 'src': src, 'dst': dst, 'edge_attr_128': edge_attr_128, 'edge_type_8': edge_type_8, 'L1_gnn_weight': _L1_gnn_in['weight'], 'L1_gnn_root': _L1_gnn_in['root'], 'L1_gnn_bias': _L1_gnn_in['bias'], 'L1_gnn_bn_gamma': _L1_gnn_in['bn_gamma'], 'L1_gnn_bn_beta': _L1_gnn_in['bn_beta'], 'L2_gnn_W': _L2_gnn_in['W'], 'L2_gnn_b': _L2_gnn_in['b'], 'L2_gnn_gamma': _L2_gnn_in['gamma'], 'L2_gnn_beta': _L2_gnn_in['beta'], 'L3_gnn_w1_q': _L3_gnn_in['w1_q'], 'L3_gnn_b1_q': _L3_gnn_in['b1_q'], 'L3_gnn_w1_k': _L3_gnn_in['w1_k'], 'L3_gnn_b1_k': _L3_gnn_in['b1_k'], 'L3_gnn_w1_v': _L3_gnn_in['w1_v'], 'L3_gnn_b1_v': _L3_gnn_in['b1_v'], 'L3_gnn_w1_s': _L3_gnn_in['w1_s'], 'L3_gnn_b1_s': _L3_gnn_in['b1_s'], 'L3_gnn_w2_q': _L3_gnn_in['w2_q'], 'L3_gnn_b2_q': _L3_gnn_in['b2_q'], 'L3_gnn_w2_k': _L3_gnn_in['w2_k'], 'L3_gnn_b2_k': _L3_gnn_in['b2_k'], 'L3_gnn_w2_v': _L3_gnn_in['w2_v'], 'L3_gnn_b2_v': _L3_gnn_in['b2_v'], 'L3_gnn_w2_s': _L3_gnn_in['w2_s'], 'L3_gnn_b2_s': _L3_gnn_in['b2_s']}

def reference(x, src, dst, edge_attr_128, edge_type_8, L1_gnn_weight, L1_gnn_root, L1_gnn_bias, L1_gnn_bn_gamma, L1_gnn_bn_beta, L2_gnn_W, L2_gnn_b, L2_gnn_gamma, L2_gnn_beta, L3_gnn_w1_q, L3_gnn_b1_q, L3_gnn_w1_k, L3_gnn_b1_k, L3_gnn_w1_v, L3_gnn_b1_v, L3_gnn_w1_s, L3_gnn_b1_s, L3_gnn_w2_q, L3_gnn_b2_q, L3_gnn_w2_k, L3_gnn_b2_k, L3_gnn_w2_v, L3_gnn_b2_v, L3_gnn_w2_s, L3_gnn_b2_s):
    import jax
    import jax.numpy as jnp

    def _L0_gnn_ref(x, edge_index):
        import jax, jax.numpy as jnp
        import numpy as np
        N_NODES = 50000
        src, dst = (edge_index[0], edge_index[1])
        x_j = jnp.take(x, src, axis=0)
        out = jax.ops.segment_sum(x_j, dst, num_segments=x.shape[0])
        return out

    def _L1_gnn_ref(x, xe, edge_index, edge_type, weight, root, bias, bn_gamma, bn_beta):
        import jax, jax.numpy as jnp
        import numpy as np
        N_NODES = 50000
        N_EDGES = 15625
        D = 128
        R = 8
        L = 2
        BN_EPS = 1e-05

        def _rgcn_edge_conv(h, xe, src, dst, etype, w, rt, b):
            m = jax.nn.relu(h[src] + xe)
            n = h.shape[0]
            seg = etype * n + dst
            sums = jax.ops.segment_sum(m, seg, num_segments=R * n)
            cnt = jax.ops.segment_sum(jnp.ones((m.shape[0],), m.dtype), seg, num_segments=R * n)
            mean = sums / jnp.maximum(cnt, 1.0)[:, None]
            hr = mean.reshape(R, n, -1)
            out = jnp.einsum('rnd,rdo->no', hr, w)
            out = out + h @ rt + b
            return out

        def _batch_norm(h, gamma, beta):
            mu = h.mean(axis=0)
            var = jnp.mean((h - mu) ** 2, axis=0)
            return (h - mu) * jax.lax.rsqrt(var + BN_EPS) * gamma + beta
        src, dst = (edge_index[0], edge_index[1])
        h = x
        for l in range(L):
            h = _rgcn_edge_conv(h, xe, src, dst, edge_type, weight[l], root[l], bias[l])
            h = _batch_norm(h, bn_gamma[l], bn_beta[l])
            if l != L - 1:
                h = jax.nn.relu(h)
        return h

    def _L2_gnn_ref(x, edge_index, W, b, gamma, beta):
        import jax, jax.numpy as jnp
        import numpy as np
        N_NODES = 3125
        N_EDGES = 50000
        D = 128
        EPS = 1e-05
        N = x.shape[0]
        loops = jnp.arange(N, dtype=edge_index.dtype)
        src = jnp.concatenate([edge_index[0], loops])
        dst = jnp.concatenate([edge_index[1], loops])
        deg = jax.ops.segment_sum(jnp.ones_like(dst, dtype=x.dtype), dst, num_segments=N)
        dis = jax.lax.rsqrt(deg)
        xw = x @ W
        norm = (dis[src] * dis[dst])[:, None]
        agg = jax.ops.segment_sum(xw[src] * norm, dst, num_segments=N) + b
        h = agg + x
        mu = jnp.mean(h, axis=-1, keepdims=True)
        var = jnp.mean(jnp.square(h - mu), axis=-1, keepdims=True)
        h = (h - mu) * jax.lax.rsqrt(var + EPS) * gamma + beta
        return jax.nn.relu(h)

    def _L3_gnn_ref(x, edge_index, w1_q, b1_q, w1_k, b1_k, w1_v, b1_v, w1_s, b1_s, w2_q, b2_q, w2_k, b2_k, w2_v, b2_v, w2_s, b2_s):
        import jax, jax.numpy as jnp
        import numpy as np
        N = 50000
        E = 25000
        IN = 128
        HID = 32
        HEADS = 4
        OUT = 128

        def _glorot(key, shape):
            fan_in, fan_out = (shape[0], shape[1])
            s = jnp.sqrt(6.0 / (fan_in + fan_out))
            return jax.random.uniform(key, shape, jnp.float32, -s, s)

        def _segment_softmax(logits, seg, n):
            m = jax.ops.segment_max(logits, seg, num_segments=n)
            m = jnp.where(jnp.isfinite(m), m, 0.0)
            e = jnp.exp(logits - m[seg])
            s = jax.ops.segment_sum(e, seg, num_segments=n)
            return e / (s[seg] + 1e-16)

        def _transformer_conv(x, src, dst, wq, bq, wk, bk, wv, bv, ws, bs, heads, ch):
            n = x.shape[0]
            q = (x @ wq + bq).reshape(n, heads, ch)
            k = (x @ wk + bk).reshape(n, heads, ch)
            v = (x @ wv + bv).reshape(n, heads, ch)
            alpha = jnp.einsum('ehc,ehc->eh', q[dst], k[src]) / jnp.sqrt(jnp.float32(ch))
            alpha = _segment_softmax(alpha, dst, n)
            msg = v[src] * alpha[:, :, None]
            out = jax.ops.segment_sum(msg, dst, num_segments=n).reshape(n, heads * ch)
            return out + x @ ws + bs
        src = edge_index[0]
        dst = edge_index[1]
        h = _transformer_conv(x, src, dst, w1_q, b1_q, w1_k, b1_k, w1_v, b1_v, w1_s, b1_s, HEADS, HID)
        h = jax.nn.relu(h)
        out = _transformer_conv(h, src, dst, w2_q, b2_q, w2_k, b2_k, w2_v, b2_v, w2_s, b2_s, 1, OUT)
        return out
    edge_index = jnp.stack([src, dst])
    h = jnp.maximum(_layernorm(x, axis=-1), 0.0)
    x = x + _L0_gnn_ref(h, edge_index)
    h = jnp.maximum(_layernorm(x, axis=-1), 0.0)
    x = x + _L1_gnn_ref(h, edge_attr_128, edge_index, edge_type_8, L1_gnn_weight, L1_gnn_root, L1_gnn_bias, L1_gnn_bn_gamma, L1_gnn_bn_beta)
    h = jnp.maximum(_layernorm(x, axis=-1), 0.0)
    x = x + _L2_gnn_ref(h, edge_index, L2_gnn_W, L2_gnn_b, L2_gnn_gamma, L2_gnn_beta)
    h = jnp.maximum(_layernorm(x, axis=-1), 0.0)
    x = x + _L3_gnn_ref(h, edge_index, L3_gnn_w1_q, L3_gnn_b1_q, L3_gnn_w1_k, L3_gnn_b1_k, L3_gnn_w1_v, L3_gnn_b1_v, L3_gnn_w1_s, L3_gnn_b1_s, L3_gnn_w2_q, L3_gnn_b2_q, L3_gnn_w2_k, L3_gnn_b2_k, L3_gnn_w2_v, L3_gnn_b2_v, L3_gnn_w2_s, L3_gnn_b2_s)
    return x

_drawn_inputs = setup_inputs


def setup_inputs(seed=0):
    import zlib

    import numpy as np

    out = dict(_drawn_inputs(seed))
    spreads = {'L1_gnn_bias': (0.0, 2.0),
     'L1_gnn_bn_gamma': (1.0, 0.2),
     'L1_gnn_bn_beta': (0.0, 0.45),
     'L2_gnn_b': (0.0, 0.697),
     'L2_gnn_gamma': (1.0, 0.6),
     'L2_gnn_beta': (0.0, 0.8),
     'L3_gnn_b1_q': (0.0, 0.8),
     'L3_gnn_b1_k': (0.0, 2.0),
     'L3_gnn_b1_v': (0.0, 0.774),
     'L3_gnn_b1_s': (0.0, 0.744),
     'L3_gnn_b2_q': (0.0, 2.0),
     'L3_gnn_b2_k': (0.0, 2.0),
     'L3_gnn_b2_v': (0.0, 0.74),
     'L3_gnn_b2_s': (0.0, 0.689)}
    factors = {'L3_gnn_w1_q': 7.446, 'L3_gnn_w1_k': 7.407, 'L3_gnn_w2_q': 8.0, 'L3_gnn_w2_k': 8.0}
    for name, (base, spread) in spreads.items():
        noise = np.random.default_rng([zlib.crc32(name.encode()), seed]).standard_normal(out[name].shape)
        drawn = base * np.exp(spread * noise) if base else spread * noise
        out[name] = jnp.asarray(drawn.astype(out[name].dtype))
    for name, factor in factors.items():
        out[name] = (out[name] * factor).astype(out[name].dtype)
    return out
```

```python
import concourse.bass as bass
from concourse import mybir
from contextlib import ExitStack

F32 = mybir.dt.float32
I32 = mybir.dt.int32
ALU = mybir.AluOpType
ACT = mybir.ActivationFunctionType
AX = mybir.AxisListType

P = 128
D = 128
N = 3125
E = 53125
NB = -(-N // P)
NP = NB * P
NREST = N - (NB - 1) * P
NT = -(-E // P)
EP = NT * P
NCH = -(-NT // P)
NTREST = NT - (NCH - 1) * P
PAD_DST = 4095
R = 8
KEYSTEP = 4096
WA, WB = P, 32
NBB = -(-N // WB)
H8 = 8
STEPS_A = NT + NB - 1
STEPS_B = NT + NBB - 1
HALVES_A = -(-STEPS_A // H8)
HALVES_B = -(-STEPS_B // H8)
assert HALVES_A % 2 == 1 and HALVES_B % 2 == 1
SA = HALVES_A * H8
SB = HALVES_B * H8
SEG = R * WB
FAR = 1.0e6
BIG = 1.0e30
EPS = 1e-5
RW_MAX = 137


class Count:

    def __init__(self):
        self.base, self.k = 0, 0

    def up(self):
        self.k += 1
        return 1

    def count(self):
        return self.base + self.k

    def at(self, base):
        self.base, self.k = base, 0


def gnn_kernel(nc, x, src, dst, xe, ety, w1, root, bias1, bng, bnb, w2, b2, g2, be2,
               waq, baq, wak, bak, wav, bav, was, bas, wbq, bbq, wbk, bbk, wbv, bbv, wbs, bbs,
               h_tab, kv_tab, out):
    ctx = ExitStack()
    with ctx:
        def sb(name, shape, dt=F32):
            return ctx.enter_context(nc.sbuf_tensor(name, shape, dt))

        def sem(name):
            return ctx.enter_context(nc.semaphore(name))

        X = sb("X", [P, NB, D])
        H = sb("H", [P, NB, D])
        Y = sb("Y", [P, NB, D])
        arena = sb("arena", [P, R * NP])
        rings = sb("rings", [P, 8192])
        iota = sb("iota", [P, SB])
        iota_p = sb("iota_p", [P, 1])
        iota_key = sb("iota_key", [P, R, WB])
        tile_no = sb("tile_no", [P, NCH])
        ident = sb("ident", [P, P])
        ones = sb("ones", [P, P])
        ones_rest = sb("ones_rest", [P, P])
        eps_col = sb("eps_col", [P, 1])
        locA = sb("locA", [P, SA + H8])
        srcA = sb("srcA", [P, SA + H8], I32)
        blkA = sb("blkA", [P, SA + H8], I32)
        locB = sb("locB", [P, SB])
        srcB = sb("srcB", [P, SB], I32)
        blkB = sb("blkB", [P, SB], I32)
        tileB = sb("tileB", [P, SB], I32)
        idx = sb("idx", [P, 2, H8], I32)
        wrel = sb("wrel", [P, R + 1, D])
        rows = sb("rows", [P, 3, D])
        inv_cnt = sb("inv_cnt", [P, NB, R])
        dis = sb("dis", [P, NB])
        st = sb("st", [P, 4, NB])
        small = sb("small", [P, 512])

        ring_g = rings[:, 0:2048].rearrange("p (s f) -> p s f", s=16)
        ring_xe = rings[:, 2048:4096].rearrange("p (s f) -> p s f", s=16)
        ring_oh2 = rings[:, 4096:8192].rearrange("p (s f) -> p s f", s=16)
        ring_kv = rings[:, 0:4096].rearrange("p (s f) -> p s f", s=16)
        ring_oh = rings[:, 4096:6144].rearrange("p (s f) -> p s f", s=16)
        oh_t = rings[:, 6144:7168].rearrange("p (s f) -> p s f", s=8)
        prod = rings[:, 7168:8192].rearrange("p (s f) -> p s f", s=8)
        acb = rings[:, 0:1024]
        h_fix = rings[:, 1024:1152]
        hT_fix = rings[:, 1152:1280]
        relsum = rings[:, 1280:2304].rearrange("p (r f) -> p r f", r=R)
        relred = rings[:, 2304:2432]

        bank = [ctx.enter_context(nc.psum_tensor(f"bank{i}", [P, 512], F32)) for i in range(8)]

        o = 8192
        row_i = arena[:, o:o + 3 * NCH * P].bitcast(I32).rearrange("p (a c f) -> p a c f", a=3, c=NCH); o += 3 * NCH * P
        row_f = arena[:, o:o + 3 * NCH * P].rearrange("p (a c f) -> p a c f", a=3, c=NCH); o += 3 * NCH * P
        row_key = arena[:, o:o + NCH * P].rearrange("p (c f) -> p c f", c=NCH); o += NCH * P
        hit = arena[:, o:o + NCH * SB].rearrange("p (c s) -> p c s", c=NCH); o += NCH * SB
        spread = arena[:, o:o + 2 * NCH * P].rearrange("p (a c f) -> p a c f", a=2, c=NCH); o += 2 * NCH * P
        tri = arena[:, o:o + P]; o += P
        tmp_s = arena[:, o:o + 3 * SB].rearrange("p (a s) -> p a s", a=3); o += 3 * SB
        tc = arena[:, o:o + 9 * NCH].rearrange("p (a c) -> p a c", a=9); o += 9 * NCH
        tci = arena[:, o:o + 2 * NCH].bitcast(I32).rearrange("p (a c) -> p a c", a=2); o += 2 * NCH
        assert o <= 21000
        A0 = D + R
        acc0 = arena[:, 0:NB * A0].rearrange("p (b f) -> p b f", b=NB)
        rel_hot = arena[:, 4096:4096 + SA * R].rearrange("p (s r) -> p s r", r=R)
        acc1 = arena[:, :]
        acc2 = arena[:, 0:NP].rearrange("p (b f) -> p b f", b=NB)
        y2 = arena[:, NP:2 * NP].rearrange("p (b f) -> p b f", b=NB)
        scratch = arena[:, R * NP - NP:R * NP].rearrange("p (b f) -> p b f", b=NB)
        qt = arena[:, 0:NP]
        skip = arena[:, NP:2 * NP].rearrange("p (b f) -> p b f", b=NB)
        kvt = arena[:, 2 * NP:4 * NP].rearrange("p (b f) -> p b f", b=NB)
        o = 4 * NP
        wqkvs = arena[:, o:o + 4 * D]; o += 4 * D
        bqkvs = arena[:, o:o + 4 * D]; o += 4 * D
        acc3 = arena[:, o:o + NB * 132]; o += NB * 132
        part = arena[:, o:o + H8 * 132]; o += H8 * 132
        rhs3 = arena[:, o:o + H8 * RW_MAX]; o += H8 * RW_MAX
        assert o <= R * NP - NP
        fl = sb("fl", [P, 1536])
        mst = sb("mst", [P, NB * 4])

        ORDER = ["list0", "ln0", "sum", "list1", "ln1", "rel0", "rel1", "ln2", "gcn", "gcn_ln", "ln3", "att0", "att1"]
        PHASES = ["sum", "rel0", "rel1", "gcn", "att0", "att1"]
        RELS, ATTS, PROJ = ("rel0", "rel1"), ("att0", "att1"), ("rel0", "rel1", "gcn", "att0", "att1")
        halves_of = {ph: HALVES_B if ph in RELS else HALVES_A for ph in PHASES}
        LOADS = ("table", "w", "w_root", "row0", "row1", "row2", "w0", "w1", "w2", "w3", "b0", "b1", "b2", "b3")

        def total(stage, event):
            hv = halves_of.get(stage, 0)
            if event == "idx_made":
                return hv + (stage in ATTS)
            if event == "hot_made":
                return (hv + (stage in ATTS)) * H8
            if event == "step_done":
                return 16 * (hv > 0) + hv * H8
            if event == "added":
                return hv if stage in ATTS else 8 * (hv > 0) + hv * H8
            if event in ("msg_sum", "msg_made"):
                return hv * H8 * (stage in RELS)
            if event in ("hotT", "hotT_copied", "q_done"):
                return 2 * (hv + 1) * (stage in ATTS)
            if event in ("logits", "logT", "max_made", "maxT", "diff", "exped", "rhs_made", "resc", "resc_exped"):
                return hv * (stage in ATTS)
            if event == "parted":
                return hv * H8 * (stage == "att1")
            if event in ("h_fixed", "hT_done", "hT_made", "proj_done", "proj_read"):
                return NB * (stage in PROJ)
            if event == "sums_fixed":
                return NB * (stage in RELS)
            if event in ("picked", "read"):
                return 2 * (stage in ("list0", "list1"))
            if event in ("counts", "starts", "hits", "made"):
                return 1 * (stage in ("list0", "list1"))
            if event in ("centred", "squared"):
                return 1 * (stage[:2] == "ln" or stage in ("gcn_ln",) + RELS)
            if event in ("var", "root"):
                return 1 * (stage[:2] == "ln" or stage in ("gcn_ln",) + RELS)
            if event == "ready":
                return 1 * (stage[:2] == "ln")
            if event in ("mean_sum", "var_sum"):
                return 1 * (stage in RELS)
            if event == "table_made":
                return 1 * (stage in ("gcn",) + ATTS)
            if event == "start":
                return 1 * (hv > 0)
            if event == "over":
                return 1 * (stage in PROJ)
            if event in LOADS:
                of = dict(table=PHASES, w=("rel0", "rel1", "gcn"), w_root=RELS, row0=("rel0", "rel1", "gcn"), row1=("rel0", "rel1", "gcn"),
                          row2=("rel0", "rel1", "gcn")).get(event, ATTS)
                return 16 * (stage in of)
            raise KeyError(event)

        PRIMED = {"pe": ("hT_done", "proj_done", "q_done"), "act": ("hT_made",), "dve": ("proj_read",)}

        def prime(eng, name):
            for event in PRIMED[name]:
                eng.sem_inc(ev("rel0." + event), 1)

        made = {}

        def ev(name):
            stage, _, event = name.rpartition(".")
            key = event if stage in ORDER else name.replace(".", "_")
            if key not in made:
                made[key] = ctx.enter_context(nc.semaphore(key))
            return made[key]

        def at(name, count):
            stage, _, event = name.rpartition(".")
            if stage not in ORDER:
                return count
            before = sum(total(q, event) for q in ORDER[:ORDER.index(stage)])
            return before + any(event in events for events in PRIMED.values()) + count

        gath = [ev(f"gathered{k}") for k in range(16)]
        xe_in = [ev(f"edge_rows_in{k}") for k in range(16)]

        def rounds_before(ph, par, phases=PHASES):
            return sum((halves_of[q] + 1 - par) // 2 for q in phases[:phases.index(ph)])

        def gathers_seen(ph, i, par):
            return 16 * (rounds_before(ph, par) + i)

        def edge_rows_seen(ph, i, par):
            return 16 * (rounds_before(ph, par, ["rel0", "rel1"]) + i)

        def halves(eng, count, body):
            with eng.Fori(0, count // 2) as i:
                body(2 * i, i, 0)
                body(2 * i + 1, i, 1)
            body(count - 1, count // 2, 0)

        def skewed(eng, body):
            body(0, 0, 0)
            with eng.Fori(0, HALVES_A // 2) as i:
                body(2 * i + 1, i, 1)
                body(2 * i + 2, i + 1, 0)

        def registers(eng, table, h, top):
            _, regs = nc.values_load_multi_w_load_instructions(
                table[0:1, bass.ds(H8 * h, H8)], engines=[eng.engine], min_val=0, max_val=top - 1,
                skip_runtime_bounds_check_because="the step list's entries are below this by construction")
            return regs

        block = ctx.enter_context(nc.Block())

        @block.sync
        def _(sp):
            full = (NCH - 1) * P
            sp.wait_ge(ev("rows.zeroed"), at("rows.zeroed", 1))
            for a, arr in enumerate((dst, src, ety)):
                v = arr.rearrange("(t p) -> t p", p=P)
                sp.dma_start(row_i[:, a, 0:NCH - 1, :], v[0:full, :].rearrange("(c t) p -> t c p", t=P)).then_inc(ev(f"rows.in{2 * a}"), 16)
                sp.dma_start(row_i[0:NTREST, a, NCH - 1, :], v[full:NT, :]).then_inc(ev(f"rows.in{2 * a + 1}"), 16)
            sp.wait_ge(ev("x.zeroed"), at("x.zeroed", 1))
            sp.dma_start(X[:, 0:NB - 1, :], x[0:(NB - 1) * P, :].rearrange("(b p) f -> p b f", p=P)).then_inc(ev("x.in0"), 16)
            sp.dma_start(X[0:NREST, NB - 1, :], x[(NB - 1) * P:N, :]).then_inc(ev("x.in1"), 16)

            def store_table(ph, rows_t, tab, ready):
                sp.wait_ge(ev(ready), at(ready, 1))
                sp.dma_start(tab.rearrange("(b p) f -> p b f", p=P), rows_t).then_inc(ev(ph + ".table"), 16)

            def load_rel(layer):
                ph = f"rel{layer}"
                sp.dma_start(wrel[:, 0:R, :], w1[layer].rearrange("r k n -> k r n")).then_inc(ev(ph + ".w"), 16)
                sp.dma_start(wrel[:, R, :], root[layer]).then_inc(ev(ph + ".w_root"), 16)
                for j, v in enumerate((bias1, bng, bnb)):
                    sp.dma_start(rows[:, j, :], v[layer:layer + 1, :].broadcast_to([P, D])).then_inc(ev(f"{ph}.row{j}"), 16)

            def load_edge_rows(ph):
                def half(h, i, par):
                    tiles = registers(sp, tileB, h, NT)
                    for k in range(H8):
                        s = par * H8 + k
                        sp.wait_ge(ev(ph + ".step_done"), at(ph + ".step_done", H8 * h + k + 1))
                        sp.dma_start(ring_xe[:, s, :], xe[bass.ds(tiles[k] * P, P), :]).then_inc(xe_in[s], 16)
                halves(sp, HALVES_B, half)

            load_rel(0)
            store_table("sum", H[:, :, :], h_tab, "ln0.ready")
            store_table("rel0", H[:, :, :], h_tab, "ln1.ready")
            sp.wait_ge(ev("list1.made"), at("list1.made", 1))
            load_edge_rows("rel0")
            sp.wait_ge(ev("rel0.over"), at("rel0.over", 1))
            load_rel(1)
            store_table("rel1", H[:, :, :], h_tab, "rel0.over")
            load_edge_rows("rel1")
            sp.wait_ge(ev("rel1.over"), at("rel1.over", 1))
            sp.dma_start(wrel[:, 0, :], w2).then_inc(ev("gcn.w"), 16)
            for j, v in enumerate((b2, g2, be2)):
                sp.dma_start(rows[:, j, :], v.rearrange("(a f) -> a f", a=1).broadcast_to([P, D])).then_inc(ev(f"gcn.row{j}"), 16)
            store_table("gcn", y2, h_tab, "gcn.table_made")
            weights = ((waq, wak, wav, was), (wbq, wbk, wbv, wbs))
            biases = ((baq, bak, bav, bas), (bbq, bbk, bbv, bbs))
            for l, ph in enumerate(("att0", "att1")):
                sp.wait_ge(ev(("gcn.over", "att0.over")[l]), at(("gcn.over", "att0.over")[l], 1))
                for j in range(4):
                    sp.dma_start(wqkvs[:, j * D:(j + 1) * D], weights[l][j]).then_inc(ev(f"{ph}.w{j}"), 16)
                    sp.dma_start(bqkvs[:, j * D:(j + 1) * D], biases[l][j].rearrange("(a f) -> a f", a=1).broadcast_to([P, D]))\
                      .then_inc(ev(f"{ph}.b{j}"), 16)
                store_table(ph, kvt, kv_tab, ph + ".table_made")
            sp.wait_ge(ev("att1.over"), at("att1.over", 1))
            sp.dma_start(out[0:(NB - 1) * P, :].rearrange("(b p) f -> p b f", p=P), X[:, 0:NB - 1, :]).then_inc(ev("out0"), 16)
            sp.dma_start(out[(NB - 1) * P:N, :], X[0:NREST, NB - 1, :]).then_inc(ev("out1"), 16)
            sp.wait_ge(ev("out0"), at("out0", 16))
            sp.wait_ge(ev("out1"), at("out1", 16))

        @block.gpsimd
        def _(pool):
            kw = dict(allow_small_or_imprecise_dtypes=True)
            for t, pattern, cm in ((iota[:, :], [[1, SB]], 0), (iota_p[:, :], [[1, 1]], 1), (iota_key[:, :, :], [[KEYSTEP, R], [1, WB]], 0), (tile_no[:, :], [[P, NCH]], 1)):
                nc.gpsimd.iota(t, pattern=pattern, base=0, channel_multiplier=cm, **kw).then_inc(ev("iotas"), 1)
            for ph in PHASES:
                att = ph in ("att0", "att1")
                table, ring = (kv_tab, ring_kv) if att else (h_tab, ring_g)
                pool.wait_ge(ev(ph + ".table"), at(ph + ".table", 16))

                def half(h, i, par):
                    pool.wait_ge(ev(ph + ".idx_made"), at(ph + ".idx_made", h + 1))
                    pool.wait_ge(ev(ph + ".step_done"), at(ph + ".step_done", H8 * h + H8))
                    pool.sem_inc(ev("pool_turns"), 1)
                    for k in range(H8):
                        s = par * H8 + k
                        nc.gpsimd.indirect_dma_start(
                            out=ring[:, s, :], out_offset=None, in_=table,
                            in_offset=bass.IndirectOffsetOnAxis(ap=idx[:, par, k:k + 1], axis=0)).then_inc(gath[s], 16)
                halves(pool, halves_of[ph], half)

        @block.scalar
        def _(act):
            def norm_parts(name, t):
                act.wait_ge(ev(name + ".centred"), at(name + ".centred", 1))
                act.activation(scratch, t, ACT.Square).then_inc(ev(name + ".squared"), 1)
                act.wait_ge(ev(name + ".var"), at(name + ".var", 1))
                act.activation(st[:, 2, :], st[:, 1, :], ACT.Sqrt, bias=eps_col[:, :], scale=1.0 / D).then_inc(ev(name + ".root"), 1)

            def gather_indices(ph, tab):
                def half(h, i, par):
                    act.wait_ge(ev(ph + ".step_done"), at(ph + ".step_done", H8 * h + H8))
                    act.activation(idx[:, par, :], tab[:, bass.ds(H8 * h, H8)], ACT.Copy).then_inc(ev(ph + ".idx_made"), 1)
                return half

            def fixed_block(name, i):
                act.wait_ge(ev(name + ".hT_done"), at(name + ".hT_done", i))
                act.activation(h_fix, H[:, bass.ds(i, 1), :].rearrange("p a f -> p (a f)"), ACT.Copy).then_inc(ev(name + ".h_fixed"), 1)
                act.wait_ge(ev(name + ".hT_done"), at(name + ".hT_done", i + 1))
                act.wait_ge(ev(name + ".proj_done"), at(name + ".proj_done", i))
                act.activation(hT_fix, bank[0][:, 0:P], ACT.Copy).then_inc(ev(name + ".hT_made"), 1)

            prime(act, "act")
            norm_parts("ln0", H[:, :, :])
            act.wait_ge(ev("list0.made"), at("list0.made", 1))
            halves(act, HALVES_A, gather_indices("sum", srcA))
            norm_parts("ln1", H[:, :, :])
            act.wait_ge(ev("list1.made"), at("list1.made", 1))
            for l, ph in enumerate(("rel0", "rel1")):
                prep = gather_indices(ph, srcB)

                def half(h, i, par):
                    prep(h, i, par)
                    for k in range(H8):
                        s = par * H8 + k
                        act.wait_ge(ev(ph + ".msg_sum"), at(ph + ".msg_sum", H8 * h + k + 1))
                        act.activation(ring_xe[:, s, :], ring_xe[:, s, :], ACT.Relu).then_inc(ev(ph + ".msg_made"), 1)
                halves(act, HALVES_B, half)
                act.wait_ge(ev(ph + ".added"), at(ph + ".added", 8 + SB))
                with act.Fori(0, NB) as i:
                    act.wait_ge(ev(ph + ".proj_done"), at(ph + ".proj_done", i))
                    act.activation(acb.rearrange("p (r b n) -> p b r n", r=R, b=P // WB),
                                   acc1[:, bass.ds(R * P * i, R * P)].rearrange("p (b r n) -> p b r n", b=P // WB, r=R),
                                   ACT.Copy).then_inc(ev(ph + ".sums_fixed"), 1)
                    fixed_block(ph, i)
                act.wait_ge(ev(ph + ".centred"), at(ph + ".centred", 1))
                act.activation(scratch, Y[:, :, :], ACT.Square).then_inc(ev(ph + ".squared"), 1)
                act.wait_ge(ev(ph + ".var"), at(ph + ".var", 1))
                act.activation(small[:, 128:256], small[:, 0:128], ACT.Sqrt, bias=eps_col[:, :], scale=1.0 / N).then_inc(ev(ph + ".root"), 1)
            norm_parts("ln2", H[:, :, :])
            act.wait_ge(ev("deg.made"), at("deg.made", 1))
            act.activation(st[:, 2, :], st[:, 3, :], ACT.Sqrt).then_inc(ev("deg.root"), 1)
            act.wait_ge(ev("ln2.ready"), at("ln2.ready", 1))
            with act.Fori(0, NB) as i:
                fixed_block("gcn", i)
            halves(act, HALVES_A, gather_indices("gcn", srcA))
            norm_parts("gcn_ln", Y[:, :, :])
            norm_parts("ln3", H[:, :, :])
            for l, ph in enumerate(("att0", "att1")):
                nh = (4, 1)[l]
                scale = float(D // nh) ** -0.5
                q8 = H8 * nh
                act.wait_ge(ev(("ln3.ready", "att0.over")[l]), at(("ln3.ready", "att0.over")[l], 1))
                with act.Fori(0, NB) as i:
                    fixed_block(ph, i)
                prep = gather_indices(ph, srcA)
                dif, ex, ab = fl[:, 0:q8], fl[:, 64:64 + q8], fl[:, 256:256 + 2 * q8]

                def copy_hotT(h):
                    for j in range(2):
                        act.wait_ge(ev(ph + ".hotT"), at(ph + ".hotT", 2 * h + j + 1))
                        act.wait_ge(ev(ph + ".q_done"), at(ph + ".q_done", 2 * h))
                        act.activation(oh_t[:, 4 * j:4 * j + 4, :], bank[j][:, :].rearrange("p (s f) -> p s f", s=4), ACT.Copy)\
                           .then_inc(ev(ph + ".hotT_copied"), 1)

                def rescale(h):
                    act.wait_ge(ev(ph + ".resc"), at(ph + ".resc", h + 1))
                    act.activation(ab, ab, ACT.Exp, scale=scale).then_inc(ev(ph + ".resc_exped"), 1)
                    if nh == 1:
                        act.wait_ge(ev(ph + ".resc_exped"), at(ph + ".resc_exped", h + 1))
                        act.wait_ge(ev(ph + ".added"), at(ph + ".added", h))
                        for k in range(H8):
                            act.activation(part[:, k * (D + 1):(k + 1) * (D + 1)], bank[5 + k // 3][:, (k % 3) * (D + 3):(k % 3) * (D + 3) + D + 1],
                                           ACT.Copy, scale=ab[:, q8 + k:q8 + k + 1]).then_inc(ev(ph + ".parted"), 1)

                def half(h, i, par):
                    if par == 1:
                        prep(h + 1, i + 1, 0)
                    else:
                        prep(h + 1, i, 1)
                    copy_hotT(h + 1)
                    if not (isinstance(h, int) and h == 0):
                        rescale(h - 1)
                    act.wait_ge(ev(ph + ".diff"), at(ph + ".diff", h + 1))
                    act.activation(ex, dif, ACT.Exp, scale=scale).then_inc(ev(ph + ".exped"), 1)

                prep(0, 0, 0)
                copy_hotT(0)
                skewed(act, half)
                rescale(HALVES_A - 1)

        def open_ring(pe, ph):
            pe.wait_ge(ev(ph + ".start"), at(ph + ".start", 1))
            pe.sem_inc(ev(ph + ".step_done"), 16)

        def plain_products(pe, ph):
            open_ring(pe, ph)

            def half(h, i, par):
                for k in range(H8):
                    s = par * H8 + k
                    step = H8 * h + k
                    pe.wait_ge(gath[s], gathers_seen(ph, i + 1, par))
                    pe.wait_ge(ev(ph + ".hot_made"), at(ph + ".hot_made", step + 1))
                    pe.wait_ge(ev(ph + ".added"), at(ph + ".added", step + 1))
                    last = nc.tensor.matmul(bank[k][:, 0:D], ring_oh[:, s, :], ring_g[:, s, :], start=True, stop=True)
                    if ph == "sum":
                        last = nc.tensor.matmul(bank[k][:, D:D + R], ring_oh[:, s, :],
                                                rel_hot[:, bass.ds(step, 1), :].rearrange("p a r -> p (a r)"), start=True, stop=True)
                    last.then_inc(ev(ph + ".step_done"), 1)
            halves(pe, HALVES_A, half)

        def node_sum(pe, t, name):
            nc.tensor.matmul(bank[5][:, 0:D], ones[:, :], t[:, 0, :], start=True, stop=False)
            with pe.Fori(1, NB - 1) as i:
                nc.tensor.matmul(bank[5][:, 0:D], ones[:, :], t[:, bass.ds(i, 1), :].rearrange("p a f -> p (a f)"), start=False, stop=False)
            nc.tensor.matmul(bank[5][:, 0:D], ones_rest[:, :], t[:, NB - 1, :], start=False, stop=True).then_inc(ev(name), 1)

        @block.tensor
        def _(pe):
            prime(pe, "pe")
            for n, cols in enumerate((SA, SB)):
                nm = f"list{n}"
                pe.wait_ge(ev(nm + ".counts"), at(nm + ".counts", 1))
                nc.tensor.matmul(bank[0][:, 0:NCH], tri, tc[:, 2, :], start=True, stop=False)
                nc.tensor.matmul(bank[0][:, 0:NCH], ones[:, :], tc[:, 3, :], start=False, stop=True).then_inc(ev(nm + ".starts"), 1)
                pe.wait_ge(ev(nm + ".hits"), at(nm + ".hits", 1))
                hw = cols // 2
                for hf in range(2):
                    if hf:
                        pe.wait_ge(ev(nm + ".read"), at(nm + ".read", hf))
                    for q in range(5):
                        for c in range(NCH):
                            lhs = (spread[:, 0, c, :], ones[:, :],
                                   (row_f[:, 0, c, :], row_key[:, c, :])[n],
                                   row_f[:, 1, c, :],
                                   (row_f[:, 2, c, :], spread[:, 1, c, :])[n])[q]
                            last = nc.tensor.matmul(bank[1 + q][:, 0:hw], lhs, hit[:, c, hf * hw:(hf + 1) * hw],
                                                    start=(c == 0), stop=(c == NCH - 1))
                    last.then_inc(ev(nm + ".picked"), 1)
                if n == 0:
                    plain_products(pe, "sum")

            for l, ph in enumerate(("rel0", "rel1")):
                open_ring(pe, ph)

                def half(h, i, par):
                    for k in range(H8):
                        s = par * H8 + k
                        step = H8 * h + k
                        pe.wait_ge(ev(ph + ".hot_made"), at(ph + ".hot_made", step + 1))
                        pe.wait_ge(ev(ph + ".msg_made"), at(ph + ".msg_made", step + 1))
                        pe.wait_ge(ev(ph + ".added"), at(ph + ".added", step + 1))
                        nc.tensor.matmul(bank[k][:, 0:SEG], ring_xe[:, s, :], ring_oh2[:, s, :], start=True, stop=True)\
                            .then_inc(ev(ph + ".step_done"), 1)
                halves(pe, HALVES_B, half)
                pe.wait_ge(ev(ph + ".w"), at(ph + ".w", 16))
                pe.wait_ge(ev(ph + ".w_root"), at(ph + ".w_root", 16))
                pe.wait_ge(ev(ph + ".added"), at(ph + ".added", 8 + SB))
                with pe.Fori(0, NB) as i:
                    pe.wait_ge(ev(ph + ".h_fixed"), at(ph + ".h_fixed", i + 1))
                    pe.wait_ge(ev(ph + ".hT_made"), at(ph + ".hT_made", i))
                    nc.tensor.transpose(bank[0][:, 0:P], h_fix, ident[:, :]).then_inc(ev(ph + ".hT_done"), 1)
                    pe.wait_ge(ev(ph + ".sums_fixed"), at(ph + ".sums_fixed", i + 1))
                    pe.wait_ge(ev(ph + ".proj_read"), at(ph + ".proj_read", i))
                    for r in range(R):
                        nc.tensor.matmul(bank[1 + r // 4][:, (r % 4) * D:(r % 4 + 1) * D], acb[:, r * P:(r + 1) * P], wrel[:, r, :], start=True, stop=True)
                    pe.wait_ge(ev(ph + ".hT_made"), at(ph + ".hT_made", i + 1))
                    nc.tensor.matmul(bank[3][:, 0:D], hT_fix, wrel[:, R, :], start=True, stop=True).then_inc(ev(ph + ".proj_done"), 1)
                pe.wait_ge(ev(ph + ".proj_read"), at(ph + ".proj_read", NB))
                node_sum(pe, Y[:, :, :], ph + ".mean_sum")
                pe.wait_ge(ev(ph + ".squared"), at(ph + ".squared", 1))
                node_sum(pe, scratch, ph + ".var_sum")

            def project(ph, weights, width, loads):
                for name in loads:
                    pe.wait_ge(ev(name), at(name, 16))
                with pe.Fori(0, NB) as i:
                    pe.wait_ge(ev(ph + ".h_fixed"), at(ph + ".h_fixed", i + 1))
                    pe.wait_ge(ev(ph + ".hT_made"), at(ph + ".hT_made", i))
                    nc.tensor.transpose(bank[0][:, 0:P], h_fix, ident[:, :]).then_inc(ev(ph + ".hT_done"), 1)
                    pe.wait_ge(ev(ph + ".proj_read"), at(ph + ".proj_read", i))
                    pe.wait_ge(ev(ph + ".hT_made"), at(ph + ".hT_made", i + 1))
                    nc.tensor.matmul(bank[1][:, 0:width], hT_fix, weights, start=True, stop=True).then_inc(ev(ph + ".proj_done"), 1)

            project("gcn", wrel[:, 0, :], D, ["gcn.w"])
            plain_products(pe, "gcn")
            for l, ph in enumerate(("att0", "att1")):
                nh = (4, 1)[l]
                q8 = H8 * nh
                rw = D + 2 * nh + 1
                rhs = rhs3[:, 0:H8 * rw].rearrange("p (s f) -> p s f", s=H8)
                project(ph, wqkvs, 4 * D, [f"{ph}.w{j}" for j in range(4)])
                open_ring(pe, ph)
                logits, locs = fl[:, 128:128 + q8], fl[:, 192:192 + q8]
                tri3 = fl[0:q8, 648:648 + 3 * P].rearrange("p (a f) -> p a f", a=3)

                def transpose_hots(h, par):
                    pe.wait_ge(ev(ph + ".hot_made"), at(ph + ".hot_made", H8 * h + H8))
                    for j in range(2):
                        for k in range(4):
                            last = nc.tensor.transpose(bank[j][:, k * P:(k + 1) * P], ring_oh[:, par * H8 + 4 * j + k, :], ident[:, :])
                        last.then_inc(ev(ph + ".hotT"), 1)

                def pick_queries(h):
                    blks = registers(pe, blkA, h, NB)
                    for j in range(2):
                        pe.wait_ge(ev(ph + ".hotT_copied"), at(ph + ".hotT_copied", 2 * h + j + 1))
                        for k in range(4):
                            last = nc.tensor.matmul(bank[2 + j][:, k * P:(k + 1) * P], oh_t[:, 4 * j + k, :], qt[:, bass.ds(blks[4 * j + k] * D, D)],
                                                    start=True, stop=True)
                        last.then_inc(ev(ph + ".q_done"), 1)

                def half(h, i, par):
                    pe.wait_ge(ev(ph + ".logits"), at(ph + ".logits", h + 1))
                    nc.tensor.transpose(bank[4][0:q8, 0:P], logits, ident[:, :])
                    nc.tensor.transpose(bank[4][0:q8, P:2 * P], locs, ident[:, :]).then_inc(ev(ph + ".logT"), 1)
                    transpose_hots(h + 1, 1 - par)
                    pe.wait_ge(ev(ph + ".max_made"), at(ph + ".max_made", h + 1))
                    for a in range(3):
                        last = nc.tensor.matmul(bank[4][:, 2 * P + a * q8:2 * P + (a + 1) * q8], tri3[:, a, :], ident[0:q8, 0:q8], start=True, stop=True)
                    last.then_inc(ev(ph + ".maxT"), 1)
                    pick_queries(h + 1)
                    pe.wait_ge(ev(ph + ".rhs_made"), at(ph + ".rhs_made", h + 1))
                    pe.wait_ge(ev(ph + ".added"), at(ph + ".added", h))
                    for k in range(H8):
                        nc.tensor.matmul(bank[5 + k // 3][:, (k % 3) * rw:(k % 3 + 1) * rw], ring_oh[:, par * H8 + k, :], rhs[:, k, :], start=True, stop=True)\
                            .then_inc(ev(ph + ".step_done"), 1)

                transpose_hots(0, 0)
                pick_queries(0)
                skewed(pe, half)

        @block.vector
        def _(dve):
            v = nc.vector
            own, dve_done = Count(), ev("dve_done")
            prime(dve, "dve")
            v.memset(row_i[:, :, NCH - 1, :], 0).then_inc(ev("rows.zeroed"), 1)
            v.memset(X[:, NB - 1, :], 0.0).then_inc(ev("x.zeroed"), 1)
            v.memset(ones[:, :], 1.0).then_inc(dve_done, own.up())
            v.memset(eps_col[:, :], EPS).then_inc(dve_done, own.up())
            v.memset(arena[:, 0:NB * A0], 0.0).then_inc(dve_done, own.up())
            v.memset(locA[:, SA:SA + H8], FAR).then_inc(dve_done, own.up())
            v.memset(srcA[:, SA:SA + H8], 0).then_inc(dve_done, own.up())
            v.memset(blkA[:, SA:SA + H8], 0).then_inc(dve_done, own.up())
            dve.wait_ge(ev("iotas"), at("iotas", 4))
            v.tensor_scalar(ident[:, :], iota[:, 0:P], iota_p[:, :], None, ALU.is_equal).then_inc(dve_done, own.up())
            v.tensor_scalar(tri, iota[:, 0:P], iota_p[:, :], None, ALU.is_gt).then_inc(dve_done, own.up())
            dve.wait_ge(dve_done, own.count())
            v.tensor_scalar(tmp_s[:, 0, 0:P], ones[:, :], iota_p[:, :], None, ALU.mult).then_inc(dve_done, own.up())
            dve.wait_ge(dve_done, own.count())
            v.tensor_scalar(ones_rest[:, :], tmp_s[:, 0, 0:P], float(NREST), None, ALU.is_lt).then_inc(dve_done, own.up())
            for k in range(6):
                dve.wait_ge(ev(f"rows.in{k}"), at(f"rows.in{k}", 16))
            v.tensor_copy(row_f[:, :, :, :], row_i[:, :, :, :]).then_inc(dve_done, own.up())
            dve.wait_ge(dve_done, own.count())
            v.scalar_tensor_tensor(row_key, row_f[:, 2, :, :], float(KEYSTEP), row_f[:, 0, :, :], ALU.mult, ALU.add).then_inc(dve_done, own.up())
            for c in range(NCH):
                v.tensor_scalar(spread[:, 1, c, :], ones[:, :], tile_no[:, c:c + 1], None, ALU.mult).then_inc(dve_done, own.up())

            def step_list(n):
                nm = f"list{n}"
                shift, nb, cols, width = ((7, NB, SA, WA), (5, NBB, SB, WB))[n]
                for a, lane in ((0, 0), (1, P - 1)):
                    v.tensor_scalar(tci[:, a, :], row_i[:, 0, :, lane], shift, None, ALU.arith_shift_right).then_inc(dve_done, own.up())
                dve.wait_ge(dve_done, own.count())
                v.tensor_copy(tc[:, 0:2, :], tci[:, :, :]).then_inc(dve_done, own.up())
                v.tensor_scalar(tc[:, 5, :], tile_no[:, :], float(NT), None, ALU.is_lt).then_inc(dve_done, own.up())
                v.memset(tc[:, 3, 0:1], 0.0).then_inc(dve_done, own.up())
                dve.wait_ge(dve_done, own.count())
                v.tensor_scalar(tc[:, 0:2, :], tc[:, 0:2, :], float(nb - 1), None, ALU.min).then_inc(dve_done, own.up())
                dve.wait_ge(dve_done, own.count())
                v.tensor_tensor(tc[:, 4, :], tc[:, 1, :], tc[:, 0, :], ALU.subtract).then_inc(dve_done, own.up())
                dve.wait_ge(dve_done, own.count())
                v.scalar_tensor_tensor(tc[:, 2, :], tc[:, 4, :], 1.0, tc[:, 5, :], ALU.add, ALU.mult).then_inc(dve_done, own.up())
                for c in range(1, NCH):
                    dve.wait_ge(dve_done, own.count())
                    v.tensor_tensor(tc[:, 3, c:c + 1], tc[:, 3, c - 1:c], tc[:, 2, c - 1:c], ALU.add).then_inc(dve_done, own.up())
                dve.wait_ge(dve_done, own.count())
                dve.sem_inc(ev(nm + ".counts"), 1)
                dve.wait_ge(ev(nm + ".starts"), at(nm + ".starts", 1))
                v.tensor_copy(tc[:, 6, :], bank[0][:, 0:NCH]).then_inc(dve_done, own.up())
                dve.wait_ge(dve_done, own.count())
                v.tensor_tensor(tc[:, 7, :], tc[:, 6, :], tc[:, 2, :], ALU.add).then_inc(dve_done, own.up())
                v.tensor_tensor(tc[:, 4, :], tc[:, 0, :], tc[:, 6, :], ALU.subtract).then_inc(dve_done, own.up())
                dve.wait_ge(dve_done, own.count())
                for c in range(NCH):
                    v.tensor_scalar(hit[:, c, 0:cols], iota[:, 0:cols], tc[:, 6, c:c + 1], None, ALU.is_ge).then_inc(dve_done, own.up())
                    v.tensor_scalar(spread[:, 0, c, :], ones[:, :], tc[:, 4, c:c + 1], None, ALU.mult).then_inc(dve_done, own.up())
                dve.wait_ge(dve_done, own.count())
                for c in range(NCH):
                    v.scalar_tensor_tensor(hit[:, c, 0:cols], iota[:, 0:cols], tc[:, 7, c:c + 1], hit[:, c, 0:cols], ALU.is_lt, ALU.mult).then_inc(dve_done, own.up())
                dve.wait_ge(dve_done, own.count())
                dve.sem_inc(ev(nm + ".hits"), 1)
                hw = cols // 2
                loc, srct, blk = ((locA, srcA, blkA), (locB, srcB, blkB))[n]
                for hf in range(2):
                    dve.wait_ge(ev(nm + ".picked"), at(nm + ".picked", hf + 1))
                    w = slice(hf * hw, (hf + 1) * hw)
                    a, b, c = tmp_s[:, 0, 0:hw], tmp_s[:, 1, 0:hw], tmp_s[:, 2, 0:hw]
                    v.tensor_tensor(a, bank[2][:, 0:hw], iota[:, w], ALU.mult).then_inc(dve_done, own.up())
                    v.tensor_scalar(c, bank[2][:, 0:hw], -FAR, FAR, ALU.mult, ALU.add).then_inc(dve_done, own.up())
                    dve.wait_ge(dve_done, own.count())
                    v.tensor_tensor(b, bank[1][:, 0:hw], a, ALU.add).then_inc(dve_done, own.up())
                    v.tensor_tensor(c, bank[3][:, 0:hw], c, ALU.add).then_inc(dve_done, own.up())
                    v.tensor_copy(srct[:, w], bank[4][:, 0:hw]).then_inc(dve_done, own.up())
                    dve.wait_ge(dve_done, own.count())
                    v.tensor_copy(blk[:, w], b).then_inc(dve_done, own.up())
                    v.scalar_tensor_tensor(loc[:, w], b, -float(width), c, ALU.mult, ALU.add).then_inc(dve_done, own.up())
                    if n == 0:
                        v.tensor_tensor(rel_hot[:, w, :], bank[5][:, 0:hw].rearrange("p (s a) -> p s a", a=1).broadcast_to([P, hw, R]),
                                           iota[:, 0:R].rearrange("p (a r) -> p a r", a=1).broadcast_to([P, hw, R]), ALU.is_equal).then_inc(dve_done, own.up())
                    else:
                        v.tensor_copy(tileB[:, w], bank[5][:, 0:hw]).then_inc(dve_done, own.up())
                    dve.wait_ge(dve_done, own.count())
                    dve.sem_inc(ev(nm + ".read"), 1)
                dve.sem_inc(ev(nm + ".made"), 1)

            def normalise(name, t, src_t):
                v.tensor_reduce(st[:, 0, :], src_t, AX.X, ALU.add).then_inc(dve_done, own.up())
                dve.wait_ge(dve_done, own.count())
                v.tensor_scalar(st[:, 0, :], st[:, 0, :], 1.0 / D, None, ALU.mult).then_inc(dve_done, own.up())
                dve.wait_ge(dve_done, own.count())
                v.tensor_tensor(t, src_t, per_node(st[:, 0, :]), ALU.subtract).then_inc(ev(name + ".centred"), 1)
                dve.wait_ge(ev(name + ".squared"), at(name + ".squared", 1))
                v.tensor_reduce(st[:, 1, :], scratch, AX.X, ALU.add).then_inc(ev(name + ".var"), 1)
                dve.wait_ge(ev(name + ".root"), at(name + ".root", 1))
                v.reciprocal(st[:, 3, :], st[:, 2, :]).then_inc(dve_done, own.up())
                dve.wait_ge(dve_done, own.count())
                v.tensor_tensor(t, t, per_node(st[:, 3, :]), ALU.mult).then_inc(dve_done, own.up())
                dve.wait_ge(dve_done, own.count())

            def per_node(cols):
                return cols.rearrange("p (b a) -> p b a", a=1).broadcast_to([P, NB, D])

            def per_feature(row):
                return row.rearrange("p (a f) -> p a f", a=1).broadcast_to([P, NB, D])

            def add_up(ph, acc, tab, top, width, h):
                blks = registers(dve, tab, h, top)
                for k in range(H8):
                    step = H8 * h + k
                    dve.wait_ge(ev(ph + ".step_done"), at(ph + ".step_done", 16 + step + 1))
                    dve.wait_ge(ev(ph + ".added"), at(ph + ".added", 8 + step))
                    a = acc[:, bass.ds(blks[k] * width, width)]
                    v.tensor_tensor(a, bank[k][:, 0:width], a, ALU.add).then_inc(ev(ph + ".added"), 1)

            def begin(ph):
                dve.wait_ge(dve_done, own.count())
                dve.sem_inc(ev(ph + ".start"), 1)

            def hots(ph, h, par):
                for k in range(H8):
                    s = par * H8 + k
                    step = H8 * h + k
                    dve.wait_ge(ev(ph + ".step_done"), at(ph + ".step_done", step + 1))
                    v.tensor_scalar(ring_oh[:, s, :], iota[:, 0:P], locA[:, bass.ds(step, 1)], None, ALU.is_equal)\
                        .then_inc(ev(ph + ".hot_made"), 1)

            def plain_phase(ph, acc, width):
                begin(ph)
                dve.sem_inc(ev(ph + ".added"), 8)
                hots(ph, 0, 0)
                with dve.Fori(0, HALVES_A // 2) as i:
                    hots(ph, 2 * i + 1, 1)
                    add_up(ph, acc, blkA, NB, width, 2 * i)
                    hots(ph, 2 * i + 2, 0)
                    add_up(ph, acc, blkA, NB, width, 2 * i + 1)
                add_up(ph, acc, blkA, NB, width, HALVES_A - 1)
                dve.wait_ge(ev(ph + ".added"), at(ph + ".added", 8 + SA))

            step_list(0)
            for k in range(2):
                dve.wait_ge(ev(f"x.in{k}"), at(f"x.in{k}", 16))
            normalise("ln0", H[:, :, :], X[:, :, :])
            v.tensor_scalar(H[:, :, :], H[:, :, :], 0.0, None, ALU.max).then_inc(ev("ln0.ready"), 1)
            plain_phase("sum", arena, A0)
            v.tensor_tensor(X[:, :, :], X[:, :, :], acc0[:, :, 0:D], ALU.add).then_inc(dve_done, own.up())
            v.tensor_reduce(dis[:, :], acc0[:, :, D:D + R], AX.X, ALU.add).then_inc(dve_done, own.up())
            v.tensor_scalar(inv_cnt[:, :, :], acc0[:, :, D:D + R], 1.0, None, ALU.max).then_inc(dve_done, own.up())
            dve.wait_ge(dve_done, own.count())
            v.reciprocal(inv_cnt[:, :, :], inv_cnt[:, :, :]).then_inc(dve_done, own.up())
            step_list(1)

            normalise("ln1", H[:, :, :], X[:, :, :])
            v.tensor_scalar(H[:, :, :], H[:, :, :], 0.0, None, ALU.max).then_inc(ev("ln1.ready"), 1)
            for l, ph in enumerate(("rel0", "rel1")):
                v.memset(acc1, 0.0).then_inc(dve_done, own.up())
                begin(ph)
                dve.sem_inc(ev(ph + ".added"), 8)

                def produce(h, i, par):
                    for k in range(H8):
                        s = par * H8 + k
                        step = H8 * h + k
                        dve.wait_ge(ev(ph + ".step_done"), at(ph + ".step_done", step + 1))
                        v.tensor_scalar(ring_oh2[:, s, :], iota_key[:, :, :].rearrange("p r n -> p (r n)"), locB[:, bass.ds(step, 1)], None, ALU.is_equal)\
                            .then_inc(ev(ph + ".hot_made"), 1)
                        dve.wait_ge(gath[s], gathers_seen(ph, i + 1, par))
                        dve.wait_ge(xe_in[s], edge_rows_seen(ph, i + 1, par))
                        v.tensor_tensor(ring_xe[:, s, :], ring_g[:, s, :], ring_xe[:, s, :], ALU.add).then_inc(ev(ph + ".msg_sum"), 1)

                produce(0, 0, 0)
                with dve.Fori(0, HALVES_B // 2) as i:
                    produce(2 * i + 1, i, 1)
                    add_up(ph, acc1, blkB, NBB, SEG, 2 * i)
                    produce(2 * i + 2, i + 1, 0)
                    add_up(ph, acc1, blkB, NBB, SEG, 2 * i + 1)
                add_up(ph, acc1, blkB, NBB, SEG, HALVES_B - 1)
                for j in range(3):
                    dve.wait_ge(ev(f"{ph}.row{j}"), at(f"{ph}.row{j}", 16))
                start = own.count()
                with dve.Fori(0, NB) as i:
                    own.at(start + 4 * i)
                    dve.wait_ge(ev(ph + ".proj_done"), at(ph + ".proj_done", i + 1))
                    for j in range(2):
                        v.tensor_tensor(relsum[:, 4 * j:4 * j + 4, :], bank[1 + j][:, :].rearrange("p (r f) -> p r f", r=4),
                                           inv_cnt[:, bass.ds(i, 1), 4 * j:4 * j + 4].rearrange("p a (r b) -> p (a r) b", b=1).broadcast_to([P, 4, D]), ALU.mult).then_inc(dve_done, own.up())
                    dve.wait_ge(dve_done, own.count())
                    v.tensor_reduce(relred, relsum.rearrange("p r f -> p f r"), AX.X, ALU.add).then_inc(dve_done, own.up())
                    dve.wait_ge(dve_done, own.count())
                    v.tensor_tensor(relred, relred, bank[3][:, 0:D], ALU.add).then_inc(dve_done, own.up())
                    dve.wait_ge(dve_done, own.count())
                    v.tensor_tensor(Y[:, bass.ds(i, 1), :].rearrange("p a f -> p (a f)"), relred, rows[:, 0, :], ALU.add).then_inc(ev(ph + ".proj_read"), 1)
                own.at(start + 4 * NB)
                dve.wait_ge(ev(ph + ".mean_sum"), at(ph + ".mean_sum", 1))
                v.tensor_scalar(small[:, 256:384], bank[5][:, 0:D], 1.0 / N, None, ALU.mult).then_inc(dve_done, own.up())
                dve.wait_ge(dve_done, own.count())
                v.tensor_tensor(Y[:, :, :], Y[:, :, :], per_feature(small[:, 256:384]), ALU.subtract).then_inc(ev(ph + ".centred"), 1)
                dve.wait_ge(ev(ph + ".var_sum"), at(ph + ".var_sum", 1))
                v.tensor_copy(small[:, 0:128], bank[5][:, 0:D]).then_inc(ev(ph + ".var"), 1)
                dve.wait_ge(ev(ph + ".root"), at(ph + ".root", 1))
                v.reciprocal(small[:, 384:512], small[:, 128:256]).then_inc(dve_done, own.up())
                dve.wait_ge(dve_done, own.count())
                v.tensor_tensor(small[:, 384:512], small[:, 384:512], rows[:, 1, :], ALU.mult).then_inc(dve_done, own.up())
                dve.wait_ge(dve_done, own.count())
                v.tensor_tensor(Y[:, :, :], Y[:, :, :], per_feature(small[:, 384:512]), ALU.mult).then_inc(dve_done, own.up())
                dve.wait_ge(dve_done, own.count())
                v.tensor_tensor(Y[:, :, :], Y[:, :, :], per_feature(rows[:, 2, :]), ALU.add).then_inc(dve_done, own.up())
                dve.wait_ge(dve_done, own.count())
                if l == 0:
                    v.tensor_scalar(H[:, :, :], Y[:, :, :], 0.0, None, ALU.max).then_inc(ev("rel0.over"), 1)
                else:
                    v.tensor_tensor(X[:, :, :], X[:, :, :], Y[:, :, :], ALU.add).then_inc(ev("rel1.over"), 1)
            dve.wait_ge(ev("rel1.over"), at("rel1.over", 1))

            normalise("ln2", H[:, :, :], X[:, :, :])
            v.memset(acc2, 0.0).then_inc(dve_done, own.up())
            v.tensor_scalar(st[:, 1, :], dis[:, :], 1.0, None, ALU.add).then_inc(dve_done, own.up())
            v.tensor_scalar(H[:, :, :], H[:, :, :], 0.0, None, ALU.max).then_inc(ev("ln2.ready"), 1)
            dve.wait_ge(dve_done, own.count())
            v.tensor_copy(st[:, 3, :], st[:, 1, :]).then_inc(ev("deg.made"), 1)
            dve.wait_ge(ev("deg.root"), at("deg.root", 1))
            v.reciprocal(dis[:, :], st[:, 2, :]).then_inc(dve_done, own.up())
            dve.wait_ge(dve_done, own.count())
            with dve.Fori(0, NB) as i:
                dve.wait_ge(ev("gcn.proj_done"), at("gcn.proj_done", i + 1))
                v.tensor_scalar(y2[:, bass.ds(i, 1), :].rearrange("p a f -> p (a f)"), bank[1][:, 0:D], dis[:, bass.ds(i, 1)], None, ALU.mult)\
                    .then_inc(ev("gcn.proj_read"), 1)
            dve.wait_ge(ev("gcn.proj_read"), at("gcn.proj_read", NB))
            dve.sem_inc(ev("gcn.table_made"), 1)
            plain_phase("gcn", arena, D)
            for j in range(3):
                dve.wait_ge(ev(f"gcn.row{j}"), at(f"gcn.row{j}", 16))
            v.tensor_tensor(Y[:, :, :], acc2, y2, ALU.add).then_inc(dve_done, own.up())
            dve.wait_ge(dve_done, own.count())
            v.tensor_tensor(Y[:, :, :], Y[:, :, :], per_node(dis[:, :]), ALU.mult).then_inc(dve_done, own.up())
            dve.wait_ge(dve_done, own.count())
            v.tensor_tensor(Y[:, :, :], Y[:, :, :], per_feature(rows[:, 0, :]), ALU.add).then_inc(dve_done, own.up())
            dve.wait_ge(dve_done, own.count())
            v.tensor_tensor(Y[:, :, :], Y[:, :, :], H[:, :, :], ALU.add).then_inc(dve_done, own.up())
            dve.wait_ge(dve_done, own.count())
            normalise("gcn_ln", Y[:, :, :], Y[:, :, :])
            v.tensor_tensor(Y[:, :, :], Y[:, :, :], per_feature(rows[:, 1, :]), ALU.mult).then_inc(dve_done, own.up())
            dve.wait_ge(dve_done, own.count())
            v.tensor_tensor(Y[:, :, :], Y[:, :, :], per_feature(rows[:, 2, :]), ALU.add).then_inc(dve_done, own.up())
            dve.wait_ge(dve_done, own.count())
            v.tensor_scalar(Y[:, :, :], Y[:, :, :], 0.0, None, ALU.max).then_inc(dve_done, own.up())
            dve.wait_ge(dve_done, own.count())
            v.tensor_tensor(X[:, :, :], X[:, :, :], Y[:, :, :], ALU.add).then_inc(ev("gcn.over"), 1)
            dve.wait_ge(ev("gcn.over"), at("gcn.over", 1))

            normalise("ln3", H[:, :, :], X[:, :, :])
            v.tensor_scalar(H[:, :, :], H[:, :, :], 0.0, None, ALU.max).then_inc(ev("ln3.ready"), 1)
            for l, ph in enumerate(("att0", "att1")):
                nh = (4, 1)[l]
                ch = D // nh
                q8 = H8 * nh
                aw = D + nh
                rw = aw + nh + 1
                rhs = rhs3[:, 0:H8 * rw].rearrange("p (s f) -> p s f", s=H8)
                acc = acc3[:, 0:NB * aw]
                opart = part[:, 0:H8 * aw].rearrange("p (s f) -> p s f", s=H8)
                dif, ex, ab = fl[:, 0:q8], fl[:, 64:64 + q8], fl[:, 256:256 + 2 * q8]
                logits, locs = fl[:, 128:128 + q8], fl[:, 192:192 + q8]
                pres, mnew = fl[:, 320:320 + H8], fl[:, 336:336 + q8]
                mold, mstep = fl[:, 1168:1168 + q8], fl[:, 1200:1200 + q8]
                keyT = fl[0:q8, 384:384 + P]
                reset = fl[0:q8, 512:512 + P + 1]
                tri3 = fl[0:q8, 648:648 + 3 * P].rearrange("p (a f) -> p a f", a=3)
                fwd = fl[0:q8, 1040:1040 + P]
                for j in range(4):
                    dve.wait_ge(ev(f"{ph}.b{j}"), at(f"{ph}.b{j}", 16))
                start = own.count()
                with dve.Fori(0, NB) as i:
                    own.at(start + 2 * i)
                    dve.wait_ge(ev(ph + ".proj_done"), at(ph + ".proj_done", i + 1))
                    v.tensor_tensor(qt[:, bass.ds(D * i, D)], bank[1][:, 0:D], bqkvs[:, 0:D], ALU.add).then_inc(dve_done, own.up())
                    v.tensor_tensor(kvt[:, bass.ds(i, 1), :].rearrange("p a f -> p (a f)"), bank[1][:, D:3 * D], bqkvs[:, D:3 * D], ALU.add).then_inc(dve_done, own.up())
                    v.tensor_tensor(skip[:, bass.ds(i, 1), :].rearrange("p a f -> p (a f)"), bank[1][:, 3 * D:4 * D], bqkvs[:, 3 * D:4 * D], ALU.add)\
                        .then_inc(ev(ph + ".proj_read"), 1)
                own.at(start + 2 * NB)
                dve.wait_ge(dve_done, own.count())
                dve.wait_ge(ev(ph + ".proj_read"), at(ph + ".proj_read", NB))
                dve.sem_inc(ev(ph + ".table_made"), 1)
                v.memset(acc, 0.0).then_inc(dve_done, own.up())
                v.memset(mst[:, 0:NB * nh], -BIG).then_inc(dve_done, own.up())
                v.memset(reset[:, 0:1], -BIG).then_inc(dve_done, own.up())
                v.memset(reset[:, P:P + 1], -BIG).then_inc(dve_done, own.up())
                v.memset(tri3[:, 2, 0:1], 1.0).then_inc(dve_done, own.up())
                begin(ph)

                def make_logits(h, i, par):
                    v.tensor_scalar(locs.rearrange("p (s a) -> p s a", a=nh),
                                    locA[:, bass.ds(H8 * h, H8)].rearrange("p (s a) -> p s a", a=1).broadcast_to([P, H8, nh]), 1.0, None, ALU.mult)\
                        .then_inc(dve_done, own.up())
                    for j in range(2):
                        dve.wait_ge(ev(ph + ".q_done"), at(ph + ".q_done", 2 * h + j + 1))
                        for k in range(4):
                            dve.wait_ge(gath[par * H8 + 4 * j + k], gathers_seen(ph, i + 1, par))
                        v.tensor_tensor(prod[:, 4 * j:4 * j + 4, :], bank[2 + j][:, :].rearrange("p (s f) -> p s f", s=4),
                                        ring_kv[:, par * H8 + 4 * j:par * H8 + 4 * j + 4, 0:D], ALU.mult).then_inc(dve_done, own.up())
                    dve.wait_ge(dve_done, own.count())
                    v.tensor_reduce(logits, prod.rearrange("p s (a c) -> p (s a) c", a=nh), AX.X, ALU.add).then_inc(ev(ph + ".logits"), 1)

                def run_maxima(h):
                    dve.wait_ge(ev(ph + ".logT"), at(ph + ".logT", h + 1))
                    v.tensor_copy(keyT, bank[4][0:q8, P:2 * P]).then_inc(dve_done, own.up())
                    dve.wait_ge(dve_done, own.count())
                    v.tensor_tensor(tri3[:, 2, 1:P], keyT[:, 1:P], keyT[:, 0:P - 1], ALU.not_equal).then_inc(dve_done, own.up())
                    dve.wait_ge(dve_done, own.count())
                    v.tensor_scalar(reset[:, 1:P], tri3[:, 2, 1:P], -BIG, None, ALU.mult).then_inc(dve_done, own.up())
                    dve.wait_ge(dve_done, own.count())
                    v.tensor_tensor_scan(fwd, reset[:, 0:P], bank[4][0:q8, 0:P], -BIG, ALU.add, ALU.max).then_inc(dve_done, own.up())
                    dve.wait_ge(dve_done, own.count())
                    v.tensor_tensor_scan(tri3[:, 0, ::-1], reset[:, 1:P + 1][:, ::-1], fwd[:, ::-1], -BIG, ALU.add, ALU.max).then_inc(dve_done, own.up())
                    dve.wait_ge(dve_done, own.count())
                    v.tensor_tensor(tri3[:, 1, :], tri3[:, 0, :], tri3[:, 2, :], ALU.mult).then_inc(ev(ph + ".max_made"), 1)

                def subtract_maxima(h):
                    dve.wait_ge(ev(ph + ".maxT"), at(ph + ".maxT", h + 1))
                    v.tensor_tensor(dif, logits, bank[4][:, 2 * P:2 * P + q8], ALU.subtract).then_inc(ev(ph + ".diff"), 1)

                def make_rhs(h, par):
                    v.tensor_copy(rhs[:, :, aw:aw + nh], bank[4][:, 2 * P + q8:2 * P + 2 * q8].rearrange("p (s a) -> p s a", a=nh)).then_inc(dve_done, own.up())
                    v.tensor_copy(rhs[:, :, aw + nh:rw], bank[4][:, 2 * P + 2 * q8:2 * P + 3 * q8].rearrange("p (s a) -> p s a", a=nh)[:, :, 0:1])\
                        .then_inc(dve_done, own.up())
                    dve.wait_ge(ev(ph + ".exped"), at(ph + ".exped", h + 1))
                    heads = rhs[:, :, 0:aw].rearrange("p s (a c) -> p s a c", a=nh)
                    v.tensor_copy(heads[:, :, :, ch:ch + 1].rearrange("p s a c -> p s (a c)"), ex.rearrange("p (s a) -> p s a", a=nh))\
                        .then_inc(dve_done, own.up())
                    exb = ex.rearrange("p (s a b) -> p s a b", a=nh, b=1).broadcast_to([P, H8, nh, ch])
                    v.tensor_tensor(heads[:, :, :, 0:ch], ring_kv[:, par * H8:par * H8 + H8, D:2 * D].rearrange("p s (a c) -> p s a c", a=nh),
                                    exb, ALU.mult).then_inc(dve_done, own.up())
                    dve.wait_ge(dve_done, own.count())
                    dve.sem_inc(ev(ph + ".rhs_made"), 1)

                def merge_maxima(h, blks):
                    dve.wait_ge(ev(ph + ".step_done"), at(ph + ".step_done", 16 + H8 * h + H8))
                    for j in range(3):
                        m = min(3, H8 - 3 * j)
                        v.tensor_scalar(pres[:, 3 * j:3 * j + m], bank[5 + j][:, 0:m * rw].rearrange("p (s f) -> p s f", s=m)[:, :, rw - 1],
                                        BIG, -BIG, ALU.mult, ALU.add).then_inc(dve_done, own.up())
                    dve.wait_ge(dve_done, own.count())
                    for j in range(3):
                        m = min(3, H8 - 3 * j)
                        v.tensor_tensor(mstep[:, 3 * j * nh:(3 * j + m) * nh].rearrange("p (s a) -> p s a", a=nh),
                                        bank[5 + j][:, 0:m * rw].rearrange("p (s f) -> p s f", s=m)[:, :, aw:aw + nh],
                                        pres[:, 3 * j:3 * j + m].rearrange("p (s a) -> p s a", a=1).broadcast_to([P, m, nh]), ALU.add)\
                            .then_inc(dve_done, own.up())
                    for k in range(H8):
                        state = mst[:, bass.ds(blks[k] * nh, nh)]
                        dve.wait_ge(dve_done, own.count())
                        v.tensor_scalar(mold[:, k * nh:(k + 1) * nh], state, 1.0, None, ALU.mult).then_inc(dve_done, own.up())
                        v.tensor_tensor(state, state, mstep[:, k * nh:(k + 1) * nh], ALU.max).then_inc(dve_done, own.up())
                    dve.wait_ge(dve_done, own.count())
                    v.tensor_tensor(mnew, mold, mstep, ALU.max).then_inc(dve_done, own.up())
                    dve.wait_ge(dve_done, own.count())
                    v.tensor_tensor(ab[:, 0:q8], mold, mnew, ALU.subtract).then_inc(dve_done, own.up())
                    v.tensor_tensor(ab[:, q8:2 * q8], mstep, mnew, ALU.subtract).then_inc(dve_done, own.up())
                    dve.wait_ge(dve_done, own.count())
                    dve.sem_inc(ev(ph + ".resc"), 1)

                def new_parts(h):
                    dve.wait_ge(ev(ph + ".resc_exped"), at(ph + ".resc_exped", h + 1))
                    for j in range(3):
                        m = min(3, H8 - 3 * j)
                        v.tensor_tensor(opart[:, 3 * j:3 * j + m, :].rearrange("p s (a c) -> p s a c", a=nh),
                                        bank[5 + j][:, 0:m * rw].rearrange("p (s f) -> p s f", s=m)[:, :, 0:aw].rearrange("p s (a c) -> p s a c", a=nh),
                                        ab[:, q8 + 3 * j * nh:q8 + (3 * j + m) * nh].rearrange("p (s a b) -> p s a b", a=nh, b=1).broadcast_to([P, m, nh, ch + 1]),
                                        ALU.mult).then_inc(dve_done, own.up())

                def merge_sums(h, blks, ks):
                    for k in ks:
                        a = acc[:, bass.ds(blks[k] * aw, aw)]
                        a3 = a.rearrange("p (a c) -> p a c", a=nh)
                        dve.wait_ge(dve_done, own.count())
                        if nh > 1:
                            v.tensor_tensor(a3, a3, ab[:, k * nh:(k + 1) * nh].rearrange("p (a b) -> p a b", b=1).broadcast_to([P, nh, ch + 1]), ALU.mult)\
                                .then_inc(dve_done, own.up())
                            dve.wait_ge(dve_done, own.count())
                            v.tensor_tensor(a, a, opart[:, k, :], ALU.add).then_inc(dve_done, own.up())
                        else:
                            dve.wait_ge(ev(ph + ".parted"), at(ph + ".parted", H8 * h + k + 1))
                            v.scalar_tensor_tensor(a, a, ab[:, k:k + 1], opart[:, k, :], ALU.mult, ALU.add).then_inc(dve_done, own.up())
                    if ks[-1] == H8 - 1:
                        dve.wait_ge(dve_done, own.count())
                        dve.sem_inc(ev(ph + ".added"), 1)

                def half(h, i, par):
                    first = isinstance(h, int) and h == 0
                    own.at(start + (0 if first else FIRST + (h - 1) * PER))
                    make_logits(h, i, par)
                    hots(ph, h + 1, 1 - par)
                    if not first:
                        blks = registers(dve, blkA, h - 1, NB)
                        merge_maxima(h - 1, blks)
                    run_maxima(h)
                    if not first:
                        if nh > 1:
                            new_parts(h - 1)
                        merge_sums(h - 1, blks, range(H8 // 2))
                    subtract_maxima(h)
                    if not first:
                        merge_sums(h - 1, blks, range(H8 // 2, H8))
                    make_rhs(h, par)
                    assert own.k == (FIRST if first else PER), own.k

                start = own.count()
                FIRST = 3 + 5 + 4
                PER = FIRST + (6 + 2 * H8 + 3) + (3 + 2 * H8 if nh > 1 else H8)
                hots(ph, 0, 0)
                skewed(dve, half)
                own.at(start + FIRST + (HALVES_A - 1) * PER)
                blks = registers(dve, blkA, HALVES_A - 1, NB)
                merge_maxima(HALVES_A - 1, blks)
                if nh > 1:
                    new_parts(HALVES_A - 1)
                merge_sums(HALVES_A - 1, blks, range(H8))
                dve.wait_ge(dve_done, own.count())
                a4 = acc.rearrange("p (b a c) -> p b a c", b=NB, a=nh)
                den = small[:, 0:NB * nh].rearrange("p (b a) -> p b a", b=NB)
                v.tensor_scalar(den, a4[:, :, :, ch:ch + 1].rearrange("p b a c -> p b (a c)"), 1e-16, None, ALU.add).then_inc(dve_done, own.up())
                dve.wait_ge(dve_done, own.count())
                v.reciprocal(den, den).then_inc(dve_done, own.up())
                dve.wait_ge(dve_done, own.count())
                y4 = Y[:, :, :].rearrange("p b (a c) -> p b a c", a=nh)
                v.tensor_tensor(y4, a4[:, :, :, 0:ch], small[:, 0:NB * nh].rearrange("p (b a c) -> p b a c", b=NB, c=1).broadcast_to([P, NB, nh, ch]), ALU.mult).then_inc(dve_done, own.up())
                dve.wait_ge(dve_done, own.count())
                v.tensor_tensor(Y[:, :, :], Y[:, :, :], skip, ALU.add).then_inc(dve_done, own.up())
                dve.wait_ge(dve_done, own.count())
                if l == 0:
                    v.tensor_scalar(H[:, :, :], Y[:, :, :], 0.0, None, ALU.max).then_inc(ev("att0.over"), 1)
                else:
                    v.tensor_tensor(X[:, :, :], X[:, :, :], Y[:, :, :], ALU.add).then_inc(ev("att1.over"), 1)


_INS = ["x", "src", "dst", "edge_attr_128", "edge_type_8", "L1_gnn_weight", "L1_gnn_root", "L1_gnn_bias", "L1_gnn_bn_gamma",
        "L1_gnn_bn_beta", "L2_gnn_W", "L2_gnn_b", "L2_gnn_gamma", "L2_gnn_beta",
        "L3_gnn_w1_q", "L3_gnn_b1_q", "L3_gnn_w1_k", "L3_gnn_b1_k", "L3_gnn_w1_v", "L3_gnn_b1_v", "L3_gnn_w1_s", "L3_gnn_b1_s",
        "L3_gnn_w2_q", "L3_gnn_b2_q", "L3_gnn_w2_k", "L3_gnn_b2_k", "L3_gnn_w2_v", "L3_gnn_b2_v", "L3_gnn_w2_s", "L3_gnn_b2_s"]


def kernel(**inputs):
    import numpy as _np
    import concourse.bacc as _bacc
    from concourse import mybir as _mybir
    from concourse.bass_utils import run_bass_kernel_spmd as _run

    nc = _bacc.Bacc("TRN2", target_bir_lowering=False, num_devices=1)
    arrays, args = {}, []
    pads = {"src": 0, "dst": PAD_DST, "edge_type_8": 0, "edge_attr_128": 0}
    for name in _INS:
        a = _np.ascontiguousarray(inputs[name])
        if name in pads:
            rest = _np.full((EP - E,) + a.shape[1:], pads[name], a.dtype)
            a = _np.concatenate([a, rest])
        arrays[f"in_{name}"] = a
        args.append(nc.dram_tensor(f"in_{name}", a.shape, _mybir.dt.from_np(a.dtype), kind="ExternalInput").ap())
    args.append(nc.dram_tensor("h_table", (NP, D), F32).ap())
    args.append(nc.dram_tensor("kv_table", (NP, 2 * D), F32).ap())
    args.append(nc.dram_tensor("out_0", (N, D), F32, kind="ExternalOutput").ap())
    gnn_kernel(nc, *args)
    r = _run(nc, [arrays], core_ids=[0])
    return r.results[0]["out_0"]
```

```python
import concourse.bass as bass
from concourse import mybir
from contextlib import ExitStack

F32 = mybir.dt.float32
I32 = mybir.dt.int32
ALU = mybir.AluOpType
ACT = mybir.ActivationFunctionType
AX = mybir.AxisListType

P = 128
D = 128
N = 3125
E = 53125
NB = -(-N // P)
NP = NB * P
NREST = N - (NB - 1) * P
NT = -(-E // P)
EP = NT * P
NCH = -(-NT // P)
NTREST = NT - (NCH - 1) * P
PAD_DST = 4095
R = 8
KEYSTEP = 4096
WA, WB = P, 32
NBB = -(-N // WB)
H8 = 8
STEPS_A = NT + NB - 1
STEPS_B = NT + NBB - 1
HALVES_A = -(-STEPS_A // H8)
HALVES_B = -(-STEPS_B // H8)
assert HALVES_A % 2 == 1 and HALVES_B % 2 == 1
SA = HALVES_A * H8
SB = HALVES_B * H8
SEG = R * WB
FAR = 1.0e6
BIG = 1.0e30
EPS = 1e-5
RW_MAX = 137


class Count:

    def __init__(self):
        self.base, self.k, self.marked = 0, 0, 0

    def up(self):
        self.k += 1
        return 1

    def count(self):
        return self.base + self.k

    def at(self, base):
        self.base, self.k = base, 0


def gnn_kernel(nc, x, src, dst, xe, ety, w1, root, bias1, bng, bnb, w2, b2, g2, be2,
               waq, baq, wak, bak, wav, bav, was, bas, wbq, bbq, wbk, bbk, wbv, bbv, wbs, bbs,
               h_tab, kv_tab, out):
    ctx = ExitStack()
    with ctx:
        def sb(name, shape, dt=F32):
            return ctx.enter_context(nc.sbuf_tensor(name, shape, dt))

        def sem(name):
            return ctx.enter_context(nc.semaphore(name))

        X = sb("X", [P, NB, D])
        H = sb("H", [P, NB, D])
        Y = sb("Y", [P, NB, D])
        arena = sb("arena", [P, R * NP])
        rings = sb("rings", [P, 8192])
        iota = sb("iota", [P, SB])
        iota_p = sb("iota_p", [P, 1])
        iota_key = sb("iota_key", [P, R, WB])
        tile_no = sb("tile_no", [P, NCH])
        ident = sb("ident", [P, P])
        ones = sb("ones", [P, P])
        ones_rest = sb("ones_rest", [P, P])
        eps_col = sb("eps_col", [P, 1])
        locA = sb("locA", [P, SA + H8])
        srcA = sb("srcA", [P, SA + H8], I32)
        blkA = sb("blkA", [P, SA + H8], I32)
        locB = sb("locB", [P, SB])
        srcB = sb("srcB", [P, SB], I32)
        blkB = sb("blkB", [P, SB], I32)
        tileB = sb("tileB", [P, SB], I32)
        idx = sb("idx", [P, 2, H8], I32)
        wrel = sb("wrel", [P, R + 1, D])
        rows = sb("rows", [P, 3, D])
        inv_cnt = sb("inv_cnt", [P, NB, R])
        dis = sb("dis", [P, NB])
        st = sb("st", [P, 4, NB])
        small = sb("small", [P, 512])

        ring_g = rings[:, 0:2048].rearrange("p (s f) -> p s f", s=16)
        ring_xe = rings[:, 2048:4096].rearrange("p (s f) -> p s f", s=16)
        ring_oh2 = rings[:, 4096:8192].rearrange("p (s f) -> p s f", s=16)
        ring_kv = rings[:, 0:4096].rearrange("p (s f) -> p s f", s=16)
        ring_oh = rings[:, 4096:6144].rearrange("p (s f) -> p s f", s=16)
        oh_t = rings[:, 6144:7168].rearrange("p (s f) -> p s f", s=8)
        prod = rings[:, 7168:8192].rearrange("p (s f) -> p s f", s=8)
        acb = [rings[:, j * 1024:(j + 1) * 1024] for j in range(2)]
        h_fix = [rings[:, 2048 + j * P:2048 + (j + 1) * P] for j in range(2)]
        hT_fix = [rings[:, 2304 + j * P:2304 + (j + 1) * P] for j in range(2)]
        relsum = rings[:, 2560:3584].rearrange("p (r f) -> p r f", r=R)
        relred = rings[:, 3584:3712]

        bank = [ctx.enter_context(nc.psum_tensor(f"bank{i}", [P, 512], F32)) for i in range(8)]

        o = 8192
        row_i = arena[:, o:o + 3 * NCH * P].bitcast(I32).rearrange("p (a c f) -> p a c f", a=3, c=NCH); o += 3 * NCH * P
        row_f = arena[:, o:o + 3 * NCH * P].rearrange("p (a c f) -> p a c f", a=3, c=NCH); o += 3 * NCH * P
        row_key = arena[:, o:o + NCH * P].rearrange("p (c f) -> p c f", c=NCH); o += NCH * P
        hit = arena[:, o:o + NCH * SB].rearrange("p (c s) -> p c s", c=NCH); o += NCH * SB
        spread = arena[:, o:o + 2 * NCH * P].rearrange("p (a c f) -> p a c f", a=2, c=NCH); o += 2 * NCH * P
        tri = arena[:, o:o + P]; o += P
        tmp_s = arena[:, o:o + 3 * SB].rearrange("p (a s) -> p a s", a=3); o += 3 * SB
        tc = arena[:, o:o + 9 * NCH].rearrange("p (a c) -> p a c", a=9); o += 9 * NCH
        tci = arena[:, o:o + 2 * NCH].bitcast(I32).rearrange("p (a c) -> p a c", a=2); o += 2 * NCH
        assert o <= 21000
        A0 = D + R
        acc0 = arena[:, 0:NB * A0].rearrange("p (b f) -> p b f", b=NB)
        rel_hot = arena[:, 4096:4096 + SA * R].rearrange("p (s r) -> p s r", r=R)
        acc1 = arena[:, :]
        acc2 = arena[:, 0:NP].rearrange("p (b f) -> p b f", b=NB)
        y2 = arena[:, NP:2 * NP].rearrange("p (b f) -> p b f", b=NB)
        scratch = arena[:, R * NP - NP:R * NP].rearrange("p (b f) -> p b f", b=NB)
        qt = arena[:, 0:NP]
        skip = arena[:, NP:2 * NP].rearrange("p (b f) -> p b f", b=NB)
        kvt = arena[:, 2 * NP:4 * NP].rearrange("p (b f) -> p b f", b=NB)
        o = 4 * NP
        wqkvs = arena[:, o:o + 4 * D]; o += 4 * D
        bqkvs = arena[:, o:o + 4 * D]; o += 4 * D
        acc3 = arena[:, o:o + NB * 132]; o += NB * 132
        part = arena[:, o:o + H8 * 132]; o += H8 * 132
        rhs3 = arena[:, o:o + H8 * RW_MAX]; o += H8 * RW_MAX
        assert o <= R * NP - NP
        fl = sb("fl", [P, 1536])
        mst = sb("mst", [P, NB * 4])

        ORDER = ["list0", "ln0", "sum", "list1", "ln1", "rel0", "rel1", "ln2", "gcn", "gcn_ln", "ln3", "att0", "att1"]
        PHASES = ["sum", "rel0", "rel1", "gcn", "att0", "att1"]
        RELS, ATTS, PROJ = ("rel0", "rel1"), ("att0", "att1"), ("rel0", "rel1", "gcn", "att0", "att1")
        halves_of = {ph: HALVES_B if ph in RELS else HALVES_A for ph in PHASES}
        LOADS = ("table", "w", "w_root", "row0", "row1", "row2", "w0", "w1", "w2", "w3", "b0", "b1", "b2", "b3")

        def total(stage, event):
            hv = halves_of.get(stage, 0)
            if event == "idx_made":
                return hv + (stage in ATTS)
            if event == "hot_made":
                return (hv + (stage in ATTS)) * H8
            if event == "step_done":
                return 16 * (hv > 0) + hv * H8
            if event == "added":
                return hv if stage in ATTS else 8 * (hv > 0) + hv * H8
            if event in ("msg_sum", "msg_made"):
                return hv * H8 * (stage in RELS)
            if event in ("hotT", "hotT_copied", "q_done"):
                return 2 * (hv + 1) * (stage in ATTS)
            if event in ("logits", "logT", "max_made", "maxT", "diff", "exped", "resc", "resc_exped"):
                return hv * (stage in ATTS)
            if event == "rhs_made":
                return hv * {"att0": 1, "att1": H8}.get(stage, 0)
            if event == "parted":
                return hv * H8 * (stage in ATTS)
            if event in ("locs_made", "keyT_made"):
                return hv * (stage in ATTS)
            if event == "marked":
                return 2 * hv * (stage in ATTS)
            if event in ("h_fixed", "hT_done", "hT_made", "proj_done", "proj_read"):
                return NB * (stage in PROJ)
            if event == "sums_fixed":
                return NB * (stage in RELS)
            if event in ("picked", "read"):
                return 2 * (stage in ("list0", "list1"))
            if event in ("counts", "starts", "hits", "made"):
                return 1 * (stage in ("list0", "list1"))
            if event in ("centred", "squared"):
                return 1 * (stage[:2] == "ln" or stage in ("gcn_ln",) + RELS)
            if event in ("var", "root"):
                return 1 * (stage[:2] == "ln" or stage in ("gcn_ln",) + RELS)
            if event == "ready":
                return 1 * (stage[:2] == "ln")
            if event in ("mean_sum", "var_sum"):
                return 1 * (stage in RELS)
            if event == "table_made":
                return 1 * (stage in ("gcn",) + ATTS)
            if event == "start":
                return 1 * (hv > 0)
            if event == "over":
                return 1 * (stage in PROJ)
            if event in LOADS:
                of = dict(table=PHASES, w=("rel0", "rel1", "gcn"), w_root=RELS, row0=("rel0", "rel1", "gcn"), row1=("rel0", "rel1", "gcn"),
                          row2=("rel0", "rel1", "gcn")).get(event, ATTS)
                return 16 * (stage in of)
            raise KeyError(event)

        PRIME = 2
        PRIMED = {"pe": ("hT_done", "proj_done", "q_done"), "act": ("hT_made",), "dve": ("proj_read",)}

        def prime(eng, name):
            for event in PRIMED[name]:
                eng.sem_inc(ev("rel0." + event), PRIME)

        made = {}

        def ev(name):
            stage, _, event = name.rpartition(".")
            key = event if stage in ORDER else name.replace(".", "_")
            if key not in made:
                made[key] = ctx.enter_context(nc.semaphore(key))
            return made[key]

        def at(name, count):
            stage, _, event = name.rpartition(".")
            if stage not in ORDER:
                return count
            before = sum(total(q, event) for q in ORDER[:ORDER.index(stage)])
            return before + PRIME * any(event in events for events in PRIMED.values()) + count

        gath = [ev(f"gathered{k}") for k in range(16)]
        xe_in = [ev(f"edge_rows_in{k}") for k in range(16)]

        def rounds_before(ph, par, phases=PHASES):
            return sum((halves_of[q] + 1 - par) // 2 for q in phases[:phases.index(ph)])

        def gathers_seen(ph, i, par):
            return 16 * (rounds_before(ph, par) + i)

        def edge_rows_seen(ph, i, par):
            return 16 * (rounds_before(ph, par, ["rel0", "rel1"]) + i)

        def halves(eng, count, body):
            with eng.Fori(0, count // 2) as i:
                body(2 * i, i, 0)
                body(2 * i + 1, i, 1)
            body(count - 1, count // 2, 0)

        def skewed(eng, body):
            body(0, 0, 0)
            with eng.Fori(0, HALVES_A // 2) as i:
                body(2 * i + 1, i, 1)
                body(2 * i + 2, i + 1, 0)

        def registers(eng, table, h, top):
            _, regs = nc.values_load_multi_w_load_instructions(
                table[0:1, bass.ds(H8 * h, H8)], engines=[eng.engine], min_val=0, max_val=top - 1,
                skip_runtime_bounds_check_because="the step list's entries are below this by construction")
            return regs

        block = ctx.enter_context(nc.Block())

        @block.sync
        def _(sp):
            full = (NCH - 1) * P
            sp.wait_ge(ev("rows.zeroed"), at("rows.zeroed", 1))
            for a, arr in enumerate((dst, src, ety)):
                v = arr.rearrange("(t p) -> t p", p=P)
                sp.dma_start(row_i[:, a, 0:NCH - 1, :], v[0:full, :].rearrange("(c t) p -> t c p", t=P)).then_inc(ev(f"rows.in{2 * a}"), 16)
                sp.dma_start(row_i[0:NTREST, a, NCH - 1, :], v[full:NT, :]).then_inc(ev(f"rows.in{2 * a + 1}"), 16)
            sp.wait_ge(ev("x.zeroed"), at("x.zeroed", 1))
            sp.dma_start(X[:, 0:NB - 1, :], x[0:(NB - 1) * P, :].rearrange("(b p) f -> p b f", p=P)).then_inc(ev("x.in0"), 16)
            sp.dma_start(X[0:NREST, NB - 1, :], x[(NB - 1) * P:N, :]).then_inc(ev("x.in1"), 16)

            def store_table(ph, rows_t, tab, ready):
                sp.wait_ge(ev(ready), at(ready, 1))
                sp.dma_start(tab.rearrange("(b p) f -> p b f", p=P), rows_t).then_inc(ev(ph + ".table"), 16)

            def load_rel(layer):
                ph = f"rel{layer}"
                sp.dma_start(wrel[:, 0:R, :], w1[layer].rearrange("r k n -> k r n")).then_inc(ev(ph + ".w"), 16)
                sp.dma_start(wrel[:, R, :], root[layer]).then_inc(ev(ph + ".w_root"), 16)
                for j, v in enumerate((bias1, bng, bnb)):
                    sp.dma_start(rows[:, j, :], v[layer:layer + 1, :].broadcast_to([P, D])).then_inc(ev(f"{ph}.row{j}"), 16)

            def load_edge_rows(ph):
                def half(h, i, par):
                    tiles = registers(sp, tileB, h, NT)
                    for k in range(H8):
                        s = par * H8 + k
                        sp.wait_ge(ev(ph + ".step_done"), at(ph + ".step_done", H8 * h + k + 1))
                        sp.dma_start(ring_xe[:, s, :], xe[bass.ds(tiles[k] * P, P), :]).then_inc(xe_in[s], 16)
                halves(sp, HALVES_B, half)

            load_rel(0)
            store_table("sum", H[:, :, :], h_tab, "ln0.ready")
            store_table("rel0", H[:, :, :], h_tab, "ln1.ready")
            sp.wait_ge(ev("list1.made"), at("list1.made", 1))
            load_edge_rows("rel0")
            sp.wait_ge(ev("rel0.over"), at("rel0.over", 1))
            load_rel(1)
            store_table("rel1", H[:, :, :], h_tab, "rel0.over")
            load_edge_rows("rel1")
            sp.wait_ge(ev("rel1.over"), at("rel1.over", 1))
            sp.dma_start(wrel[:, 0, :], w2).then_inc(ev("gcn.w"), 16)
            for j, v in enumerate((b2, g2, be2)):
                sp.dma_start(rows[:, j, :], v.rearrange("(a f) -> a f", a=1).broadcast_to([P, D])).then_inc(ev(f"gcn.row{j}"), 16)
            store_table("gcn", y2, h_tab, "gcn.table_made")
            weights = ((waq, wak, wav, was), (wbq, wbk, wbv, wbs))
            biases = ((baq, bak, bav, bas), (bbq, bbk, bbv, bbs))
            for l, ph in enumerate(("att0", "att1")):
                sp.wait_ge(ev(("gcn.over", "att0.over")[l]), at(("gcn.over", "att0.over")[l], 1))
                for j in range(4):
                    sp.dma_start(wqkvs[:, j * D:(j + 1) * D], weights[l][j]).then_inc(ev(f"{ph}.w{j}"), 16)
                    sp.dma_start(bqkvs[:, j * D:(j + 1) * D], biases[l][j].rearrange("(a f) -> a f", a=1).broadcast_to([P, D]))\
                      .then_inc(ev(f"{ph}.b{j}"), 16)
                store_table(ph, kvt, kv_tab, ph + ".table_made")
            sp.wait_ge(ev("att1.over"), at("att1.over", 1))
            sp.dma_start(out[0:(NB - 1) * P, :].rearrange("(b p) f -> p b f", p=P), X[:, 0:NB - 1, :]).then_inc(ev("out0"), 16)
            sp.dma_start(out[(NB - 1) * P:N, :], X[0:NREST, NB - 1, :]).then_inc(ev("out1"), 16)
            sp.wait_ge(ev("out0"), at("out0", 16))
            sp.wait_ge(ev("out1"), at("out1", 16))

        @block.gpsimd
        def _(pool):
            kw = dict(allow_small_or_imprecise_dtypes=True)
            for t, pattern, cm in ((iota[:, :], [[1, SB]], 0), (iota_p[:, :], [[1, 1]], 1), (iota_key[:, :, :], [[KEYSTEP, R], [1, WB]], 0), (tile_no[:, :], [[P, NCH]], 1)):
                nc.gpsimd.iota(t, pattern=pattern, base=0, channel_multiplier=cm, **kw).then_inc(ev("iotas"), 1)
            for ph in PHASES:
                att = ph in ("att0", "att1")
                table, ring = (kv_tab, ring_kv) if att else (h_tab, ring_g)
                pool.wait_ge(ev(ph + ".table"), at(ph + ".table", 16))

                def half(h, i, par):
                    pool.wait_ge(ev(ph + ".idx_made"), at(ph + ".idx_made", h + 1))
                    pool.wait_ge(ev(ph + ".step_done"), at(ph + ".step_done", H8 * h + H8))
                    pool.sem_inc(ev("pool_turns"), 1)
                    for k in range(H8):
                        s = par * H8 + k
                        nc.gpsimd.indirect_dma_start(
                            out=ring[:, s, :], out_offset=None, in_=table,
                            in_offset=bass.IndirectOffsetOnAxis(ap=idx[:, par, k:k + 1], axis=0)).then_inc(gath[s], 16)
                halves(pool, halves_of[ph], half)

        @block.scalar
        def _(act):
            def norm_parts(name, t):
                act.wait_ge(ev(name + ".centred"), at(name + ".centred", 1))
                act.activation(scratch, t, ACT.Square).then_inc(ev(name + ".squared"), 1)
                act.wait_ge(ev(name + ".var"), at(name + ".var", 1))
                act.activation(st[:, 2, :], st[:, 1, :], ACT.Sqrt, bias=eps_col[:, :], scale=1.0 / D).then_inc(ev(name + ".root"), 1)

            def gather_indices(ph, tab):
                def half(h, i, par):
                    act.wait_ge(ev(ph + ".step_done"), at(ph + ".step_done", H8 * h + H8))
                    act.activation(idx[:, par, :], tab[:, bass.ds(H8 * h, H8)], ACT.Copy).then_inc(ev(ph + ".idx_made"), 1)
                return half

            def fixed_block(name, n, par):
                act.wait_ge(ev(name + ".hT_done"), at(name + ".hT_done", n - 1))
                act.activation(h_fix[par], H[:, bass.ds(n, 1), :].rearrange("p a f -> p (a f)"), ACT.Copy).then_inc(ev(name + ".h_fixed"), 1)
                act.wait_ge(ev(name + ".hT_done"), at(name + ".hT_done", n + 1))
                act.wait_ge(ev(name + ".proj_done"), at(name + ".proj_done", n - 1))
                act.activation(hT_fix[par], bank[7 * par][:, 0:P], ACT.Copy).then_inc(ev(name + ".hT_made"), 1)

            prime(act, "act")
            norm_parts("ln0", H[:, :, :])
            act.wait_ge(ev("list0.made"), at("list0.made", 1))
            halves(act, HALVES_A, gather_indices("sum", srcA))
            norm_parts("ln1", H[:, :, :])
            act.wait_ge(ev("list1.made"), at("list1.made", 1))
            for l, ph in enumerate(("rel0", "rel1")):
                prep = gather_indices(ph, srcB)

                def relus(h, par):
                    for k in range(H8):
                        s = par * H8 + k
                        act.wait_ge(ev(ph + ".msg_sum"), at(ph + ".msg_sum", H8 * h + k + 1))
                        act.activation(ring_xe[:, s, :], ring_xe[:, s, :], ACT.Relu).then_inc(ev(ph + ".msg_made"), 1)

                prep(0, 0, 0)
                with act.Fori(0, HALVES_B // 2) as i:
                    prep(2 * i + 1, i, 1)
                    relus(2 * i, 0)
                    prep(2 * i + 2, i + 1, 0)
                    relus(2 * i + 1, 1)
                relus(HALVES_B - 1, 0)
                act.wait_ge(ev(ph + ".added"), at(ph + ".added", 8 + SB))

                def node_block(n, i, par):
                    act.wait_ge(ev(ph + ".proj_done"), at(ph + ".proj_done", n - 1))
                    act.activation(acb[par].rearrange("p (r b n) -> p b r n", r=R, b=P // WB),
                                   acc1[:, bass.ds(R * P * n, R * P)].rearrange("p (b r n) -> p b r n", b=P // WB, r=R),
                                   ACT.Copy).then_inc(ev(ph + ".sums_fixed"), 1)
                    fixed_block(ph, n, par)
                halves(act, NB, node_block)
                act.wait_ge(ev(ph + ".centred"), at(ph + ".centred", 1))
                act.activation(scratch, Y[:, :, :], ACT.Square).then_inc(ev(ph + ".squared"), 1)
                act.wait_ge(ev(ph + ".var"), at(ph + ".var", 1))
                act.activation(small[:, 128:256], small[:, 0:128], ACT.Sqrt, bias=eps_col[:, :], scale=1.0 / N).then_inc(ev(ph + ".root"), 1)
            norm_parts("ln2", H[:, :, :])
            act.wait_ge(ev("deg.made"), at("deg.made", 1))
            act.activation(st[:, 2, :], st[:, 3, :], ACT.Sqrt).then_inc(ev("deg.root"), 1)
            act.wait_ge(ev("ln2.ready"), at("ln2.ready", 1))
            halves(act, NB, lambda n, i, par: fixed_block("gcn", n, par))
            halves(act, HALVES_A, gather_indices("gcn", srcA))
            norm_parts("gcn_ln", Y[:, :, :])
            norm_parts("ln3", H[:, :, :])
            for l, ph in enumerate(("att0", "att1")):
                nh = (4, 1)[l]
                scale = float(D // nh) ** -0.5
                q8 = H8 * nh
                act.wait_ge(ev(("ln3.ready", "att0.over")[l]), at(("ln3.ready", "att0.over")[l], 1))
                halves(act, NB, lambda n, i, par: fixed_block(ph, n, par))
                prep = gather_indices(ph, srcA)
                dif, ab = fl[:, 0:q8], fl[:, 256:256 + 2 * q8]
                locs = fl[:, 192:192 + q8]
                keyT = fl[0:q8, 384:384 + P]
                ch, aw, rw = D // nh, D + nh, D + 2 * nh + 1
                rhs = rhs3[:, 0:H8 * rw].rearrange("p (s f) -> p s f", s=H8)

                def copy_hotT(h, j):
                    act.wait_ge(ev(ph + ".hotT"), at(ph + ".hotT", 2 * h + j + 1))
                    act.wait_ge(ev(ph + ".q_done"), at(ph + ".q_done", 2 * h))
                    act.activation(oh_t[:, 4 * j:4 * j + 4, :], bank[j][:, :].rearrange("p (s f) -> p s f", s=4), ACT.Copy)\
                       .then_inc(ev(ph + ".hotT_copied"), 1)

                def factors(h):
                    act.wait_ge(ev(ph + ".resc"), at(ph + ".resc", h + 1))
                    act.activation(ab, ab, ACT.Exp, scale=scale).then_inc(ev(ph + ".resc_exped"), 1)
                    act.wait_ge(ev(ph + ".resc_exped"), at(ph + ".resc_exped", h + 1))
                    act.wait_ge(ev(ph + ".added"), at(ph + ".added", h))

                def new_part(k):
                    for a in range(nh):
                        ins = act.activation(part[:, k * aw + a * (ch + 1):k * aw + (a + 1) * (ch + 1)],
                                             bank[5 + k // 3][:, (k % 3) * rw + a * (ch + 1):(k % 3) * rw + (a + 1) * (ch + 1)],
                                             ACT.Copy, scale=ab[:, q8 + k * nh + a:q8 + k * nh + a + 1])
                    ins.then_inc(ev(ph + ".parted"), 1)

                def half(h, i, par):
                    first = isinstance(h, int) and h == 0
                    if par == 1:
                        prep(h + 1, i + 1, 0)
                    else:
                        prep(h + 1, i, 1)
                    act.activation(locs.rearrange("p (s a) -> p s a", a=nh),
                                   locA[:, bass.ds(H8 * h, H8)].rearrange("p (s a) -> p s a", a=1).broadcast_to([P, H8, nh]), ACT.Copy)\
                       .then_inc(ev(ph + ".locs_made"), 1)
                    act.wait_ge(ev(ph + ".logT"), at(ph + ".logT", h + 1))
                    act.activation(keyT, bank[4][0:q8, P:2 * P], ACT.Copy).then_inc(ev(ph + ".keyT_made"), 1)
                    if first:
                        copy_hotT(h + 1, 0)
                        copy_hotT(h + 1, 1)
                    else:
                        factors(h - 1)
                        for k in range(H8):
                            if k in (2, 5):
                                copy_hotT(h + 1, k // 3)
                            new_part(k)
                    act.wait_ge(ev(ph + ".diff"), at(ph + ".diff", h + 1))
                    act.activation(rhs[:, :, 0:aw].rearrange("p s (a c) -> p s a c", a=nh)[:, :, :, ch:ch + 1].rearrange("p s a c -> p s (a c)"),
                                   dif.rearrange("p (s a) -> p s a", a=nh), ACT.Exp, scale=scale).then_inc(ev(ph + ".exped"), 1)
                    act.activation(rhs[:, :, aw:aw + nh], bank[4][:, 2 * P + q8:2 * P + 2 * q8].rearrange("p (s a) -> p s a", a=nh), ACT.Copy)\
                       .then_inc(ev(ph + ".marked"), 1)
                    act.activation(rhs[:, :, aw + nh:rw], bank[4][:, 2 * P + 2 * q8:2 * P + 3 * q8].rearrange("p (s a) -> p s a", a=nh)[:, :, 0:1], ACT.Copy)\
                       .then_inc(ev(ph + ".marked"), 1)
                    if nh == 1:
                        act.wait_ge(ev(ph + ".exped"), at(ph + ".exped", h + 1))
                        for k in range(H8):
                            act.activation(rhs[:, k, 0:D], ring_kv[:, par * H8 + k, D:2 * D], ACT.Copy, scale=rhs[:, k, D:D + 1])\
                               .then_inc(ev(ph + ".rhs_made"), 1)

                prep(0, 0, 0)
                copy_hotT(0, 0)
                copy_hotT(0, 1)
                skewed(act, half)
                factors(HALVES_A - 1)
                for k in range(H8):
                    new_part(k)

        def open_ring(pe, ph):
            pe.wait_ge(ev(ph + ".start"), at(ph + ".start", 1))
            pe.sem_inc(ev(ph + ".step_done"), 16)

        def plain_products(pe, ph):
            open_ring(pe, ph)

            def half(h, i, par):
                for k in range(H8):
                    s = par * H8 + k
                    step = H8 * h + k
                    pe.wait_ge(gath[s], gathers_seen(ph, i + 1, par))
                    pe.wait_ge(ev(ph + ".hot_made"), at(ph + ".hot_made", step + 1))
                    pe.wait_ge(ev(ph + ".added"), at(ph + ".added", step + 1))
                    last = nc.tensor.matmul(bank[k][:, 0:D], ring_oh[:, s, :], ring_g[:, s, :], start=True, stop=True)
                    if ph == "sum":
                        last = nc.tensor.matmul(bank[k][:, D:D + R], ring_oh[:, s, :],
                                                rel_hot[:, bass.ds(step, 1), :].rearrange("p a r -> p (a r)"), start=True, stop=True)
                    last.then_inc(ev(ph + ".step_done"), 1)
            halves(pe, HALVES_A, half)

        def node_sum(pe, t, name):
            nc.tensor.matmul(bank[5][:, 0:D], ones[:, :], t[:, 0, :], start=True, stop=False)
            with pe.Fori(1, NB - 1) as i:
                nc.tensor.matmul(bank[5][:, 0:D], ones[:, :], t[:, bass.ds(i, 1), :].rearrange("p a f -> p (a f)"), start=False, stop=False)
            nc.tensor.matmul(bank[5][:, 0:D], ones_rest[:, :], t[:, NB - 1, :], start=False, stop=True).then_inc(ev(name), 1)

        @block.tensor
        def _(pe):
            prime(pe, "pe")
            for n, cols in enumerate((SA, SB)):
                nm = f"list{n}"
                pe.wait_ge(ev(nm + ".counts"), at(nm + ".counts", 1))
                nc.tensor.matmul(bank[0][:, 0:NCH], tri, tc[:, 2, :], start=True, stop=False)
                nc.tensor.matmul(bank[0][:, 0:NCH], ones[:, :], tc[:, 3, :], start=False, stop=True).then_inc(ev(nm + ".starts"), 1)
                pe.wait_ge(ev(nm + ".hits"), at(nm + ".hits", 1))
                hw = cols // 2
                for hf in range(2):
                    if hf:
                        pe.wait_ge(ev(nm + ".read"), at(nm + ".read", hf))
                    for q in range(5):
                        for c in range(NCH):
                            lhs = (spread[:, 0, c, :], ones[:, :],
                                   (row_f[:, 0, c, :], row_key[:, c, :])[n],
                                   row_f[:, 1, c, :],
                                   (row_f[:, 2, c, :], spread[:, 1, c, :])[n])[q]
                            last = nc.tensor.matmul(bank[1 + q][:, 0:hw], lhs, hit[:, c, hf * hw:(hf + 1) * hw],
                                                    start=(c == 0), stop=(c == NCH - 1))
                    last.then_inc(ev(nm + ".picked"), 1)
                if n == 0:
                    plain_products(pe, "sum")

            for l, ph in enumerate(("rel0", "rel1")):
                open_ring(pe, ph)

                def half(h, i, par):
                    for k in range(H8):
                        s = par * H8 + k
                        step = H8 * h + k
                        pe.wait_ge(ev(ph + ".hot_made"), at(ph + ".hot_made", step + 1))
                        pe.wait_ge(ev(ph + ".msg_made"), at(ph + ".msg_made", step + 1))
                        pe.wait_ge(ev(ph + ".added"), at(ph + ".added", step + 1))
                        nc.tensor.matmul(bank[k][:, 0:SEG], ring_xe[:, s, :], ring_oh2[:, s, :], start=True, stop=True)\
                            .then_inc(ev(ph + ".step_done"), 1)
                halves(pe, HALVES_B, half)
                pe.wait_ge(ev(ph + ".w"), at(ph + ".w", 16))
                pe.wait_ge(ev(ph + ".w_root"), at(ph + ".w_root", 16))
                pe.wait_ge(ev(ph + ".added"), at(ph + ".added", 8 + SB))

                def node_block(n, i, par):
                    pe.wait_ge(ev(ph + ".h_fixed"), at(ph + ".h_fixed", n + 1))
                    pe.wait_ge(ev(ph + ".hT_made"), at(ph + ".hT_made", n - 1))
                    nc.tensor.transpose(bank[7 * par][:, 0:P], h_fix[par], ident[:, :]).then_inc(ev(ph + ".hT_done"), 1)
                    pe.wait_ge(ev(ph + ".sums_fixed"), at(ph + ".sums_fixed", n + 1))
                    pe.wait_ge(ev(ph + ".proj_read"), at(ph + ".proj_read", n - 1))
                    for r in range(R):
                        nc.tensor.matmul(bank[1 + 3 * par + r // 4][:, (r % 4) * D:(r % 4 + 1) * D], acb[par][:, r * P:(r + 1) * P], wrel[:, r, :],
                                         start=True, stop=True)
                    pe.wait_ge(ev(ph + ".hT_made"), at(ph + ".hT_made", n + 1))
                    nc.tensor.matmul(bank[3 + 3 * par][:, 0:D], hT_fix[par], wrel[:, R, :], start=True, stop=True).then_inc(ev(ph + ".proj_done"), 1)
                halves(pe, NB, node_block)
                pe.wait_ge(ev(ph + ".proj_read"), at(ph + ".proj_read", NB))
                node_sum(pe, Y[:, :, :], ph + ".mean_sum")
                pe.wait_ge(ev(ph + ".squared"), at(ph + ".squared", 1))
                node_sum(pe, scratch, ph + ".var_sum")

            def project(ph, weights, width, loads):
                for name in loads:
                    pe.wait_ge(ev(name), at(name, 16))

                def node_block(n, i, par):
                    pe.wait_ge(ev(ph + ".h_fixed"), at(ph + ".h_fixed", n + 1))
                    pe.wait_ge(ev(ph + ".hT_made"), at(ph + ".hT_made", n - 1))
                    nc.tensor.transpose(bank[7 * par][:, 0:P], h_fix[par], ident[:, :]).then_inc(ev(ph + ".hT_done"), 1)
                    pe.wait_ge(ev(ph + ".proj_read"), at(ph + ".proj_read", n - 1))
                    pe.wait_ge(ev(ph + ".hT_made"), at(ph + ".hT_made", n + 1))
                    nc.tensor.matmul(bank[1 + 3 * par][:, 0:width], hT_fix[par], weights, start=True, stop=True).then_inc(ev(ph + ".proj_done"), 1)
                halves(pe, NB, node_block)

            project("gcn", wrel[:, 0, :], D, ["gcn.w"])
            plain_products(pe, "gcn")
            for l, ph in enumerate(("att0", "att1")):
                nh = (4, 1)[l]
                q8 = H8 * nh
                rw = D + 2 * nh + 1
                rhs = rhs3[:, 0:H8 * rw].rearrange("p (s f) -> p s f", s=H8)
                project(ph, wqkvs, 4 * D, [f"{ph}.w{j}" for j in range(4)])
                open_ring(pe, ph)
                logits, locs = fl[:, 128:128 + q8], fl[:, 192:192 + q8]
                tri3 = fl[0:q8, 648:648 + 3 * P].rearrange("p (a f) -> p a f", a=3)

                def transpose_hots(h, par):
                    pe.wait_ge(ev(ph + ".hot_made"), at(ph + ".hot_made", H8 * h + H8))
                    for j in range(2):
                        for k in range(4):
                            last = nc.tensor.transpose(bank[j][:, k * P:(k + 1) * P], ring_oh[:, par * H8 + 4 * j + k, :], ident[:, :])
                        last.then_inc(ev(ph + ".hotT"), 1)

                def pick_queries(h):
                    blks = registers(pe, blkA, h, NB)
                    for j in range(2):
                        pe.wait_ge(ev(ph + ".hotT_copied"), at(ph + ".hotT_copied", 2 * h + j + 1))
                        for k in range(4):
                            last = nc.tensor.matmul(bank[2 + j][:, k * P:(k + 1) * P], oh_t[:, 4 * j + k, :], qt[:, bass.ds(blks[4 * j + k] * D, D)],
                                                    start=True, stop=True)
                        last.then_inc(ev(ph + ".q_done"), 1)

                def half(h, i, par):
                    pe.wait_ge(ev(ph + ".logits"), at(ph + ".logits", h + 1))
                    nc.tensor.transpose(bank[4][0:q8, 0:P], logits, ident[:, :])
                    pe.wait_ge(ev(ph + ".locs_made"), at(ph + ".locs_made", h + 1))
                    nc.tensor.transpose(bank[4][0:q8, P:2 * P], locs, ident[:, :]).then_inc(ev(ph + ".logT"), 1)
                    transpose_hots(h + 1, 1 - par)
                    pe.wait_ge(ev(ph + ".max_made"), at(ph + ".max_made", h + 1))
                    for a in range(3):
                        last = nc.tensor.matmul(bank[4][:, 2 * P + a * q8:2 * P + (a + 1) * q8], tri3[:, a, :], ident[0:q8, 0:q8], start=True, stop=True)
                    last.then_inc(ev(ph + ".maxT"), 1)
                    pick_queries(h + 1)
                    pe.wait_ge(ev(ph + ".marked"), at(ph + ".marked", 2 * h + 2))
                    pe.wait_ge(ev(ph + ".exped"), at(ph + ".exped", h + 1))
                    pe.wait_ge(ev(ph + ".rhs_made"), at(ph + ".rhs_made", h + 1) if nh > 1 else at(ph + ".rhs_made", H8 * h + H8))
                    pe.wait_ge(ev(ph + ".added"), at(ph + ".added", h))
                    for k in range(H8):
                        nc.tensor.matmul(bank[5 + k // 3][:, (k % 3) * rw:(k % 3 + 1) * rw], ring_oh[:, par * H8 + k, :], rhs[:, k, :], start=True, stop=True)\
                            .then_inc(ev(ph + ".step_done"), 1)

                transpose_hots(0, 0)
                pick_queries(0)
                skewed(pe, half)

        @block.vector
        def _(dve):
            v = nc.vector
            own, dve_done = Count(), ev("dve_done")
            prime(dve, "dve")
            v.memset(row_i[:, :, NCH - 1, :], 0).then_inc(ev("rows.zeroed"), 1)
            v.memset(X[:, NB - 1, :], 0.0).then_inc(ev("x.zeroed"), 1)
            v.memset(ones[:, :], 1.0).then_inc(dve_done, own.up())
            v.memset(eps_col[:, :], EPS).then_inc(dve_done, own.up())
            v.memset(arena[:, 0:NB * A0], 0.0).then_inc(dve_done, own.up())
            v.memset(locA[:, SA:SA + H8], FAR).then_inc(dve_done, own.up())
            v.memset(srcA[:, SA:SA + H8], 0).then_inc(dve_done, own.up())
            v.memset(blkA[:, SA:SA + H8], 0).then_inc(dve_done, own.up())
            dve.wait_ge(ev("iotas"), at("iotas", 4))
            v.tensor_scalar(ident[:, :], iota[:, 0:P], iota_p[:, :], None, ALU.is_equal).then_inc(dve_done, own.up())
            v.tensor_scalar(tri, iota[:, 0:P], iota_p[:, :], None, ALU.is_gt).then_inc(dve_done, own.up())
            dve.wait_ge(dve_done, own.count())
            v.tensor_scalar(tmp_s[:, 0, 0:P], ones[:, :], iota_p[:, :], None, ALU.mult).then_inc(dve_done, own.up())
            dve.wait_ge(dve_done, own.count())
            v.tensor_scalar(ones_rest[:, :], tmp_s[:, 0, 0:P], float(NREST), None, ALU.is_lt).then_inc(dve_done, own.up())
            for k in range(6):
                dve.wait_ge(ev(f"rows.in{k}"), at(f"rows.in{k}", 16))
            v.tensor_copy(row_f[:, :, :, :], row_i[:, :, :, :]).then_inc(dve_done, own.up())
            dve.wait_ge(dve_done, own.count())
            v.scalar_tensor_tensor(row_key, row_f[:, 2, :, :], float(KEYSTEP), row_f[:, 0, :, :], ALU.mult, ALU.add).then_inc(dve_done, own.up())
            for c in range(NCH):
                v.tensor_scalar(spread[:, 1, c, :], ones[:, :], tile_no[:, c:c + 1], None, ALU.mult).then_inc(dve_done, own.up())

            def step_list(n):
                nm = f"list{n}"
                shift, nb, cols, width = ((7, NB, SA, WA), (5, NBB, SB, WB))[n]
                for a, lane in ((0, 0), (1, P - 1)):
                    v.tensor_scalar(tci[:, a, :], row_i[:, 0, :, lane], shift, None, ALU.arith_shift_right).then_inc(dve_done, own.up())
                dve.wait_ge(dve_done, own.count())
                v.tensor_copy(tc[:, 0:2, :], tci[:, :, :]).then_inc(dve_done, own.up())
                v.tensor_scalar(tc[:, 5, :], tile_no[:, :], float(NT), None, ALU.is_lt).then_inc(dve_done, own.up())
                v.memset(tc[:, 3, 0:1], 0.0).then_inc(dve_done, own.up())
                dve.wait_ge(dve_done, own.count())
                v.tensor_scalar(tc[:, 0:2, :], tc[:, 0:2, :], float(nb - 1), None, ALU.min).then_inc(dve_done, own.up())
                dve.wait_ge(dve_done, own.count())
                v.tensor_tensor(tc[:, 4, :], tc[:, 1, :], tc[:, 0, :], ALU.subtract).then_inc(dve_done, own.up())
                dve.wait_ge(dve_done, own.count())
                v.scalar_tensor_tensor(tc[:, 2, :], tc[:, 4, :], 1.0, tc[:, 5, :], ALU.add, ALU.mult).then_inc(dve_done, own.up())
                for c in range(1, NCH):
                    dve.wait_ge(dve_done, own.count())
                    v.tensor_tensor(tc[:, 3, c:c + 1], tc[:, 3, c - 1:c], tc[:, 2, c - 1:c], ALU.add).then_inc(dve_done, own.up())
                dve.wait_ge(dve_done, own.count())
                dve.sem_inc(ev(nm + ".counts"), 1)
                dve.wait_ge(ev(nm + ".starts"), at(nm + ".starts", 1))
                v.tensor_copy(tc[:, 6, :], bank[0][:, 0:NCH]).then_inc(dve_done, own.up())
                dve.wait_ge(dve_done, own.count())
                v.tensor_tensor(tc[:, 7, :], tc[:, 6, :], tc[:, 2, :], ALU.add).then_inc(dve_done, own.up())
                v.tensor_tensor(tc[:, 4, :], tc[:, 0, :], tc[:, 6, :], ALU.subtract).then_inc(dve_done, own.up())
                dve.wait_ge(dve_done, own.count())
                for c in range(NCH):
                    v.tensor_scalar(hit[:, c, 0:cols], iota[:, 0:cols], tc[:, 6, c:c + 1], None, ALU.is_ge).then_inc(dve_done, own.up())
                    v.tensor_scalar(spread[:, 0, c, :], ones[:, :], tc[:, 4, c:c + 1], None, ALU.mult).then_inc(dve_done, own.up())
                dve.wait_ge(dve_done, own.count())
                for c in range(NCH):
                    v.scalar_tensor_tensor(hit[:, c, 0:cols], iota[:, 0:cols], tc[:, 7, c:c + 1], hit[:, c, 0:cols], ALU.is_lt, ALU.mult).then_inc(dve_done, own.up())
                dve.wait_ge(dve_done, own.count())
                dve.sem_inc(ev(nm + ".hits"), 1)
                hw = cols // 2
                loc, srct, blk = ((locA, srcA, blkA), (locB, srcB, blkB))[n]
                for hf in range(2):
                    dve.wait_ge(ev(nm + ".picked"), at(nm + ".picked", hf + 1))
                    w = slice(hf * hw, (hf + 1) * hw)
                    a, b, c = tmp_s[:, 0, 0:hw], tmp_s[:, 1, 0:hw], tmp_s[:, 2, 0:hw]
                    v.tensor_tensor(a, bank[2][:, 0:hw], iota[:, w], ALU.mult).then_inc(dve_done, own.up())
                    v.tensor_scalar(c, bank[2][:, 0:hw], -FAR, FAR, ALU.mult, ALU.add).then_inc(dve_done, own.up())
                    dve.wait_ge(dve_done, own.count())
                    v.tensor_tensor(b, bank[1][:, 0:hw], a, ALU.add).then_inc(dve_done, own.up())
                    v.tensor_tensor(c, bank[3][:, 0:hw], c, ALU.add).then_inc(dve_done, own.up())
                    v.tensor_copy(srct[:, w], bank[4][:, 0:hw]).then_inc(dve_done, own.up())
                    dve.wait_ge(dve_done, own.count())
                    v.tensor_copy(blk[:, w], b).then_inc(dve_done, own.up())
                    v.scalar_tensor_tensor(loc[:, w], b, -float(width), c, ALU.mult, ALU.add).then_inc(dve_done, own.up())
                    if n == 0:
                        v.tensor_tensor(rel_hot[:, w, :], bank[5][:, 0:hw].rearrange("p (s a) -> p s a", a=1).broadcast_to([P, hw, R]),
                                           iota[:, 0:R].rearrange("p (a r) -> p a r", a=1).broadcast_to([P, hw, R]), ALU.is_equal).then_inc(dve_done, own.up())
                    else:
                        v.tensor_copy(tileB[:, w], bank[5][:, 0:hw]).then_inc(dve_done, own.up())
                    dve.wait_ge(dve_done, own.count())
                    dve.sem_inc(ev(nm + ".read"), 1)
                dve.sem_inc(ev(nm + ".made"), 1)

            def normalise(name, t, src_t):
                v.tensor_reduce(st[:, 0, :], src_t, AX.X, ALU.add).then_inc(dve_done, own.up())
                dve.wait_ge(dve_done, own.count())
                v.tensor_scalar(st[:, 0, :], st[:, 0, :], 1.0 / D, None, ALU.mult).then_inc(dve_done, own.up())
                dve.wait_ge(dve_done, own.count())
                v.tensor_tensor(t, src_t, per_node(st[:, 0, :]), ALU.subtract).then_inc(ev(name + ".centred"), 1)
                dve.wait_ge(ev(name + ".squared"), at(name + ".squared", 1))
                v.tensor_reduce(st[:, 1, :], scratch, AX.X, ALU.add).then_inc(ev(name + ".var"), 1)
                dve.wait_ge(ev(name + ".root"), at(name + ".root", 1))
                v.reciprocal(st[:, 3, :], st[:, 2, :]).then_inc(dve_done, own.up())
                dve.wait_ge(dve_done, own.count())
                v.tensor_tensor(t, t, per_node(st[:, 3, :]), ALU.mult).then_inc(dve_done, own.up())
                dve.wait_ge(dve_done, own.count())

            def per_node(cols):
                return cols.rearrange("p (b a) -> p b a", a=1).broadcast_to([P, NB, D])

            def per_feature(row):
                return row.rearrange("p (a f) -> p a f", a=1).broadcast_to([P, NB, D])

            def add_up(ph, acc, blks, width, h, k):
                step = H8 * h + k
                dve.wait_ge(ev(ph + ".step_done"), at(ph + ".step_done", 16 + step + 1))
                dve.wait_ge(ev(ph + ".added"), at(ph + ".added", 8 + step))
                a = acc[:, bass.ds(blks[k] * width, width)]
                v.tensor_tensor(a, bank[k][:, 0:width], a, ALU.add).then_inc(ev(ph + ".added"), 1)

            def begin(ph):
                dve.wait_ge(dve_done, own.count())
                dve.sem_inc(ev(ph + ".start"), 1)

            def hot(ph, h, par, k):
                step = H8 * h + k
                dve.wait_ge(ev(ph + ".step_done"), at(ph + ".step_done", step + 1))
                v.tensor_scalar(ring_oh[:, par * H8 + k, :], iota[:, 0:P], locA[:, bass.ds(step, 1)], None, ALU.is_equal)\
                    .then_inc(ev(ph + ".hot_made"), 1)

            def woven(ph, acc, tab, top, width, produce):
                begin(ph)
                dve.sem_inc(ev(ph + ".added"), 8)
                for k in range(H8):
                    produce(0, 0, 0, k)
                with dve.Fori(0, halves_of[ph] // 2) as i:
                    for h, r, par in ((2 * i + 1, i, 1), (2 * i + 2, i + 1, 0)):
                        blks = registers(dve, tab, h - 1, top)
                        for k in range(H8):
                            add_up(ph, acc, blks, width, h - 1, k)
                            produce(h, r, par, k)
                last = halves_of[ph] - 1
                blks = registers(dve, tab, last, top)
                for k in range(H8):
                    add_up(ph, acc, blks, width, last, k)
                dve.wait_ge(ev(ph + ".added"), at(ph + ".added", 8 + H8 * halves_of[ph]))

            def plain_phase(ph, acc, width):
                woven(ph, acc, blkA, NB, width, lambda h, i, par, k: hot(ph, h, par, k))

            step_list(0)
            for k in range(2):
                dve.wait_ge(ev(f"x.in{k}"), at(f"x.in{k}", 16))
            normalise("ln0", H[:, :, :], X[:, :, :])
            v.tensor_scalar(H[:, :, :], H[:, :, :], 0.0, None, ALU.max).then_inc(ev("ln0.ready"), 1)
            plain_phase("sum", arena, A0)
            v.tensor_tensor(X[:, :, :], X[:, :, :], acc0[:, :, 0:D], ALU.add).then_inc(dve_done, own.up())
            v.tensor_reduce(dis[:, :], acc0[:, :, D:D + R], AX.X, ALU.add).then_inc(dve_done, own.up())
            v.tensor_scalar(inv_cnt[:, :, :], acc0[:, :, D:D + R], 1.0, None, ALU.max).then_inc(dve_done, own.up())
            dve.wait_ge(dve_done, own.count())
            v.reciprocal(inv_cnt[:, :, :], inv_cnt[:, :, :]).then_inc(dve_done, own.up())
            step_list(1)

            normalise("ln1", H[:, :, :], X[:, :, :])
            v.tensor_scalar(H[:, :, :], H[:, :, :], 0.0, None, ALU.max).then_inc(ev("ln1.ready"), 1)
            for l, ph in enumerate(("rel0", "rel1")):
                v.memset(acc1, 0.0).then_inc(dve_done, own.up())

                def produce(h, i, par, k):
                    s = par * H8 + k
                    step = H8 * h + k
                    dve.wait_ge(ev(ph + ".step_done"), at(ph + ".step_done", step + 1))
                    v.tensor_scalar(ring_oh2[:, s, :], iota_key[:, :, :].rearrange("p r n -> p (r n)"), locB[:, bass.ds(step, 1)], None, ALU.is_equal)\
                        .then_inc(ev(ph + ".hot_made"), 1)
                    dve.wait_ge(gath[s], gathers_seen(ph, i + 1, par))
                    dve.wait_ge(xe_in[s], edge_rows_seen(ph, i + 1, par))
                    v.tensor_tensor(ring_xe[:, s, :], ring_g[:, s, :], ring_xe[:, s, :], ALU.add).then_inc(ev(ph + ".msg_sum"), 1)
                woven(ph, acc1, blkB, NBB, SEG, produce)
                for j in range(3):
                    dve.wait_ge(ev(f"{ph}.row{j}"), at(f"{ph}.row{j}", 16))
                start = own.count()

                def node_block(n, i, par):
                    own.at(start + 4 * n)
                    dve.wait_ge(ev(ph + ".proj_done"), at(ph + ".proj_done", n + 1))
                    for j in range(2):
                        v.tensor_tensor(relsum[:, 4 * j:4 * j + 4, :], bank[1 + 3 * par + j][:, :].rearrange("p (r f) -> p r f", r=4),
                                        inv_cnt[:, bass.ds(n, 1), 4 * j:4 * j + 4].rearrange("p a (r b) -> p (a r) b", b=1).broadcast_to([P, 4, D]), ALU.mult)\
                            .then_inc(dve_done, own.up())
                    dve.wait_ge(dve_done, own.count())
                    v.tensor_reduce(relred, relsum.rearrange("p r f -> p f r"), AX.X, ALU.add).then_inc(dve_done, own.up())
                    dve.wait_ge(dve_done, own.count())
                    v.tensor_tensor(relred, relred, bank[3 + 3 * par][:, 0:D], ALU.add).then_inc(dve_done, own.up())
                    dve.wait_ge(dve_done, own.count())
                    v.tensor_tensor(Y[:, bass.ds(n, 1), :].rearrange("p a f -> p (a f)"), relred, rows[:, 0, :], ALU.add).then_inc(ev(ph + ".proj_read"), 1)
                halves(dve, NB, node_block)
                own.at(start + 4 * NB)
                dve.wait_ge(ev(ph + ".mean_sum"), at(ph + ".mean_sum", 1))
                v.tensor_scalar(small[:, 256:384], bank[5][:, 0:D], 1.0 / N, None, ALU.mult).then_inc(dve_done, own.up())
                dve.wait_ge(dve_done, own.count())
                v.tensor_tensor(Y[:, :, :], Y[:, :, :], per_feature(small[:, 256:384]), ALU.subtract).then_inc(ev(ph + ".centred"), 1)
                dve.wait_ge(ev(ph + ".var_sum"), at(ph + ".var_sum", 1))
                v.tensor_copy(small[:, 0:128], bank[5][:, 0:D]).then_inc(ev(ph + ".var"), 1)
                dve.wait_ge(ev(ph + ".root"), at(ph + ".root", 1))
                v.reciprocal(small[:, 384:512], small[:, 128:256]).then_inc(dve_done, own.up())
                dve.wait_ge(dve_done, own.count())
                v.tensor_tensor(small[:, 384:512], small[:, 384:512], rows[:, 1, :], ALU.mult).then_inc(dve_done, own.up())
                dve.wait_ge(dve_done, own.count())
                v.tensor_tensor(Y[:, :, :], Y[:, :, :], per_feature(small[:, 384:512]), ALU.mult).then_inc(dve_done, own.up())
                dve.wait_ge(dve_done, own.count())
                v.tensor_tensor(Y[:, :, :], Y[:, :, :], per_feature(rows[:, 2, :]), ALU.add).then_inc(dve_done, own.up())
                dve.wait_ge(dve_done, own.count())
                if l == 0:
                    v.tensor_scalar(H[:, :, :], Y[:, :, :], 0.0, None, ALU.max).then_inc(ev("rel0.over"), 1)
                else:
                    v.tensor_tensor(X[:, :, :], X[:, :, :], Y[:, :, :], ALU.add).then_inc(ev("rel1.over"), 1)
            dve.wait_ge(ev("rel1.over"), at("rel1.over", 1))

            normalise("ln2", H[:, :, :], X[:, :, :])
            v.memset(acc2, 0.0).then_inc(dve_done, own.up())
            v.tensor_scalar(st[:, 1, :], dis[:, :], 1.0, None, ALU.add).then_inc(dve_done, own.up())
            v.tensor_scalar(H[:, :, :], H[:, :, :], 0.0, None, ALU.max).then_inc(ev("ln2.ready"), 1)
            dve.wait_ge(dve_done, own.count())
            v.tensor_copy(st[:, 3, :], st[:, 1, :]).then_inc(ev("deg.made"), 1)
            dve.wait_ge(ev("deg.root"), at("deg.root", 1))
            v.reciprocal(dis[:, :], st[:, 2, :]).then_inc(dve_done, own.up())
            dve.wait_ge(dve_done, own.count())

            def scaled_block(n, i, par):
                dve.wait_ge(ev("gcn.proj_done"), at("gcn.proj_done", n + 1))
                v.tensor_scalar(y2[:, bass.ds(n, 1), :].rearrange("p a f -> p (a f)"), bank[1 + 3 * par][:, 0:D], dis[:, bass.ds(n, 1)], None, ALU.mult)\
                    .then_inc(ev("gcn.proj_read"), 1)
            halves(dve, NB, scaled_block)
            dve.wait_ge(ev("gcn.proj_read"), at("gcn.proj_read", NB))
            dve.sem_inc(ev("gcn.table_made"), 1)
            plain_phase("gcn", arena, D)
            for j in range(3):
                dve.wait_ge(ev(f"gcn.row{j}"), at(f"gcn.row{j}", 16))
            v.tensor_tensor(Y[:, :, :], acc2, y2, ALU.add).then_inc(dve_done, own.up())
            dve.wait_ge(dve_done, own.count())
            v.tensor_tensor(Y[:, :, :], Y[:, :, :], per_node(dis[:, :]), ALU.mult).then_inc(dve_done, own.up())
            dve.wait_ge(dve_done, own.count())
            v.tensor_tensor(Y[:, :, :], Y[:, :, :], per_feature(rows[:, 0, :]), ALU.add).then_inc(dve_done, own.up())
            dve.wait_ge(dve_done, own.count())
            v.tensor_tensor(Y[:, :, :], Y[:, :, :], H[:, :, :], ALU.add).then_inc(dve_done, own.up())
            dve.wait_ge(dve_done, own.count())
            normalise("gcn_ln", Y[:, :, :], Y[:, :, :])
            v.tensor_tensor(Y[:, :, :], Y[:, :, :], per_feature(rows[:, 1, :]), ALU.mult).then_inc(dve_done, own.up())
            dve.wait_ge(dve_done, own.count())
            v.tensor_tensor(Y[:, :, :], Y[:, :, :], per_feature(rows[:, 2, :]), ALU.add).then_inc(dve_done, own.up())
            dve.wait_ge(dve_done, own.count())
            v.tensor_scalar(Y[:, :, :], Y[:, :, :], 0.0, None, ALU.max).then_inc(dve_done, own.up())
            dve.wait_ge(dve_done, own.count())
            v.tensor_tensor(X[:, :, :], X[:, :, :], Y[:, :, :], ALU.add).then_inc(ev("gcn.over"), 1)
            dve.wait_ge(ev("gcn.over"), at("gcn.over", 1))

            normalise("ln3", H[:, :, :], X[:, :, :])
            v.tensor_scalar(H[:, :, :], H[:, :, :], 0.0, None, ALU.max).then_inc(ev("ln3.ready"), 1)
            for l, ph in enumerate(("att0", "att1")):
                nh = (4, 1)[l]
                ch = D // nh
                q8 = H8 * nh
                aw = D + nh
                rw = aw + nh + 1
                rhs = rhs3[:, 0:H8 * rw].rearrange("p (s f) -> p s f", s=H8)
                acc = acc3[:, 0:NB * aw]
                opart = part[:, 0:H8 * aw].rearrange("p (s f) -> p s f", s=H8)
                dif, ex, ab = fl[:, 0:q8], fl[:, 64:64 + q8], fl[:, 256:256 + 2 * q8]
                logits, locs = fl[:, 128:128 + q8], fl[:, 192:192 + q8]
                pres, mnew = fl[:, 320:320 + H8], fl[:, 336:336 + q8]
                mold, mstep = fl[:, 1168:1168 + q8], fl[:, 1200:1200 + q8]
                keyT = fl[0:q8, 384:384 + P]
                reset = fl[0:q8, 512:512 + P + 1]
                tri3 = fl[0:q8, 648:648 + 3 * P].rearrange("p (a f) -> p a f", a=3)
                fwd = fl[0:q8, 1040:1040 + P]
                for j in range(4):
                    dve.wait_ge(ev(f"{ph}.b{j}"), at(f"{ph}.b{j}", 16))
                start = own.count()

                def biased_block(n, i, par):
                    own.at(start + 2 * n)
                    pb = bank[1 + 3 * par]
                    dve.wait_ge(ev(ph + ".proj_done"), at(ph + ".proj_done", n + 1))
                    v.tensor_tensor(qt[:, bass.ds(D * n, D)], pb[:, 0:D], bqkvs[:, 0:D], ALU.add).then_inc(dve_done, own.up())
                    v.tensor_tensor(kvt[:, bass.ds(n, 1), :].rearrange("p a f -> p (a f)"), pb[:, D:3 * D], bqkvs[:, D:3 * D], ALU.add)\
                        .then_inc(dve_done, own.up())
                    v.tensor_tensor(skip[:, bass.ds(n, 1), :].rearrange("p a f -> p (a f)"), pb[:, 3 * D:4 * D], bqkvs[:, 3 * D:4 * D], ALU.add)\
                        .then_inc(ev(ph + ".proj_read"), 1)
                halves(dve, NB, biased_block)
                own.at(start + 2 * NB)
                dve.wait_ge(dve_done, own.count())
                dve.wait_ge(ev(ph + ".proj_read"), at(ph + ".proj_read", NB))
                dve.sem_inc(ev(ph + ".table_made"), 1)
                v.memset(acc, 0.0).then_inc(dve_done, own.up())
                v.memset(mst[:, 0:NB * nh], -BIG).then_inc(dve_done, own.up())
                v.memset(reset[:, 0:1], -BIG).then_inc(dve_done, own.up())
                v.memset(reset[:, P:P + 1], -BIG).then_inc(dve_done, own.up())
                v.memset(tri3[:, 2, 0:1], 1.0).then_inc(dve_done, own.up())
                begin(ph)

                def make_logits(h, i, par):
                    for j in range(2):
                        dve.wait_ge(ev(ph + ".q_done"), at(ph + ".q_done", 2 * h + j + 1))
                        for k in range(4):
                            dve.wait_ge(gath[par * H8 + 4 * j + k], gathers_seen(ph, i + 1, par))
                        v.tensor_tensor(prod[:, 4 * j:4 * j + 4, :], bank[2 + j][:, :].rearrange("p (s f) -> p s f", s=4),
                                        ring_kv[:, par * H8 + 4 * j:par * H8 + 4 * j + 4, 0:D], ALU.mult).then_inc(dve_done, own.up())
                    dve.wait_ge(dve_done, own.count())
                    v.tensor_reduce(logits, prod.rearrange("p s (a c) -> p (s a) c", a=nh), AX.X, ALU.add).then_inc(ev(ph + ".logits"), 1)

                def run_maxima(h, n):
                    if n == 0:
                        dve.wait_ge(ev(ph + ".keyT_made"), at(ph + ".keyT_made", h + 1))
                        v.tensor_tensor(tri3[:, 2, 1:P], keyT[:, 1:P], keyT[:, 0:P - 1], ALU.not_equal).then_inc(dve_done, own.up())
                    else:
                        dve.wait_ge(dve_done, own.marked)
                    if n == 1:
                        v.tensor_scalar(reset[:, 1:P], tri3[:, 2, 1:P], -BIG, None, ALU.mult).then_inc(dve_done, own.up())
                    if n == 2:
                        v.tensor_tensor_scan(fwd, reset[:, 0:P], bank[4][0:q8, 0:P], -BIG, ALU.add, ALU.max).then_inc(dve_done, own.up())
                    if n == 3:
                        v.tensor_tensor_scan(tri3[:, 0, ::-1], reset[:, 1:P + 1][:, ::-1], fwd[:, ::-1], -BIG, ALU.add, ALU.max).then_inc(dve_done, own.up())
                    if n == 4:
                        v.tensor_tensor(tri3[:, 1, :], tri3[:, 0, :], tri3[:, 2, :], ALU.mult).then_inc(ev(ph + ".max_made"), 1)
                    own.marked = own.count()

                def subtract_maxima(h):
                    dve.wait_ge(ev(ph + ".maxT"), at(ph + ".maxT", h + 1))
                    v.tensor_tensor(dif, logits, bank[4][:, 2 * P:2 * P + q8], ALU.subtract).then_inc(ev(ph + ".diff"), 1)

                def weigh_values(h, par):
                    heads = rhs[:, :, 0:aw].rearrange("p s (a c) -> p s a c", a=nh)
                    dve.wait_ge(ev(ph + ".exped"), at(ph + ".exped", h + 1))
                    v.tensor_tensor(heads[:, :, :, 0:ch], ring_kv[:, par * H8:par * H8 + H8, D:2 * D].rearrange("p s (a c) -> p s a c", a=nh),
                                    heads[:, :, :, ch:ch + 1].broadcast_to([P, H8, nh, ch]), ALU.mult).then_inc(ev(ph + ".rhs_made"), 1)

                def merge_maxima(h, blks, between=lambda k: None):
                    dve.wait_ge(ev(ph + ".step_done"), at(ph + ".step_done", 16 + H8 * h + H8))
                    for j in range(3):
                        m = min(3, H8 - 3 * j)
                        v.tensor_scalar(pres[:, 3 * j:3 * j + m], bank[5 + j][:, 0:m * rw].rearrange("p (s f) -> p s f", s=m)[:, :, rw - 1],
                                        BIG, -BIG, ALU.mult, ALU.add).then_inc(dve_done, own.up())
                    dve.wait_ge(dve_done, own.count())
                    for j in range(3):
                        m = min(3, H8 - 3 * j)
                        v.tensor_tensor(mstep[:, 3 * j * nh:(3 * j + m) * nh].rearrange("p (s a) -> p s a", a=nh),
                                        bank[5 + j][:, 0:m * rw].rearrange("p (s f) -> p s f", s=m)[:, :, aw:aw + nh],
                                        pres[:, 3 * j:3 * j + m].rearrange("p (s a) -> p s a", a=1).broadcast_to([P, m, nh]), ALU.add)\
                            .then_inc(dve_done, own.up())
                    chain = own.count()
                    for k in range(H8):
                        state = mst[:, bass.ds(blks[k] * nh, nh)]
                        dve.wait_ge(dve_done, chain)
                        v.tensor_scalar(mold[:, k * nh:(k + 1) * nh], state, 1.0, None, ALU.mult).then_inc(dve_done, own.up())
                        v.tensor_tensor(state, state, mstep[:, k * nh:(k + 1) * nh], ALU.max).then_inc(dve_done, own.up())
                        chain = own.count()
                        between(k)
                    dve.wait_ge(dve_done, own.count())
                    v.tensor_tensor(mnew, mold, mstep, ALU.max).then_inc(dve_done, own.up())
                    dve.wait_ge(dve_done, own.count())
                    v.tensor_tensor(ab[:, 0:q8], mold, mnew, ALU.subtract).then_inc(dve_done, own.up())
                    v.tensor_tensor(ab[:, q8:2 * q8], mstep, mnew, ALU.subtract).then_inc(dve_done, own.up())
                    dve.wait_ge(dve_done, own.count())
                    dve.sem_inc(ev(ph + ".resc"), 1)

                def merge_sums(h, blks, between):
                    chain = own.count()
                    dve.wait_ge(ev(ph + ".resc_exped"), at(ph + ".resc_exped", h + 1))
                    for k in range(H8):
                        a = acc[:, bass.ds(blks[k] * aw, aw)]
                        dve.wait_ge(dve_done, chain)
                        if nh > 1:
                            a3 = a.rearrange("p (a c) -> p a c", a=nh)
                            v.tensor_tensor(a3, a3, ab[:, k * nh:(k + 1) * nh].rearrange("p (a b) -> p a b", b=1).broadcast_to([P, nh, ch + 1]), ALU.mult)\
                                .then_inc(dve_done, own.up())
                            chain = own.count()
                            between(k)
                            dve.wait_ge(ev(ph + ".parted"), at(ph + ".parted", H8 * h + k + 1))
                            dve.wait_ge(dve_done, chain)
                            v.tensor_tensor(a, a, opart[:, k, :], ALU.add).then_inc(dve_done, own.up())
                            chain = own.count()
                        else:
                            dve.wait_ge(ev(ph + ".parted"), at(ph + ".parted", H8 * h + k + 1))
                            v.scalar_tensor_tensor(a, a, ab[:, k:k + 1], opart[:, k, :], ALU.mult, ALU.add).then_inc(dve_done, own.up())
                            chain = own.count()
                            between(k)
                    dve.wait_ge(dve_done, chain)
                    dve.sem_inc(ev(ph + ".added"), 1)

                def half(h, i, par):
                    first = isinstance(h, int) and h == 0
                    own.at(start + (0 if first else FIRST + (h - 1) * PER))
                    make_logits(h, i, par)
                    if first:
                        for k in range(H8):
                            hot(ph, h + 1, 1 - par, k)
                        for n in range(5):
                            run_maxima(h, n)
                        subtract_maxima(h)
                    else:
                        blks = registers(dve, blkA, h - 1, NB)
                        merge_maxima(h - 1, blks, lambda k: hot(ph, h + 1, 1 - par, k))
                        run_maxima(h, 0)
                        run_maxima(h, 1)

                        def between(k):
                            if k < 3:
                                run_maxima(h, 2 + k)
                            if k == 5:
                                subtract_maxima(h)
                        merge_sums(h - 1, blks, between)
                    if nh > 1:
                        weigh_values(h, par)
                    assert own.k == (FIRST if first else PER), own.k

                start = own.count()
                FIRST = 2 + 4
                PER = FIRST + (6 + 2 * H8 + 3) + (2 * H8 if nh > 1 else H8)
                for k in range(H8):
                    hot(ph, 0, 0, k)
                skewed(dve, half)
                own.at(start + FIRST + (HALVES_A - 1) * PER)
                blks = registers(dve, blkA, HALVES_A - 1, NB)
                merge_maxima(HALVES_A - 1, blks)
                merge_sums(HALVES_A - 1, blks, lambda k: None)
                dve.wait_ge(dve_done, own.count())
                a4 = acc.rearrange("p (b a c) -> p b a c", b=NB, a=nh)
                den = small[:, 0:NB * nh].rearrange("p (b a) -> p b a", b=NB)
                v.tensor_scalar(den, a4[:, :, :, ch:ch + 1].rearrange("p b a c -> p b (a c)"), 1e-16, None, ALU.add).then_inc(dve_done, own.up())
                dve.wait_ge(dve_done, own.count())
                v.reciprocal(den, den).then_inc(dve_done, own.up())
                dve.wait_ge(dve_done, own.count())
                y4 = Y[:, :, :].rearrange("p b (a c) -> p b a c", a=nh)
                v.tensor_tensor(y4, a4[:, :, :, 0:ch], small[:, 0:NB * nh].rearrange("p (b a c) -> p b a c", b=NB, c=1).broadcast_to([P, NB, nh, ch]), ALU.mult).then_inc(dve_done, own.up())
                dve.wait_ge(dve_done, own.count())
                v.tensor_tensor(Y[:, :, :], Y[:, :, :], skip, ALU.add).then_inc(dve_done, own.up())
                dve.wait_ge(dve_done, own.count())
                if l == 0:
                    v.tensor_scalar(H[:, :, :], Y[:, :, :], 0.0, None, ALU.max).then_inc(ev("att0.over"), 1)
                else:
                    v.tensor_tensor(X[:, :, :], X[:, :, :], Y[:, :, :], ALU.add).then_inc(ev("att1.over"), 1)


_INS = ["x", "src", "dst", "edge_attr_128", "edge_type_8", "L1_gnn_weight", "L1_gnn_root", "L1_gnn_bias", "L1_gnn_bn_gamma",
        "L1_gnn_bn_beta", "L2_gnn_W", "L2_gnn_b", "L2_gnn_gamma", "L2_gnn_beta",
        "L3_gnn_w1_q", "L3_gnn_b1_q", "L3_gnn_w1_k", "L3_gnn_b1_k", "L3_gnn_w1_v", "L3_gnn_b1_v", "L3_gnn_w1_s", "L3_gnn_b1_s",
        "L3_gnn_w2_q", "L3_gnn_b2_q", "L3_gnn_w2_k", "L3_gnn_b2_k", "L3_gnn_w2_v", "L3_gnn_b2_v", "L3_gnn_w2_s", "L3_gnn_b2_s"]


def kernel(**inputs):
    import numpy as _np
    import concourse.bacc as _bacc
    from concourse import mybir as _mybir
    from concourse.bass_utils import run_bass_kernel_spmd as _run

    nc = _bacc.Bacc("TRN2", target_bir_lowering=False, num_devices=1)
    arrays, args = {}, []
    pads = {"src": 0, "dst": PAD_DST, "edge_type_8": 0, "edge_attr_128": 0}
    for name in _INS:
        a = _np.ascontiguousarray(inputs[name])
        if name in pads:
            rest = _np.full((EP - E,) + a.shape[1:], pads[name], a.dtype)
            a = _np.concatenate([a, rest])
        arrays[f"in_{name}"] = a
        args.append(nc.dram_tensor(f"in_{name}", a.shape, _mybir.dt.from_np(a.dtype), kind="ExternalInput").ap())
    args.append(nc.dram_tensor("h_table", (NP, D), F32).ap())
    args.append(nc.dram_tensor("kv_table", (NP, 2 * D), F32).ap())
    args.append(nc.dram_tensor("out_0", (N, D), F32, kind="ExternalOutput").ap())
    gnn_kernel(nc, *args)
    r = _run(nc, [arrays], core_ids=[0])
    return r.results[0]["out_0"]
```

```python
import concourse.bass as bass
from concourse import mybir
from contextlib import ExitStack

F32 = mybir.dt.float32
I32 = mybir.dt.int32
ALU = mybir.AluOpType
ACT = mybir.ActivationFunctionType
AX = mybir.AxisListType

P = 128
D = 128
N = 3125
E = 53125
NB = -(-N // P)
NP = NB * P
NREST = N - (NB - 1) * P
NT = -(-E // P)
EP = NT * P
NCH = -(-NT // P)
NTREST = NT - (NCH - 1) * P
PAD_DST = 4095
R = 8
KEYSTEP = 4096
WA, WB = P, 32
NBB = -(-N // WB)
H8 = 8
NC = NT // 2
NCCH = -(-NC // P)
COUPLES_A = NC + NB - 1
STEPS_B = NT + NBB - 1
H4 = H8 // 2
HALVES_A = -(-COUPLES_A // H4)
HALVES_B = -(-STEPS_B // H8)
assert NT % 2 == 0 and HALVES_A % 2 == 0 and HALVES_B % 2 == 1
SA = HALVES_A * H8
SB = HALVES_B * H8
CA = HALVES_A * H4
assert 2 * CA <= 512
SEG = R * WB
FAR = 1.0e6
BIG = 2.0 ** 100
EPS = 1e-5
RW_MAX = 137


class Count:

    def __init__(self):
        self.base, self.k, self.marked = 0, 0, 0

    def up(self):
        self.k += 1
        return 1

    def count(self):
        return self.base + self.k

    def at(self, base):
        self.base, self.k = base, 0


def gnn_kernel(nc, x, src, dst, xe, ety, w1, root, bias1, bng, bnb, w2, b2, g2, be2,
               waq, baq, wak, bak, wav, bav, was, bas, wbq, bbq, wbk, bbk, wbv, bbv, wbs, bbs,
               h_tab, kv_tab, out):
    ctx = ExitStack()
    with ctx:
        def sb(name, shape, dt=F32):
            return ctx.enter_context(nc.sbuf_tensor(name, shape, dt))

        def sem(name):
            return ctx.enter_context(nc.semaphore(name))

        X = sb("X", [P, NB, D])
        H = sb("H", [P, NB, D])
        Y = sb("Y", [P, NB, D])
        arena = sb("arena", [P, R * NP])
        rings = sb("rings", [P, 8192])
        iota = sb("iota", [P, SB])
        iota_p = sb("iota_p", [P, 1])
        iota_key = sb("iota_key", [P, R, WB])
        tile_no = sb("tile_no", [P, NCH])
        ident = sb("ident", [P, P])
        ones = sb("ones", [P, P])
        ones_rest = sb("ones_rest", [P, P])
        eps_col = sb("eps_col", [P, 1])
        locA = sb("locA", [P, SA + H8])
        srcA = sb("srcA", [P, SA + 2 * H8], I32)
        blkA = sb("blkA", [P, CA + H4], I32)
        locB = sb("locB", [P, SB])
        srcB = sb("srcB", [P, SB], I32)
        blkB = sb("blkB", [P, SB], I32)
        tileB = sb("tileB", [P, SB], I32)
        idx = sb("idx", [P, 2, H8], I32)
        wrel = sb("wrel", [P, R + 1, D])
        rows = sb("rows", [P, 3, D])
        inv_cnt = sb("inv_cnt", [P, NB, R])
        dis = sb("dis", [P, NB])
        st = sb("st", [P, 4, NB])
        small = sb("small", [P, 512])
        stats = sb("stats", [P, NB, 6])
        block_sum = sb("block_sum", [P, D])

        ring_g = rings[:, 0:2048].rearrange("p (s f) -> p s f", s=16)
        ring_xe = rings[:, 2048:4096].rearrange("p (s f) -> p s f", s=16)
        ring_oh2 = rings[:, 4096:8192].rearrange("p (s f) -> p s f", s=16)
        ring_kv = rings[:, 0:4096].rearrange("p (s f) -> p s f", s=16)
        ring_oh = rings[:, 4096:6144].rearrange("p (s f) -> p s f", s=16)
        oh_t = rings[:, 6144:7168].rearrange("p (s f) -> p s f", s=8)
        prod = rings[:, 7168:8192].rearrange("p (s f) -> p s f", s=8)
        acb = [rings[:, j * 1024:(j + 1) * 1024] for j in range(2)]
        h_fix = [rings[:, 2048 + j * P:2048 + (j + 1) * P] for j in range(2)]
        hT_fix = [rings[:, 2304 + j * P:2304 + (j + 1) * P] for j in range(2)]
        parts = [rings[:, 2560 + j * (R + 2) * D:2560 + (j + 1) * (R + 2) * D].rearrange("p (r f) -> p r f", r=R + 2) for j in range(2)]

        bank = [ctx.enter_context(nc.psum_tensor(f"bank{i}", [P, 512], F32)) for i in range(8)]

        o = 8192
        row_i = arena[:, o:o + 3 * NCH * P].bitcast(I32).rearrange("p (a c f) -> p a c f", a=3, c=NCH); o += 3 * NCH * P
        row_f = arena[:, o:o + 3 * NCH * P].rearrange("p (a c f) -> p a c f", a=3, c=NCH); o += 3 * NCH * P
        row_key = arena[:, o:o + NCH * P].rearrange("p (c f) -> p c f", c=NCH); o += NCH * P
        hit = arena[:, o:o + NCH * SB].rearrange("p (c s) -> p c s", c=NCH); o += NCH * SB
        spread = arena[:, o:o + 2 * NCH * P].rearrange("p (a c f) -> p a c f", a=2, c=NCH); o += 2 * NCH * P
        tri = arena[:, o:o + P]; o += P
        tmp_s = arena[:, o:o + 3 * SB].rearrange("p (a s) -> p a s", a=3); o += 3 * SB
        tc = arena[:, o:o + 9 * NCH].rearrange("p (a c) -> p a c", a=9); o += 9 * NCH
        tci = arena[:, o:o + 2 * NCH].bitcast(I32).rearrange("p (a c) -> p a c", a=2); o += 2 * NCH
        couple_i = arena[:, o:o + 6 * NCCH * P].bitcast(I32).rearrange("p (a c f) -> p a c f", a=3, c=NCCH); o += 6 * NCCH * P
        couple_f = arena[:, o:o + 6 * NCCH * P].rearrange("p (a c f) -> p a c f", a=3, c=NCCH); o += 6 * NCCH * P
        assert o <= R * NP - NP
        A0 = D + R
        acc0 = arena[:, 0:NB * A0].rearrange("p (b f) -> p b f", b=NB)
        rel_hot = arena[:, 4096:4096 + SA * R].rearrange("p (s r) -> p s r", r=R)
        acc1 = arena[:, :]
        acc2 = arena[:, 0:NP].rearrange("p (b f) -> p b f", b=NB)
        y2 = arena[:, NP:2 * NP].rearrange("p (b f) -> p b f", b=NB)
        scratch = arena[:, R * NP - NP:R * NP].rearrange("p (b f) -> p b f", b=NB)
        qt = arena[:, 0:NP]
        skip = arena[:, NP:2 * NP].rearrange("p (b f) -> p b f", b=NB)
        kvt = arena[:, 2 * NP:4 * NP].rearrange("p (b f) -> p b f", b=NB)
        o = 4 * NP
        wqkvs = arena[:, o:o + 4 * D]; o += 4 * D
        bqkvs = arena[:, o:o + 4 * D]; o += 4 * D
        acc3 = arena[:, o:o + NB * 132]; o += NB * 132
        part_all = arena[:, o:o + 2 * H4 * 132]; o += 2 * H4 * 132
        rhs3 = arena[:, o:o + H8 * RW_MAX]; o += H8 * RW_MAX
        keyT_all = arena[:, o:o + 2 * P]; o += 2 * P
        reset_all = arena[:, o:o + 2 * P + 4]; o += 2 * P + 4
        fwd_all = arena[:, o:o + 2 * P]; o += 2 * P
        largest_all = arena[:, o:o + 2 * P]; o += 2 * P
        assert o <= R * NP - NP
        fl = sb("fl", [P, 512])
        mst = sb("mst", [P, NB * 4])

        ORDER = ["list0", "ln0", "sum", "list1", "ln1", "rel0", "rel1", "ln2", "gcn", "gcn_ln", "ln3", "att0", "att1"]
        PHASES = ["sum", "rel0", "rel1", "gcn", "att0", "att1"]
        RELS, ATTS, PROJ = ("rel0", "rel1"), ("att0", "att1"), ("rel0", "rel1", "gcn", "att0", "att1")
        halves_of = {ph: HALVES_B if ph in RELS else HALVES_A for ph in PHASES}
        LOADS = ("table", "w", "w_root", "row0", "row1", "row2", "w0", "w1", "w2", "w3", "b0", "b1", "b2", "b3")

        def total(stage, event):
            hv = halves_of.get(stage, 0)
            if event == "idx_made":
                return hv + 2 * (stage in ATTS)
            if event == "hot_made":
                return hv * H8 if stage in RELS else (hv + (stage in ATTS)) * H4
            if event == "step_done":
                return 16 * (hv > 0) + hv * H8
            if event == "added":
                return hv if stage in ATTS else 8 * (hv > 0) + hv * (H8 if stage in RELS else H4)
            if event in ("msg_sum", "msg_made"):
                return hv * H8 * (stage in RELS)
            if event == "logits":
                return 2 * hv * (stage in ATTS)
            if event in ("hotT", "hotT_copied", "q_done"):
                return 2 * (hv + 1) * (stage in ATTS)
            if event in ("rhs_made", "logT", "max_made", "maxT", "diff", "exped", "resc", "resc_exped"):
                return hv * (stage in ATTS)
            if event == "parted":
                return hv * H4 * (stage in ATTS)
            if event in ("locs_made", "keyT_made"):
                return hv * (stage in ATTS)
            if event == "marked":
                return hv * (stage in ATTS)
            if event in ("h_fixed", "hT_done", "hT_made", "proj_done", "proj_read"):
                return NB * (stage in PROJ)
            if event in ("sums_fixed", "root_copied"):
                return NB * (stage in RELS)
            if event in ("picked", "read"):
                return {"list0": 1, "list1": 2}.get(stage, 0)
            if event in ("counts", "starts", "hits", "made"):
                return 1 * (stage in ("list0", "list1"))
            if event in ("centred", "squared"):
                return 1 * (stage in RELS)
            if event == "blocks_summed":
                return 2 * (stage in RELS)
            if event in ("var", "root"):
                return 1 * (stage[:2] == "ln" or stage in ("gcn_ln",) + RELS)
            if event == "ready":
                return 1 * (stage[:2] == "ln")
            if event in ("mean_sum", "var_sum"):
                return 1 * (stage in RELS)
            if event == "table_made":
                return 1 * (stage in ("gcn",) + ATTS)
            if event == "start":
                return 1 * (hv > 0)
            if event == "zeroed":
                return 1 * (stage in RELS)
            if event == "over":
                return 1 * (stage in PROJ)
            if event in LOADS:
                of = dict(table=PHASES, w=("rel0", "rel1", "gcn"), w_root=RELS, row0=("rel0", "rel1", "gcn"), row1=("rel0", "rel1", "gcn"),
                          row2=("rel0", "rel1", "gcn")).get(event, ATTS)
                return 16 * (stage in of)
            raise KeyError(event)

        PRIME = 2
        PRIMED = {"pe": ("hT_done", "proj_done", "q_done"), "act": ("hT_made",), "dve": ("proj_read", "rhs_made")}

        def prime(eng, name):
            for event in PRIMED[name]:
                eng.sem_inc(ev("rel0." + event), PRIME)

        made = {}

        def ev(name):
            stage, _, event = name.rpartition(".")
            key = event if stage in ORDER else name.replace(".", "_")
            if key not in made:
                made[key] = ctx.enter_context(nc.semaphore(key))
            return made[key]

        def at(name, count):
            stage, _, event = name.rpartition(".")
            if stage not in ORDER:
                return count
            before = sum(total(q, event) for q in ORDER[:ORDER.index(stage)])
            return before + PRIME * any(event in events for events in PRIMED.values()) + count

        gath = [ev(f"gathered{k}") for k in range(16)]
        xe_in = [ev(f"edge_rows_in{k}") for k in range(16)]

        def rounds_before(ph, par, phases=PHASES):
            return sum((halves_of[q] + 1 - par) // 2 for q in phases[:phases.index(ph)])

        def gathers_seen(ph, i, par):
            return 16 * (rounds_before(ph, par) + i)

        def edge_rows_seen(ph, i, par):
            return 16 * (rounds_before(ph, par, ["rel0", "rel1"]) + i)

        def halves(eng, count, body):
            with eng.Fori(0, count // 2) as i:
                body(2 * i, i, 0)
                body(2 * i + 1, i, 1)
            if count % 2:
                body(count - 1, count // 2, 0)

        def skewed(eng, body):
            body(0, 0, 0)
            body(1, 0, 1)
            with eng.Fori(1, HALVES_A // 2) as i:
                body(2 * i, i, 0)
                body(2 * i + 1, i, 1)

        def registers(eng, table, h, top, n=H8, count=1):
            _, regs = nc.values_load_multi_w_load_instructions(
                table[0:1, bass.ds(n * h, n * count)], engines=[eng.engine], min_val=0, max_val=top - 1,
                skip_runtime_bounds_check_because="the step list's entries are below this by construction")
            return regs

        block = ctx.enter_context(nc.Block())

        @block.sync
        def _(sp):
            full = (NCH - 1) * P
            for a, arr in enumerate((dst, src, ety)):
                v = arr.rearrange("(t p) -> t p", p=2 * P)
                sp.dma_start(couple_i[:, a, 0, :], v[0:P, :]).then_inc(ev(f"couples.in{2 * a}"), 16)
            sp.wait_ge(ev("couples.zeroed"), at("couples.zeroed", 1))
            for a, arr in enumerate((dst, src, ety)):
                v = arr.rearrange("(t p) -> t p", p=2 * P)
                sp.dma_start(couple_i[0:NC - P, a, 1, :], v[P:NC, :]).then_inc(ev(f"couples.in{2 * a + 1}"), 16)
            sp.wait_ge(ev("rows.zeroed"), at("rows.zeroed", 1))
            for a, arr in enumerate((dst, src, ety)):
                v = arr.rearrange("(t p) -> t p", p=P)
                sp.dma_start(row_i[:, a, 0:NCH - 1, :], v[0:full, :].rearrange("(c t) p -> t c p", t=P)).then_inc(ev(f"rows.in{2 * a}"), 16)
                sp.dma_start(row_i[0:NTREST, a, NCH - 1, :], v[full:NT, :]).then_inc(ev(f"rows.in{2 * a + 1}"), 16)
            sp.wait_ge(ev("x.zeroed"), at("x.zeroed", 1))
            sp.dma_start(X[:, 0:NB - 1, :], x[0:(NB - 1) * P, :].rearrange("(b p) f -> p b f", p=P)).then_inc(ev("x.in0"), 16)
            sp.dma_start(X[0:NREST, NB - 1, :], x[(NB - 1) * P:N, :]).then_inc(ev("x.in1"), 16)

            def store_table(ph, rows_t, tab, ready):
                sp.wait_ge(ev(ready), at(ready, 1))
                sp.dma_start(tab.rearrange("(b p) f -> p b f", p=P), rows_t).then_inc(ev(ph + ".table"), 16)

            def load_rel(layer):
                ph = f"rel{layer}"
                sp.dma_start(wrel[:, 0:R, :], w1[layer].rearrange("r k n -> k r n")).then_inc(ev(ph + ".w"), 16)
                sp.dma_start(wrel[:, R, :], root[layer]).then_inc(ev(ph + ".w_root"), 16)
                for j, v in enumerate((bias1, bng, bnb)):
                    sp.dma_start(rows[:, j, :], v[layer:layer + 1, :].broadcast_to([P, D])).then_inc(ev(f"{ph}.row{j}"), 16)

            def load_edge_rows(ph):
                def half(h, i, par):
                    tiles = registers(sp, tileB, h, NT)
                    for k in range(H8):
                        s = par * H8 + k
                        sp.wait_ge(ev(ph + ".step_done"), at(ph + ".step_done", H8 * h + k + 1))
                        sp.dma_start(ring_xe[:, s, :], xe[bass.ds(tiles[k] * P, P), :]).then_inc(xe_in[s], 16)
                halves(sp, HALVES_B, half)

            load_rel(0)
            store_table("sum", H[:, :, :], h_tab, "ln0.ready")
            store_table("rel0", H[:, :, :], h_tab, "ln1.ready")
            sp.wait_ge(ev("list1.made"), at("list1.made", 1))
            load_edge_rows("rel0")
            sp.wait_ge(ev("rel0.over"), at("rel0.over", 1))
            load_rel(1)
            store_table("rel1", H[:, :, :], h_tab, "rel0.over")
            load_edge_rows("rel1")
            sp.wait_ge(ev("rel1.over"), at("rel1.over", 1))
            sp.dma_start(wrel[:, 0, :], w2).then_inc(ev("gcn.w"), 16)
            for j, v in enumerate((b2, g2, be2)):
                sp.dma_start(rows[:, j, :], v.rearrange("(a f) -> a f", a=1).broadcast_to([P, D])).then_inc(ev(f"gcn.row{j}"), 16)
            store_table("gcn", y2, h_tab, "gcn.table_made")
            weights = ((waq, wak, wav, was), (wbq, wbk, wbv, wbs))
            biases = ((baq, bak, bav, bas), (bbq, bbk, bbv, bbs))
            for l, ph in enumerate(("att0", "att1")):
                sp.wait_ge(ev(("gcn.over", "att0.over")[l]), at(("gcn.over", "att0.over")[l], 1))
                for j in range(4):
                    sp.dma_start(wqkvs[:, j * D:(j + 1) * D], weights[l][j]).then_inc(ev(f"{ph}.w{j}"), 16)
                    sp.dma_start(bqkvs[:, j * D:(j + 1) * D], biases[l][j].rearrange("(a f) -> a f", a=1).broadcast_to([P, D]))\
                      .then_inc(ev(f"{ph}.b{j}"), 16)
                store_table(ph, kvt, kv_tab, ph + ".table_made")
            sp.wait_ge(ev("att1.over"), at("att1.over", 1))
            sp.dma_start(out[0:(NB - 1) * P, :].rearrange("(b p) f -> p b f", p=P), X[:, 0:NB - 1, :]).then_inc(ev("out0"), 16)
            sp.dma_start(out[(NB - 1) * P:N, :], X[0:NREST, NB - 1, :]).then_inc(ev("out1"), 16)
            sp.wait_ge(ev("out0"), at("out0", 16))
            sp.wait_ge(ev("out1"), at("out1", 16))

        @block.gpsimd
        def _(pool):
            kw = dict(allow_small_or_imprecise_dtypes=True)
            for t, pattern, cm in ((iota[:, :], [[1, SB]], 0), (iota_p[:, :], [[1, 1]], 1), (iota_key[:, :, :], [[KEYSTEP, R], [1, WB]], 0), (tile_no[:, :], [[P, NCH]], 1)):
                nc.gpsimd.iota(t, pattern=pattern, base=0, channel_multiplier=cm, **kw).then_inc(ev("iotas"), 1)
            for ph in PHASES:
                att = ph in ("att0", "att1")
                if ph in ("rel0", "rel1"):
                    if ph == "rel0":
                        pool.wait_ge(ev("arena_free"), at("arena_free", 1))
                    else:
                        pool.wait_ge(ev("rel0.sums_fixed"), at("rel0.sums_fixed", NB))
                    nc.gpsimd.memset(arena[:, 0:R * NP - NP], 0.0).then_inc(ev(ph + ".zeroed"), 1)
                table, ring = (kv_tab, ring_kv) if att else (h_tab, ring_g)
                pool.wait_ge(ev(ph + ".table"), at(ph + ".table", 16))

                if att:
                    pool.wait_ge(ev(ph + ".step_done"), at(ph + ".step_done", 16))

                def half(h, i, par):
                    pool.wait_ge(ev(ph + ".idx_made"), at(ph + ".idx_made", h + 1))
                    if att:
                        pool.wait_ge(ev(ph + ".rhs_made"), at(ph + ".rhs_made", h - 1))
                    else:
                        pool.wait_ge(ev(ph + ".step_done"), at(ph + ".step_done", H8 * h + H8))
                    pool.sem_inc(ev("pool_turns"), 1)
                    for k in range(H8):
                        s = par * H8 + k
                        nc.gpsimd.indirect_dma_start(
                            out=ring[:, s, :], out_offset=None, in_=table,
                            in_offset=bass.IndirectOffsetOnAxis(ap=idx[:, par, k:k + 1], axis=0)).then_inc(gath[s], 16)
                halves(pool, halves_of[ph], half)

        @block.scalar
        def _(act):
            def norm_root(name):
                act.wait_ge(ev(name + ".var"), at(name + ".var", 1))
                act.activation(st[:, 2, :], st[:, 1, :], ACT.Sqrt, bias=eps_col[:, :], scale=1.0 / D).then_inc(ev(name + ".root"), 1)

            def gather_indices(ph, tab):
                def half(h, i, par):
                    act.wait_ge(ev(ph + ".step_done"), at(ph + ".step_done", H8 * h + H8))
                    act.activation(idx[:, par, :], tab[:, bass.ds(H8 * h, H8)], ACT.Copy).then_inc(ev(ph + ".idx_made"), 1)
                return half

            def copy_block(name, n, par):
                act.wait_ge(ev(name + ".hT_done"), at(name + ".hT_done", n - 1))
                act.activation(h_fix[par], H[:, bass.ds(n, 1), :].rearrange("p a f -> p (a f)"), ACT.Copy).then_inc(ev(name + ".h_fixed"), 1)

            def copy_transpose(name, n, par):
                act.wait_ge(ev(name + ".hT_done"), at(name + ".hT_done", n + 1))
                act.wait_ge(ev(name + ".proj_done"), at(name + ".proj_done", n - 1))
                act.activation(hT_fix[par], bank[7 * par][:, 0:P], ACT.Copy).then_inc(ev(name + ".hT_made"), 1)

            def fixed_blocks(name):
                def block_of(n, i, par):
                    if not (isinstance(n, int) and n == NB - 1):
                        copy_block(name, n + 1, 1 - par)
                    copy_transpose(name, n, par)
                copy_block(name, 0, 0)
                halves(act, NB, block_of)

            prime(act, "act")
            norm_root("ln0")
            act.wait_ge(ev("list0.made"), at("list0.made", 1))
            halves(act, HALVES_A, gather_indices("sum", srcA))
            norm_root("ln1")
            act.wait_ge(ev("list1.made"), at("list1.made", 1))
            for l, ph in enumerate(("rel0", "rel1")):
                prep = gather_indices(ph, srcB)

                def relus(h, par):
                    for k in range(H8):
                        s = par * H8 + k
                        act.wait_ge(ev(ph + ".msg_sum"), at(ph + ".msg_sum", H8 * h + k + 1))
                        act.activation(ring_xe[:, s, :], ring_xe[:, s, :], ACT.Relu).then_inc(ev(ph + ".msg_made"), 1)

                prep(0, 0, 0)
                with act.Fori(0, HALVES_B // 2) as i:
                    prep(2 * i + 1, i, 1)
                    relus(2 * i, 0)
                    prep(2 * i + 2, i + 1, 0)
                    relus(2 * i + 1, 1)
                relus(HALVES_B - 1, 0)
                act.wait_ge(ev(ph + ".added"), at(ph + ".added", 8 + SB))

                def node_block(n, i, par):
                    act.wait_ge(ev(ph + ".proj_done"), at(ph + ".proj_done", n - 1))
                    act.activation(acb[par].rearrange("p (r b n) -> p b r n", r=R, b=P // WB),
                                   acc1[:, bass.ds(R * P * n, R * P)].rearrange("p (b r n) -> p b r n", b=P // WB, r=R),
                                   ACT.Copy).then_inc(ev(ph + ".sums_fixed"), 1)
                    copy_block(ph, n, par)
                    copy_transpose(ph, n, par)

                def copy_root(n, par):
                    act.wait_ge(ev(ph + ".proj_done"), at(ph + ".proj_done", n + 1))
                    act.wait_ge(ev(ph + ".proj_read"), at(ph + ".proj_read", n - 1))
                    act.activation(parts[par][:, R, :], bank[3 + 3 * par][:, 0:D], ACT.Copy).then_inc(ev(ph + ".root_copied"), 1)

                node_block(0, 0, 0)
                with act.Fori(0, NB // 2) as i:
                    node_block(2 * i + 1, i, 1)
                    copy_root(2 * i, 0)
                    node_block(2 * i + 2, i + 1, 0)
                    copy_root(2 * i + 1, 1)
                copy_root(NB - 1, 0)
                act.wait_ge(ev(ph + ".centred"), at(ph + ".centred", 1))
                act.activation(scratch, Y[:, :, :], ACT.Square).then_inc(ev(ph + ".squared"), 1)
                act.wait_ge(ev(ph + ".var"), at(ph + ".var", 1))
                act.activation(small[:, 128:256], small[:, 0:128], ACT.Sqrt, bias=eps_col[:, :], scale=1.0 / N).then_inc(ev(ph + ".root"), 1)
            norm_root("ln2")
            act.wait_ge(ev("deg.made"), at("deg.made", 1))
            act.activation(st[:, 2, :], st[:, 3, :], ACT.Sqrt).then_inc(ev("deg.root"), 1)
            act.wait_ge(ev("ln2.ready"), at("ln2.ready", 1))
            fixed_blocks("gcn")
            halves(act, HALVES_A, gather_indices("gcn", srcA))
            norm_root("gcn_ln")
            norm_root("ln3")
            for l, ph in enumerate(("att0", "att1")):
                nh = (4, 1)[l]
                scale = float(D // nh) ** -0.5
                q4, q8 = H4 * nh, H8 * nh
                act.wait_ge(ev(("ln3.ready", "att0.over")[l]), at(("ln3.ready", "att0.over")[l], 1))
                fixed_blocks(ph)
                prep = gather_indices(ph, srcA)
                dif = fl[:, 0:q8]
                ab = [fl[:, 256 + 32 * j:256 + 32 * j + 2 * q4] for j in range(2)]
                locs = fl[:, 192:192 + q8]
                keyT = keyT_all[0:q4, :]
                ch, aw, rw = D // nh, D + nh, D + 2 * nh + 1
                rhs = rhs3[:, 0:H8 * rw].rearrange("p (s f) -> p s f", s=H8)

                def copy_hotT(h, j):
                    act.wait_ge(ev(ph + ".hotT"), at(ph + ".hotT", 2 * h + j + 1))
                    act.wait_ge(ev(ph + ".q_done"), at(ph + ".q_done", 2 * h))
                    act.activation(oh_t[:, 4 * j:4 * j + 4, :], bank[j][:, :].rearrange("p (s f) -> p s f", s=4), ACT.Copy)\
                       .then_inc(ev(ph + ".hotT_copied"), 1)

                def factors(h, par):
                    act.wait_ge(ev(ph + ".resc"), at(ph + ".resc", h + 1))
                    act.activation(ab[par], ab[par], ACT.Exp, scale=scale).then_inc(ev(ph + ".resc_exped"), 1)
                    act.wait_ge(ev(ph + ".resc_exped"), at(ph + ".resc_exped", h + 1))
                    act.wait_ge(ev(ph + ".added"), at(ph + ".added", h - 1))

                def new_part(k, par):
                    for a in range(nh):
                        ins = act.activation(part_all[:, (par * H4 + k) * aw + a * (ch + 1):(par * H4 + k) * aw + (a + 1) * (ch + 1)],
                                             bank[5 + k // 3][:, (k % 3) * rw + a * (ch + 1):(k % 3) * rw + (a + 1) * (ch + 1)],
                                             ACT.Copy, scale=ab[par][:, q4 + k * nh + a:q4 + k * nh + a + 1])
                    ins.then_inc(ev(ph + ".parted"), 1)

                def half(h, i, par):
                    first = isinstance(h, int) and h == 0
                    act.activation(locs.rearrange("p (u g a) -> p g u a", u=2, a=nh),
                                   locA[:, bass.ds(H8 * h, H8)].rearrange("p (g u a) -> p g u a", u=2, a=1).broadcast_to([P, H4, 2, nh]), ACT.Copy)\
                       .then_inc(ev(ph + ".locs_made"), 1)
                    act.wait_ge(ev(ph + ".logT"), at(ph + ".logT", h + 1))
                    act.activation(idx[:, par, :], srcA[:, bass.ds(H8 * h + 2 * H8, H8)], ACT.Copy).then_inc(ev(ph + ".idx_made"), 1)
                    act.activation(keyT, bank[4][0:q4, 2 * P:4 * P], ACT.Copy, scale=BIG).then_inc(ev(ph + ".keyT_made"), 1)
                    copy_hotT(h + 1, 0)
                    if not first:
                        factors(h - 1, 1 - par)
                        new_part(0, 1 - par)
                    copy_hotT(h + 1, 1)
                    act.wait_ge(ev(ph + ".diff"), at(ph + ".diff", h + 1))
                    act.activation(rhs[:, :, 0:aw].rearrange("p (g u) (a c) -> p g u a c", u=2, a=nh)[:, :, :, :, ch],
                                   dif.rearrange("p (u g a) -> p g u a", u=2, a=nh), ACT.Exp, scale=scale).then_inc(ev(ph + ".exped"), 1)
                    if not first:
                        for k in range(1, H4):
                            new_part(k, 1 - par)

                prep(0, 0, 0)
                prep(1, 0, 1)
                copy_hotT(0, 0)
                copy_hotT(0, 1)
                skewed(act, half)
                factors(HALVES_A - 1, 1)
                for k in range(H4):
                    new_part(k, 1)

        def open_ring(pe, ph):
            pe.wait_ge(ev(ph + ".start"), at(ph + ".start", 1))
            pe.sem_inc(ev(ph + ".step_done"), 16)

        def plain_products(pe, ph):
            def half(h, i, par):
                for g in range(H4):
                    slots = (par * H8 + 2 * g, par * H8 + 2 * g + 1)
                    sums = bank[par * H4 + g]
                    pe.wait_ge(ev(ph + ".hot_made"), at(ph + ".hot_made", H4 * h + g + 1))
                    pe.wait_ge(ev(ph + ".added"), at(ph + ".added", H4 * h + g + 1))
                    for u, s in enumerate(slots):
                        pe.wait_ge(gath[s], gathers_seen(ph, i + 1, par))
                        last = nc.tensor.matmul(sums[:, 0:D], ring_oh[:, s, :], ring_g[:, s, :], start=(u == 0), stop=(u == 1))
                        if ph == "gcn":
                            last.then_inc(ev(ph + ".step_done"), 1)
                    if ph == "sum":
                        for u, s in enumerate(slots):
                            nc.tensor.matmul(sums[:, D:D + R], ring_oh[:, s, :],
                                             rel_hot[:, bass.ds(H8 * h + 2 * g + u, 1), :].rearrange("p a r -> p (a r)"), start=(u == 0), stop=(u == 1))\
                                .then_inc(ev(ph + ".step_done"), 1)
            halves(pe, HALVES_A, half)

        def node_sum(pe, t, name):
            nc.tensor.matmul(bank[5][:, 0:D], ones[:, :], block_sum[:, :], start=True, stop=False)
            nc.tensor.matmul(bank[5][:, 0:D], ones_rest[:, :], t[:, NB - 1, :], start=False, stop=True).then_inc(ev(name), 1)

        @block.tensor
        def _(pe):
            prime(pe, "pe")
            for n, cols in enumerate((CA, SB)):
                nm = f"list{n}"
                nch = (NCCH, NCH)[n]
                pe.wait_ge(ev(nm + ".counts"), at(nm + ".counts", 1))
                nc.tensor.matmul(bank[0][:, 0:nch], tri, tc[:, 2, 0:nch], start=True, stop=False)
                nc.tensor.matmul(bank[0][:, 0:nch], ones[:, :], tc[:, 3, 0:nch], start=False, stop=True).then_inc(ev(nm + ".starts"), 1)
                pe.wait_ge(ev(nm + ".hits"), at(nm + ".hits", 1))
                if n == 0:
                    for q in range(8):
                        for c in range(NCCH):
                            lhs = (spread[:, 0, c, :], ones[:, :])[q] if q < 2 else couple_f[:, q // 2 - 1, c, (q % 2) * P:(q % 2 + 1) * P]
                            last = nc.tensor.matmul(bank[1 + q // 2][:, (q % 2) * cols:(q % 2 + 1) * cols], lhs, hit[:, c, 0:cols],
                                                    start=(c == 0), stop=(c == NCCH - 1))
                    last.then_inc(ev(nm + ".picked"), 1)
                    open_ring(pe, "sum")
                    continue
                hw = cols // 2
                for hf in range(2):
                    if hf:
                        pe.wait_ge(ev(nm + ".read"), at(nm + ".read", hf))
                    for q in range(5):
                        for c in range(NCH):
                            lhs = (spread[:, 0, c, :], ones[:, :], row_key[:, c, :], row_f[:, 1, c, :], spread[:, 1, c, :])[q]
                            last = nc.tensor.matmul(bank[1 + q][:, 0:hw], lhs, hit[:, c, hf * hw:(hf + 1) * hw],
                                                    start=(c == 0), stop=(c == NCH - 1))
                    last.then_inc(ev(nm + ".picked"), 1)
            plain_products(pe, "sum")

            for l, ph in enumerate(("rel0", "rel1")):
                open_ring(pe, ph)

                def half(h, i, par):
                    for k in range(H8):
                        s = par * H8 + k
                        step = H8 * h + k
                        pe.wait_ge(ev(ph + ".hot_made"), at(ph + ".hot_made", step + 1))
                        pe.wait_ge(ev(ph + ".msg_made"), at(ph + ".msg_made", step + 1))
                        pe.wait_ge(ev(ph + ".added"), at(ph + ".added", step + 1))
                        nc.tensor.matmul(bank[k][:, 0:SEG], ring_xe[:, s, :], ring_oh2[:, s, :], start=True, stop=True)\
                            .then_inc(ev(ph + ".step_done"), 1)
                halves(pe, HALVES_B, half)
                pe.wait_ge(ev(ph + ".w"), at(ph + ".w", 16))
                pe.wait_ge(ev(ph + ".w_root"), at(ph + ".w_root", 16))
                pe.wait_ge(ev(ph + ".added"), at(ph + ".added", 8 + SB))

                def node_block(n, i, par):
                    pe.wait_ge(ev(ph + ".h_fixed"), at(ph + ".h_fixed", n + 1))
                    pe.wait_ge(ev(ph + ".hT_made"), at(ph + ".hT_made", n - 1))
                    nc.tensor.transpose(bank[7 * par][:, 0:P], h_fix[par], ident[:, :]).then_inc(ev(ph + ".hT_done"), 1)
                    pe.wait_ge(ev(ph + ".sums_fixed"), at(ph + ".sums_fixed", n + 1))
                    pe.wait_ge(ev(ph + ".proj_read"), at(ph + ".proj_read", n - 1))
                    for r in range(R):
                        nc.tensor.matmul(bank[1 + 3 * par + r // 4][:, (r % 4) * D:(r % 4 + 1) * D], acb[par][:, r * P:(r + 1) * P], wrel[:, r, :],
                                         start=True, stop=True)
                    pe.wait_ge(ev(ph + ".hT_made"), at(ph + ".hT_made", n + 1))
                    nc.tensor.matmul(bank[3 + 3 * par][:, 0:D], hT_fix[par], wrel[:, R, :], start=True, stop=True).then_inc(ev(ph + ".proj_done"), 1)
                halves(pe, NB, node_block)
                pe.wait_ge(ev(ph + ".proj_read"), at(ph + ".proj_read", NB))
                pe.wait_ge(ev(ph + ".blocks_summed"), at(ph + ".blocks_summed", 1))
                node_sum(pe, Y[:, :, :], ph + ".mean_sum")
                pe.wait_ge(ev(ph + ".squared"), at(ph + ".squared", 1))
                pe.wait_ge(ev(ph + ".blocks_summed"), at(ph + ".blocks_summed", 2))
                node_sum(pe, scratch, ph + ".var_sum")

            def project(ph, weights, width, loads):
                for name in loads:
                    pe.wait_ge(ev(name), at(name, 16))

                def transpose_block(n, par):
                    pe.wait_ge(ev(ph + ".h_fixed"), at(ph + ".h_fixed", n + 1))
                    pe.wait_ge(ev(ph + ".hT_made"), at(ph + ".hT_made", n - 1))
                    nc.tensor.transpose(bank[7 * par][:, 0:P], h_fix[par], ident[:, :]).then_inc(ev(ph + ".hT_done"), 1)

                def node_block(n, i, par):
                    if not (isinstance(n, int) and n == NB - 1):
                        transpose_block(n + 1, 1 - par)
                    pe.wait_ge(ev(ph + ".proj_read"), at(ph + ".proj_read", n - 1))
                    pe.wait_ge(ev(ph + ".hT_made"), at(ph + ".hT_made", n + 1))
                    nc.tensor.matmul(bank[1 + 3 * par][:, 0:width], hT_fix[par], weights, start=True, stop=True).then_inc(ev(ph + ".proj_done"), 1)
                transpose_block(0, 0)
                halves(pe, NB, node_block)

            project("gcn", wrel[:, 0, :], D, ["gcn.w"])
            open_ring(pe, "gcn")
            plain_products(pe, "gcn")
            for l, ph in enumerate(("att0", "att1")):
                nh = (4, 1)[l]
                q4, q8 = H4 * nh, H8 * nh
                rw = D + 2 * nh + 1
                rhs = rhs3[:, 0:H8 * rw].rearrange("p (s f) -> p s f", s=H8)
                project(ph, wqkvs, 4 * D, [f"{ph}.w{j}" for j in range(4)])
                open_ring(pe, ph)
                logits, locs = fl[:, 128:128 + q8], fl[:, 192:192 + q8]
                largest, reset = largest_all[0:q4, :], reset_all[0:q4, 0:2 * P + 1]

                def transpose_hots(h, par, j):
                    pe.wait_ge(ev(ph + ".hot_made"), at(ph + ".hot_made", H4 * h + 2 * j + 2))
                    for k in range(4):
                        last = nc.tensor.transpose(bank[j][:, k * P:(k + 1) * P], ring_oh[:, par * H8 + 4 * j + k, :], ident[:, :])
                    last.then_inc(ev(ph + ".hotT"), 1)

                def pick_queries(h, j, blks):
                    pe.wait_ge(ev(ph + ".hotT_copied"), at(ph + ".hotT_copied", 2 * h + j + 1))
                    for k in range(4):
                        last = nc.tensor.matmul(bank[2 + j][:, k * P:(k + 1) * P], oh_t[:, 4 * j + k, :], qt[:, bass.ds(blks[2 * j + k // 2] * D, D)],
                                                start=True, stop=True)
                    last.then_inc(ev(ph + ".q_done"), 1)

                def half(h, i, par):
                    for u in range(2):
                        pe.wait_ge(ev(ph + ".logits"), at(ph + ".logits", 2 * h + u + 1))
                        nc.tensor.matmul(bank[4][0:q4, u * P:(u + 1) * P], logits[:, u * q4:(u + 1) * q4], ident[:, :], start=True, stop=True)
                    pe.wait_ge(ev(ph + ".locs_made"), at(ph + ".locs_made", h + 1))
                    for u in range(2):
                        last = nc.tensor.matmul(bank[4][0:q4, (2 + u) * P:(3 + u) * P], locs[:, u * q4:(u + 1) * q4], ident[:, :], start=True, stop=True)
                    last.then_inc(ev(ph + ".logT"), 1)
                    transpose_hots(h + 1, 1 - par, 0)
                    blks = registers(pe, blkA, h + 1, NB, H4)
                    pick_queries(h + 1, 0, blks)
                    transpose_hots(h + 1, 1 - par, 1)
                    pe.wait_ge(ev(ph + ".max_made"), at(ph + ".max_made", h + 1))
                    pe.sem_inc(ev("pe_turns"), 1)
                    for a, t in enumerate((largest, reset)):
                        for u in range(2):
                            last = nc.tensor.transpose(bank[7][:, a * q8 + u * q4:a * q8 + (u + 1) * q4], t[:, u * P:(u + 1) * P], ident[0:q4, 0:q4])
                    last.then_inc(ev(ph + ".maxT"), 1)
                    pick_queries(h + 1, 1, blks)
                    pe.wait_ge(ev(ph + ".marked"), at(ph + ".marked", h + 1))
                    pe.wait_ge(ev(ph + ".exped"), at(ph + ".exped", h + 1))
                    pe.wait_ge(ev(ph + ".rhs_made"), at(ph + ".rhs_made", h + 1))
                    if not (isinstance(h, int) and h == 0):
                        pe.wait_ge(ev(ph + ".parted"), at(ph + ".parted", H4 * h))
                    for k in range(H8):
                        g, u = k // 2, k % 2
                        nc.tensor.matmul(bank[5 + g // 3][:, (g % 3) * rw:(g % 3 + 1) * rw], ring_oh[:, par * H8 + k, :], rhs[:, k, :],
                                         start=(u == 0), stop=(u == 1)).then_inc(ev(ph + ".step_done"), 1)

                for j in range(2):
                    transpose_hots(0, 0, j)
                blks = registers(pe, blkA, 0, NB, H4)
                pick_queries(0, 0, blks)
                pick_queries(0, 1, blks)
                skewed(pe, half)

        @block.vector
        def _(dve):
            v = nc.vector
            own, dve_done = Count(), ev("dve_done")
            prime(dve, "dve")
            v.memset(row_i[:, :, NCH - 1, :], 0).then_inc(ev("rows.zeroed"), 1)
            v.memset(couple_i[:, :, 1, :], 0).then_inc(ev("couples.zeroed"), 1)
            v.memset(X[:, NB - 1, :], 0.0).then_inc(ev("x.zeroed"), 1)
            v.memset(ones[:, :], 1.0).then_inc(dve_done, own.up())
            v.memset(eps_col[:, :], EPS).then_inc(dve_done, own.up())
            v.memset(arena[:, 0:NB * A0], 0.0).then_inc(dve_done, own.up())
            v.memset(locA[:, SA:SA + H8], FAR).then_inc(dve_done, own.up())
            v.memset(srcA[:, SA:SA + 2 * H8], 0).then_inc(dve_done, own.up())
            v.memset(blkA[:, CA:CA + H4], 0).then_inc(dve_done, own.up())
            dve.wait_ge(ev("iotas"), at("iotas", 4))
            v.tensor_scalar(ident[:, :], iota[:, 0:P], iota_p[:, :], None, ALU.is_equal).then_inc(dve_done, own.up())
            v.tensor_scalar(tri, iota[:, 0:P], iota_p[:, :], None, ALU.is_gt).then_inc(dve_done, own.up())
            dve.wait_ge(dve_done, own.count())
            v.tensor_scalar(tmp_s[:, 0, 0:P], ones[:, :], iota_p[:, :], None, ALU.mult).then_inc(dve_done, own.up())
            dve.wait_ge(dve_done, own.count())
            v.tensor_scalar(ones_rest[:, :], tmp_s[:, 0, 0:P], float(NREST), None, ALU.is_lt).then_inc(dve_done, own.up())
            for k in range(6):
                dve.wait_ge(ev(f"couples.in{k}"), at(f"couples.in{k}", 16))
            v.tensor_copy(couple_f[:, :, :, :], couple_i[:, :, :, :]).then_inc(dve_done, own.up())
            for k in range(6):
                dve.wait_ge(ev(f"rows.in{k}"), at(f"rows.in{k}", 16))
            v.tensor_copy(row_f[:, :, :, :], row_i[:, :, :, :]).then_inc(dve_done, own.up())
            dve.wait_ge(dve_done, own.count())
            v.scalar_tensor_tensor(row_key, row_f[:, 2, :, :], float(KEYSTEP), row_f[:, 0, :, :], ALU.mult, ALU.add).then_inc(dve_done, own.up())
            for c in range(NCH):
                v.tensor_scalar(spread[:, 1, c, :], ones[:, :], tile_no[:, c:c + 1], None, ALU.mult).then_inc(dve_done, own.up())

            def step_list(n, meanwhile=lambda: None):
                nm = f"list{n}"
                shift, nb, cols, width, nch, count = ((7, NB, CA, WA, NCCH, NC), (5, NBB, SB, WB, NCH, NT))[n]
                lanes_i = (couple_i, row_i)[n]
                for a, lane in ((0, 0), (1, (2 * P, P)[n] - 1)):
                    v.tensor_scalar(tci[:, a, 0:nch], lanes_i[:, 0, :, lane], shift, None, ALU.arith_shift_right).then_inc(dve_done, own.up())
                dve.wait_ge(dve_done, own.count())
                v.tensor_copy(tc[:, 0:2, 0:nch], tci[:, :, 0:nch]).then_inc(dve_done, own.up())
                v.tensor_scalar(tc[:, 5, :], tile_no[:, :], float(count), None, ALU.is_lt).then_inc(dve_done, own.up())
                v.memset(tc[:, 3, 0:1], 0.0).then_inc(dve_done, own.up())
                dve.wait_ge(dve_done, own.count())
                v.tensor_scalar(tc[:, 0:2, 0:nch], tc[:, 0:2, 0:nch], float(nb - 1), None, ALU.min).then_inc(dve_done, own.up())
                dve.wait_ge(dve_done, own.count())
                v.tensor_tensor(tc[:, 4, 0:nch], tc[:, 1, 0:nch], tc[:, 0, 0:nch], ALU.subtract).then_inc(dve_done, own.up())
                dve.wait_ge(dve_done, own.count())
                v.scalar_tensor_tensor(tc[:, 2, 0:nch], tc[:, 4, 0:nch], 1.0, tc[:, 5, 0:nch], ALU.add, ALU.mult).then_inc(dve_done, own.up())
                for c in range(1, nch):
                    dve.wait_ge(dve_done, own.count())
                    v.tensor_tensor(tc[:, 3, c:c + 1], tc[:, 3, c - 1:c], tc[:, 2, c - 1:c], ALU.add).then_inc(dve_done, own.up())
                dve.wait_ge(dve_done, own.count())
                dve.sem_inc(ev(nm + ".counts"), 1)
                dve.wait_ge(ev(nm + ".starts"), at(nm + ".starts", 1))
                v.tensor_copy(tc[:, 6, 0:nch], bank[0][:, 0:nch]).then_inc(dve_done, own.up())
                dve.wait_ge(dve_done, own.count())
                v.tensor_tensor(tc[:, 7, 0:nch], tc[:, 6, 0:nch], tc[:, 2, 0:nch], ALU.add).then_inc(dve_done, own.up())
                v.tensor_tensor(tc[:, 4, 0:nch], tc[:, 0, 0:nch], tc[:, 6, 0:nch], ALU.subtract).then_inc(dve_done, own.up())
                dve.wait_ge(dve_done, own.count())
                for c in range(nch):
                    v.tensor_scalar(hit[:, c, 0:cols], iota[:, 0:cols], tc[:, 6, c:c + 1], None, ALU.is_ge).then_inc(dve_done, own.up())
                    v.tensor_scalar(spread[:, 0, c, :], ones[:, :], tc[:, 4, c:c + 1], None, ALU.mult).then_inc(dve_done, own.up())
                dve.wait_ge(dve_done, own.count())
                for c in range(nch):
                    v.scalar_tensor_tensor(hit[:, c, 0:cols], iota[:, 0:cols], tc[:, 7, c:c + 1], hit[:, c, 0:cols], ALU.is_lt, ALU.mult).then_inc(dve_done, own.up())
                dve.wait_ge(dve_done, own.count())
                dve.sem_inc(ev(nm + ".hits"), 1)
                meanwhile()
                if n == 0:
                    a, b, c = tmp_s[:, 0, 0:cols], tmp_s[:, 1, 0:cols], tmp_s[:, 2, 0:cols]
                    dve.wait_ge(ev(nm + ".picked"), at(nm + ".picked", 1))
                    valid = bank[1][:, cols:2 * cols]

                    def by_couple(t):
                        return t[:, 0:2 * cols].rearrange("p (u g) -> p g u", u=2)
                    v.tensor_tensor(a, valid, iota[:, 0:cols], ALU.mult).then_inc(dve_done, own.up())
                    v.tensor_scalar(c, valid, -FAR, FAR, ALU.mult, ALU.add).then_inc(dve_done, own.up())
                    dve.wait_ge(dve_done, own.count())
                    v.tensor_tensor(b, bank[1][:, 0:cols], a, ALU.add).then_inc(dve_done, own.up())
                    v.tensor_copy(srcA[:, 0:SA].rearrange("p (g u) -> p g u", u=2), by_couple(bank[3])).then_inc(dve_done, own.up())
                    dve.wait_ge(dve_done, own.count())
                    v.tensor_copy(blkA[:, 0:CA], b).then_inc(dve_done, own.up())
                    v.scalar_tensor_tensor(a, b, -float(width), c, ALU.mult, ALU.add).then_inc(dve_done, own.up())
                    dve.wait_ge(dve_done, own.count())
                    v.tensor_tensor(locA[:, 0:SA].rearrange("p (g u) -> p g u", u=2), by_couple(bank[2]),
                                    a.rearrange("p (g u) -> p g u", u=1).broadcast_to([P, cols, 2]), ALU.add).then_inc(dve_done, own.up())
                    dve.wait_ge(dve_done, own.count())
                    dve.sem_inc(ev(nm + ".made"), 1)
                    for u in range(2):
                        v.tensor_tensor(rel_hot.rearrange("p (g u) r -> p g u r", u=2)[:, :, u, :],
                                        bank[4][:, u * cols:(u + 1) * cols].rearrange("p (s a) -> p s a", a=1).broadcast_to([P, cols, R]),
                                        iota[:, 0:R].rearrange("p (a r) -> p a r", a=1).broadcast_to([P, cols, R]), ALU.is_equal).then_inc(dve_done, own.up())
                    dve.wait_ge(dve_done, own.count())
                    dve.sem_inc(ev(nm + ".read"), 1)
                    return
                hw = cols // 2
                for hf in range(2):
                    dve.wait_ge(ev(nm + ".picked"), at(nm + ".picked", hf + 1))
                    w = slice(hf * hw, (hf + 1) * hw)
                    a, b, c = tmp_s[:, 0, 0:hw], tmp_s[:, 1, 0:hw], tmp_s[:, 2, 0:hw]
                    v.tensor_tensor(a, bank[2][:, 0:hw], iota[:, w], ALU.mult).then_inc(dve_done, own.up())
                    v.tensor_scalar(c, bank[2][:, 0:hw], -FAR, FAR, ALU.mult, ALU.add).then_inc(dve_done, own.up())
                    dve.wait_ge(dve_done, own.count())
                    v.tensor_tensor(b, bank[1][:, 0:hw], a, ALU.add).then_inc(dve_done, own.up())
                    v.tensor_tensor(c, bank[3][:, 0:hw], c, ALU.add).then_inc(dve_done, own.up())
                    v.tensor_copy(srcB[:, w], bank[4][:, 0:hw]).then_inc(dve_done, own.up())
                    dve.wait_ge(dve_done, own.count())
                    v.tensor_copy(blkB[:, w], b).then_inc(dve_done, own.up())
                    v.scalar_tensor_tensor(locB[:, w], b, -float(width), c, ALU.mult, ALU.add).then_inc(dve_done, own.up())
                    v.tensor_copy(tileB[:, w], bank[5][:, 0:hw]).then_inc(dve_done, own.up())
                    dve.wait_ge(dve_done, own.count())
                    dve.sem_inc(ev(nm + ".read"), 1)
                dve.sem_inc(ev(nm + ".made"), 1)

            def normalise(name, t, src_t, relu=True):
                start = own.count()
                with dve.Fori(0, NB // 5) as i:
                    for k in range(5):
                        v.bn_stats(stats[:, bass.ds(5 * i + k, 1), :].rearrange("p a c -> p (a c)"),
                                   src_t[:, bass.ds(5 * i + k, 1), :].rearrange("p a f -> p (a f)")).then_inc(dve_done, 1)
                own.at(start + NB)
                dve.wait_ge(dve_done, own.count())
                even, odd = ([stats[:, :, 3 * a + b] for b in range(3)] for a in range(2))
                v.tensor_tensor(st[:, 0, :], even[1], odd[1], ALU.add).then_inc(dve_done, own.up())
                v.tensor_tensor(st[:, 1, :], even[1], odd[1], ALU.subtract).then_inc(dve_done, own.up())
                v.tensor_tensor(st[:, 3, :], even[2], odd[2], ALU.add).then_inc(dve_done, own.up())
                dve.wait_ge(dve_done, own.count())
                v.tensor_scalar(st[:, 0, :], st[:, 0, :], 0.5, None, ALU.mult).then_inc(dve_done, own.up())
                v.tensor_tensor(st[:, 1, :], st[:, 1, :], st[:, 1, :], ALU.mult).then_inc(dve_done, own.up())
                dve.wait_ge(dve_done, own.count())
                v.scalar_tensor_tensor(st[:, 1, :], st[:, 1, :], D / 4.0, st[:, 3, :], ALU.mult, ALU.add).then_inc(ev(name + ".var"), 1)
                v.tensor_tensor(t, src_t, per_node(st[:, 0, :]), ALU.subtract).then_inc(dve_done, own.up())
                dve.wait_ge(ev(name + ".root"), at(name + ".root", 1))
                v.reciprocal(st[:, 3, :], st[:, 2, :]).then_inc(dve_done, own.up())
                dve.wait_ge(dve_done, own.count())
                if relu:
                    v.scalar_tensor_tensor(t, t, 0.0, per_node(st[:, 3, :]), ALU.max, ALU.mult).then_inc(ev(name + ".ready"), 1)
                else:
                    v.tensor_tensor(t, t, per_node(st[:, 3, :]), ALU.mult).then_inc(dve_done, own.up())
                    dve.wait_ge(dve_done, own.count())

            def per_node(cols):
                return cols.rearrange("p (b a) -> p b a", a=1).broadcast_to([P, NB, D])

            def per_feature(row):
                return row.rearrange("p (a f) -> p a f", a=1).broadcast_to([P, NB, D])

            def add_up(ph, acc, blks, width, h, par, k):
                per = len(blks)
                done = (per * h + k + 1) * (H8 // per)
                dve.wait_ge(ev(ph + ".step_done"), at(ph + ".step_done", 16 + done))
                dve.wait_ge(ev(ph + ".added"), at(ph + ".added", 8 + per * h + k))
                a = acc[:, bass.ds(blks[k] * width, width)]
                v.tensor_tensor(a, bank[(per * par + k) % 8][:, 0:width], a, ALU.add).then_inc(ev(ph + ".added"), 1)

            def begin(ph):
                dve.wait_ge(dve_done, own.count())
                dve.sem_inc(ev(ph + ".start"), 1)

            def hot(ph, h, par, g):
                dve.wait_ge(ev(ph + ".step_done"), at(ph + ".step_done", H8 * h + 2 * g + 2))
                s = par * H8 + 2 * g
                v.tensor_tensor(ring_oh[:, s:s + 2, :], iota[:, 0:P].rearrange("p (a f) -> p a f", a=1).broadcast_to([P, 2, P]),
                                locA[:, bass.ds(H8 * h + 2 * g, 2)].rearrange("p (a b) -> p a b", b=1).broadcast_to([P, 2, P]), ALU.is_equal)\
                    .then_inc(ev(ph + ".hot_made"), 1)

            def woven(ph, acc, tab, top, width, per, produce):
                dve.sem_inc(ev(ph + ".added"), 8)
                last = halves_of[ph] - 1

                def half(h, r, par):
                    blks = registers(dve, tab, h - 1, top, per)
                    for k in range(per):
                        add_up(ph, acc, blks, width, h - 1, 1 - par, k)
                        produce(h, r, par, k)
                for k in range(per):
                    produce(0, 0, 0, k)
                with dve.Fori(0, last // 2) as i:
                    half(2 * i + 1, i, 1)
                    half(2 * i + 2, i + 1, 0)
                if last % 2:
                    half(last, last // 2, 1)
                blks = registers(dve, tab, last, top, per)
                for k in range(per):
                    add_up(ph, acc, blks, width, last, last % 2, k)
                dve.wait_ge(ev(ph + ".added"), at(ph + ".added", 8 + per * halves_of[ph]))

            def plain_phase(ph, acc, width):
                woven(ph, acc, blkA, NB, width, H4, lambda h, i, par, g: hot(ph, h, par, g))


            def first_norm():
                for k in range(2):
                    dve.wait_ge(ev(f"x.in{k}"), at(f"x.in{k}", 16))
                normalise("ln0", H[:, :, :], X[:, :, :])
            step_list(0, first_norm)
            begin("sum")
            step_list(1)
            plain_phase("sum", arena, A0)
            v.tensor_tensor(X[:, :, :], X[:, :, :], acc0[:, :, 0:D], ALU.add).then_inc(dve_done, own.up())
            v.tensor_reduce(dis[:, :], acc0[:, :, D:D + R], AX.X, ALU.add).then_inc(dve_done, own.up())
            v.tensor_scalar(inv_cnt[:, :, :], acc0[:, :, D:D + R], 1.0, None, ALU.max).then_inc(dve_done, own.up())
            dve.wait_ge(dve_done, own.count())
            v.reciprocal(inv_cnt[:, :, :], inv_cnt[:, :, :]).then_inc(dve_done, own.up())
            dve.wait_ge(dve_done, own.count())
            dve.sem_inc(ev("arena_free"), 1)

            normalise("ln1", H[:, :, :], X[:, :, :])
            for l, ph in enumerate(("rel0", "rel1")):
                v.memset(scratch, 0.0).then_inc(dve_done, own.up())
                begin(ph)
                dve.wait_ge(ev(ph + ".zeroed"), at(ph + ".zeroed", 1))

                def produce(h, i, par, k):
                    s = par * H8 + k
                    step = H8 * h + k
                    dve.wait_ge(ev(ph + ".step_done"), at(ph + ".step_done", step + 1))
                    v.tensor_scalar(ring_oh2[:, s, :], iota_key[:, :, :].rearrange("p r n -> p (r n)"), locB[:, bass.ds(step, 1)], None, ALU.is_equal)\
                        .then_inc(ev(ph + ".hot_made"), 1)
                    dve.wait_ge(gath[s], gathers_seen(ph, i + 1, par))
                    dve.wait_ge(xe_in[s], edge_rows_seen(ph, i + 1, par))
                    v.tensor_tensor(ring_xe[:, s, :], ring_g[:, s, :], ring_xe[:, s, :], ALU.add).then_inc(ev(ph + ".msg_sum"), 1)
                woven(ph, acc1, blkB, NBB, SEG, H8, produce)
                for j in range(3):
                    dve.wait_ge(ev(f"{ph}.row{j}"), at(f"{ph}.row{j}", 16))
                for j in range(2):
                    v.tensor_copy(parts[j][:, R + 1, :], rows[:, 0, :]).then_inc(dve_done, own.up())
                start = own.count()

                def node_block(n, i, par):
                    own.at(start + 2 * n)
                    dve.wait_ge(ev(ph + ".proj_done"), at(ph + ".proj_done", n + 1))
                    for j in range(2):
                        v.tensor_tensor(parts[par][:, 4 * j:4 * j + 4, :], bank[1 + 3 * par + j][:, :].rearrange("p (r f) -> p r f", r=4),
                                        inv_cnt[:, bass.ds(n, 1), 4 * j:4 * j + 4].rearrange("p a (r b) -> p (a r) b", b=1).broadcast_to([P, 4, D]), ALU.mult)\
                            .then_inc(dve_done, own.up())
                    dve.wait_ge(dve_done, own.count())
                    dve.wait_ge(ev(ph + ".root_copied"), at(ph + ".root_copied", n + 1))
                    v.tensor_reduce(Y[:, bass.ds(n, 1), :].rearrange("p a f -> p (a f)"), parts[par].rearrange("p r f -> p f r"), AX.X, ALU.add)\
                        .then_inc(ev(ph + ".proj_read"), 1)
                halves(dve, NB, node_block)
                own.at(start + 2 * NB)
                dve.wait_ge(ev(ph + ".proj_read"), at(ph + ".proj_read", NB))
                v.tensor_reduce(block_sum[:, :], Y[:, 0:NB - 1, :].rearrange("p b f -> p f b"), AX.X, ALU.add).then_inc(ev(ph + ".blocks_summed"), 1)
                dve.wait_ge(ev(ph + ".mean_sum"), at(ph + ".mean_sum", 1))
                v.tensor_scalar(small[:, 256:384], bank[5][:, 0:D], 1.0 / N, None, ALU.mult).then_inc(dve_done, own.up())
                dve.wait_ge(dve_done, own.count())
                v.tensor_tensor(Y[:, :, :], Y[:, :, :], per_feature(small[:, 256:384]), ALU.subtract).then_inc(ev(ph + ".centred"), 1)
                dve.wait_ge(ev(ph + ".squared"), at(ph + ".squared", 1))
                v.tensor_reduce(block_sum[:, :], scratch[:, 0:NB - 1, :].rearrange("p b f -> p f b"), AX.X, ALU.add).then_inc(ev(ph + ".blocks_summed"), 1)
                dve.wait_ge(ev(ph + ".var_sum"), at(ph + ".var_sum", 1))
                v.tensor_copy(small[:, 0:128], bank[5][:, 0:D]).then_inc(ev(ph + ".var"), 1)
                dve.wait_ge(ev(ph + ".root"), at(ph + ".root", 1))
                v.reciprocal(small[:, 384:512], small[:, 128:256]).then_inc(dve_done, own.up())
                dve.wait_ge(dve_done, own.count())
                v.tensor_tensor(small[:, 384:512], small[:, 384:512], rows[:, 1, :], ALU.mult).then_inc(dve_done, own.up())
                dve.wait_ge(dve_done, own.count())
                v.tensor_tensor(Y[:, :, :], Y[:, :, :], per_feature(small[:, 384:512]), ALU.mult).then_inc(dve_done, own.up())
                dve.wait_ge(dve_done, own.count())
                v.tensor_tensor(Y[:, :, :], Y[:, :, :], per_feature(rows[:, 2, :]), ALU.add).then_inc(dve_done, own.up())
                dve.wait_ge(dve_done, own.count())
                if l == 0:
                    v.tensor_scalar(H[:, :, :], Y[:, :, :], 0.0, None, ALU.max).then_inc(ev("rel0.over"), 1)
                else:
                    v.tensor_tensor(X[:, :, :], X[:, :, :], Y[:, :, :], ALU.add).then_inc(ev("rel1.over"), 1)
            dve.wait_ge(ev("rel1.over"), at("rel1.over", 1))

            normalise("ln2", H[:, :, :], X[:, :, :])
            v.tensor_scalar(st[:, 1, :], dis[:, :], 1.0, None, ALU.add).then_inc(dve_done, own.up())
            dve.wait_ge(dve_done, own.count())
            v.tensor_copy(st[:, 3, :], st[:, 1, :]).then_inc(ev("deg.made"), 1)
            dve.wait_ge(ev("deg.root"), at("deg.root", 1))
            v.reciprocal(dis[:, :], st[:, 2, :]).then_inc(dve_done, own.up())
            dve.wait_ge(dve_done, own.count())

            start = own.count()

            def scaled_block(n, i, par):
                own.at(start + n)
                dve.wait_ge(ev("gcn.proj_done"), at("gcn.proj_done", n + 1))
                v.tensor_scalar(acc2[:, bass.ds(n, 1), :].rearrange("p a f -> p (a f)"), bank[1 + 3 * par][:, 0:D], dis[:, bass.ds(n, 1)], None, ALU.mult)\
                    .then_inc(dve_done, own.up())
                v.tensor_scalar(y2[:, bass.ds(n, 1), :].rearrange("p a f -> p (a f)"), bank[1 + 3 * par][:, 0:D], dis[:, bass.ds(n, 1)], None, ALU.mult)\
                    .then_inc(ev("gcn.proj_read"), 1)
            halves(dve, NB, scaled_block)
            own.at(start + NB)
            dve.wait_ge(ev("gcn.proj_read"), at("gcn.proj_read", NB))
            dve.sem_inc(ev("gcn.table_made"), 1)
            begin("gcn")
            plain_phase("gcn", arena, D)
            for j in range(3):
                dve.wait_ge(ev(f"gcn.row{j}"), at(f"gcn.row{j}", 16))
            v.tensor_tensor(Y[:, :, :], acc2, per_node(dis[:, :]), ALU.mult).then_inc(dve_done, own.up())
            dve.wait_ge(dve_done, own.count())
            v.tensor_tensor(Y[:, :, :], Y[:, :, :], per_feature(rows[:, 0, :]), ALU.add).then_inc(dve_done, own.up())
            dve.wait_ge(dve_done, own.count())
            v.tensor_tensor(Y[:, :, :], Y[:, :, :], H[:, :, :], ALU.add).then_inc(dve_done, own.up())
            dve.wait_ge(dve_done, own.count())
            normalise("gcn_ln", Y[:, :, :], Y[:, :, :], relu=False)
            v.tensor_tensor(Y[:, :, :], Y[:, :, :], per_feature(rows[:, 1, :]), ALU.mult).then_inc(dve_done, own.up())
            dve.wait_ge(dve_done, own.count())
            v.tensor_tensor(Y[:, :, :], Y[:, :, :], per_feature(rows[:, 2, :]), ALU.add).then_inc(dve_done, own.up())
            dve.wait_ge(dve_done, own.count())
            v.scalar_tensor_tensor(X[:, :, :], Y[:, :, :], 0.0, X[:, :, :], ALU.max, ALU.add).then_inc(ev("gcn.over"), 1)
            dve.wait_ge(ev("gcn.over"), at("gcn.over", 1))

            normalise("ln3", H[:, :, :], X[:, :, :])
            for l, ph in enumerate(("att0", "att1")):
                nh = (4, 1)[l]
                ch = D // nh
                q4, q8 = H4 * nh, H8 * nh
                aw = D + nh
                rw = aw + nh + 1
                rhs = rhs3[:, 0:H8 * rw].rearrange("p (s f) -> p s f", s=H8)
                acc = acc3[:, 0:NB * aw]
                part = part_all[:, 0:2 * H4 * aw].rearrange("p (s f) -> p s f", s=2 * H4)
                dif = fl[:, 0:q8]
                ab = [fl[:, 256 + 32 * j:256 + 32 * j + 2 * q4] for j in range(2)]
                logits = fl[:, 128:128 + q8]
                firsts = fl[:, 448:448 + q8]
                pres, mnew = fl[:, 320:320 + H4], fl[:, 336:336 + q4]
                mold, mstep, both_max = fl[:, 384:384 + q4], fl[:, 384 + q4:384 + 2 * q4], fl[:, 384:384 + 2 * q4]
                keyT, reset, fwd = keyT_all[0:q4, :], reset_all[0:q4, 0:2 * P + 1], fwd_all[0:q4, :]
                largest = largest_all[0:q4, :]
                for j in range(4):
                    dve.wait_ge(ev(f"{ph}.b{j}"), at(f"{ph}.b{j}", 16))
                start = own.count()

                def biased_block(n, i, par):
                    own.at(start + 2 * n)
                    pb = bank[1 + 3 * par]
                    dve.wait_ge(ev(ph + ".proj_done"), at(ph + ".proj_done", n + 1))
                    v.tensor_tensor(qt[:, bass.ds(D * n, D)], pb[:, 0:D], bqkvs[:, 0:D], ALU.add).then_inc(dve_done, own.up())
                    v.tensor_tensor(kvt[:, bass.ds(n, 1), :].rearrange("p a f -> p (a f)"), pb[:, D:3 * D], bqkvs[:, D:3 * D], ALU.add)\
                        .then_inc(dve_done, own.up())
                    v.tensor_tensor(skip[:, bass.ds(n, 1), :].rearrange("p a f -> p (a f)"), pb[:, 3 * D:4 * D], bqkvs[:, 3 * D:4 * D], ALU.add)\
                        .then_inc(ev(ph + ".proj_read"), 1)
                halves(dve, NB, biased_block)
                own.at(start + 2 * NB)
                dve.wait_ge(dve_done, own.count())
                dve.wait_ge(ev(ph + ".proj_read"), at(ph + ".proj_read", NB))
                dve.sem_inc(ev(ph + ".table_made"), 1)
                if l == 1:
                    v.tensor_tensor(skip, skip, X[:, :, :], ALU.add).then_inc(dve_done, own.up())
                v.memset(acc, 0.0).then_inc(dve_done, own.up())
                v.memset(mst[:, 0:NB * nh], -BIG).then_inc(dve_done, own.up())
                v.memset(reset[:, 0:1], -BIG).then_inc(dve_done, own.up())
                v.memset(reset[:, 2 * P:2 * P + 1], -BIG).then_inc(dve_done, own.up())
                begin(ph)

                def make_logits(h, i, par):
                    for j in range(2):
                        dve.wait_ge(ev(ph + ".q_done"), at(ph + ".q_done", 2 * h + j + 1))
                        for k in range(4):
                            dve.wait_ge(gath[par * H8 + 4 * j + k], gathers_seen(ph, i + 1, par))
                        v.tensor_tensor(prod[:, 4 * j:4 * j + 4, :], bank[2 + j][:, :].rearrange("p (s f) -> p s f", s=4),
                                        ring_kv[:, par * H8 + 4 * j:par * H8 + 4 * j + 4, 0:D], ALU.mult).then_inc(dve_done, own.up())
                    dve.wait_ge(dve_done, own.count())
                    for u in range(2):
                        v.tensor_reduce(logits[:, u * q4:(u + 1) * q4].rearrange("p (g a) -> p g a", a=nh),
                                        prod.rearrange("p (g u) (a c) -> p g u a c", u=2, a=nh)[:, :, u, :, :], AX.X, ALU.add).then_inc(ev(ph + ".logits"), 1)

                def run_maxima(h, n):
                    if n == 0:
                        dve.wait_ge(ev(ph + ".keyT_made"), at(ph + ".keyT_made", h + 1))
                        v.tensor_tensor(reset[:, 1:2 * P], keyT[:, 0:2 * P - 1], keyT[:, 1:2 * P], ALU.subtract).then_inc(dve_done, own.up())
                    else:
                        dve.wait_ge(dve_done, own.marked)
                    if n == 1:
                        v.tensor_tensor_scan(fwd, reset[:, 0:2 * P], bank[4][0:q4, 0:2 * P], -BIG, ALU.add, ALU.max).then_inc(dve_done, own.up())
                    if n == 2:
                        v.tensor_tensor_scan(largest[:, ::-1], reset[:, 1:2 * P + 1][:, ::-1], fwd[:, ::-1], -BIG, ALU.add, ALU.max).then_inc(ev(ph + ".max_made"), 1)
                    own.marked = own.count()

                def subtract_maxima(h):
                    dve.wait_ge(ev(ph + ".maxT"), at(ph + ".maxT", h + 1))
                    v.tensor_tensor(dif, logits, bank[7][:, 0:q8], ALU.subtract).then_inc(ev(ph + ".diff"), 1)
                    marks = rhs.rearrange("p (g u) f -> p g u f", u=2)
                    run_max, first = (bank[7][:, j * q8:(j + 1) * q8].rearrange("p (u g a) -> p g u a", u=2, a=nh) for j in range(2))
                    v.tensor_scalar(firsts, bank[7][:, q8:2 * q8], 0.0, None, ALU.is_lt).then_inc(dve_done, own.up())
                    v.tensor_scalar(marks[:, :, :, aw + nh], first[:, :, :, 0], 0.0, None, ALU.is_lt).then_inc(dve_done, own.up())
                    dve.wait_ge(dve_done, own.count())
                    v.tensor_tensor(marks[:, :, :, aw:aw + nh], run_max, firsts.rearrange("p (u g a) -> p g u a", u=2, a=nh), ALU.mult)\
                        .then_inc(ev(ph + ".marked"), 1)

                def weigh_values(h, par):
                    heads = rhs[:, :, 0:aw].rearrange("p s (a c) -> p s a c", a=nh)
                    dve.wait_ge(ev(ph + ".exped"), at(ph + ".exped", h + 1))
                    v.tensor_tensor(heads[:, :, :, 0:ch], ring_kv[:, par * H8:par * H8 + H8, D:2 * D].rearrange("p s (a c) -> p s a c", a=nh),
                                    heads[:, :, :, ch:ch + 1].broadcast_to([P, H8, nh, ch]), ALU.mult).then_inc(ev(ph + ".rhs_made"), 1)

                def new_maxima(h):
                    dve.wait_ge(ev(ph + ".step_done"), at(ph + ".step_done", 16 + H8 * h + H8))
                    for j in range(2):
                        m = min(3, H4 - 3 * j)
                        v.tensor_scalar(pres[:, 3 * j:3 * j + m], bank[5 + j][:, 0:m * rw].rearrange("p (s f) -> p s f", s=m)[:, :, rw - 1],
                                        BIG, -BIG, ALU.mult, ALU.add).then_inc(dve_done, own.up())
                    dve.wait_ge(dve_done, own.count())
                    for j in range(2):
                        m = min(3, H4 - 3 * j)
                        v.tensor_tensor(mstep[:, 3 * j * nh:(3 * j + m) * nh].rearrange("p (s a) -> p s a", a=nh),
                                        bank[5 + j][:, 0:m * rw].rearrange("p (s f) -> p s f", s=m)[:, :, aw:aw + nh],
                                        pres[:, 3 * j:3 * j + m].rearrange("p (s a) -> p s a", a=1).broadcast_to([P, m, nh]), ALU.add)\
                            .then_inc(dve_done, own.up())

                def merge_maximum(k, blks, last):
                    state = mst[:, bass.ds(blks[k] * nh, nh)]
                    dve.wait_ge(dve_done, last)
                    v.tensor_scalar(mold[:, k * nh:(k + 1) * nh], state, 1.0, None, ALU.mult).then_inc(dve_done, own.up())
                    v.tensor_tensor(state, state, mstep[:, k * nh:(k + 1) * nh], ALU.max).then_inc(dve_done, own.up())
                    return own.count()

                def new_top(before):
                    dve.wait_ge(dve_done, before)
                    v.tensor_tensor(mnew, mold, mstep, ALU.max).then_inc(dve_done, own.up())
                    return own.count()

                def rise(par, top):
                    dve.wait_ge(dve_done, top)
                    v.tensor_tensor(ab[par].rearrange("p (b s) -> p b s", b=2), both_max.rearrange("p (b s) -> p b s", b=2),
                                    mnew.rearrange("p (b s) -> p b s", b=1).broadcast_to([P, 2, q4]), ALU.subtract).then_inc(ev(ph + ".resc"), 1)

                def scale_sums(h, par, k, blks, last):
                    if nh == 1:
                        return last
                    if k == 0:
                        dve.wait_ge(ev(ph + ".resc_exped"), at(ph + ".resc_exped", h + 1))
                    a3 = acc[:, bass.ds(blks[k] * aw, aw)].rearrange("p (a c) -> p a c", a=nh)
                    dve.wait_ge(dve_done, last)
                    v.tensor_tensor(a3, a3, ab[par][:, k * nh:(k + 1) * nh].rearrange("p (a b) -> p a b", b=1).broadcast_to([P, nh, ch + 1]), ALU.mult)\
                        .then_inc(dve_done, own.up())
                    return own.count()

                def add_part(h, par, k, blks, last):
                    a = acc[:, bass.ds(blks[k] * aw, aw)]
                    if nh == 1 and k == 0:
                        dve.wait_ge(ev(ph + ".resc_exped"), at(ph + ".resc_exped", h + 1))
                    dve.wait_ge(ev(ph + ".parted"), at(ph + ".parted", H4 * h + k + 1))
                    dve.wait_ge(dve_done, last)
                    if nh > 1:
                        v.tensor_tensor(a, a, part[:, par * H4 + k, :], ALU.add).then_inc(dve_done, own.up())
                    else:
                        v.scalar_tensor_tensor(a, a, ab[par][:, k:k + 1], part[:, par * H4 + k, :], ALU.mult, ALU.add).then_inc(dve_done, own.up())
                    return own.count()

                def sums_merged(last):
                    dve.wait_ge(dve_done, last)
                    dve.sem_inc(ev(ph + ".added"), 1)

                def half(h, i, par):
                    early = h if isinstance(h, int) else 2
                    own.at(start + (0, FIRST, FIRST + SECOND + (h - 2) * PER)[min(early, 2)])
                    make_logits(h, i, par)
                    if early == 0:
                        for k in range(H4):
                            hot(ph, h + 1, 1 - par, k)
                        for n in range(3):
                            run_maxima(h, n)
                    elif early == 1:
                        new = registers(dve, blkA, h - 1, NB, H4)
                        new_maxima(h - 1)
                        m = own.count()
                        for k in range(H4):
                            hot(ph, h + 1, 1 - par, k)
                            m = merge_maximum(k, new, m)
                        run_maxima(h, 0)
                        rise(1 - par, new_top(m))
                        for n in range(1, 3):
                            run_maxima(h, n)
                    else:
                        both = registers(dve, blkA, h - 2, NB, H4, 2)
                        old, new = both[0:H4], both[H4:H8]
                        sums = scale_sums(h - 2, par, 0, old, own.count())
                        hot(ph, h + 1, 1 - par, 0)
                        sums = add_part(h - 2, par, 0, old, sums)
                        hot(ph, h + 1, 1 - par, 1)
                        sums = scale_sums(h - 2, par, 1, old, sums)
                        new_maxima(h - 1)
                        m = own.count()
                        hot(ph, h + 1, 1 - par, 2)
                        m = merge_maximum(0, new, m)
                        sums = add_part(h - 2, par, 1, old, sums)
                        m = merge_maximum(1, new, m)
                        hot(ph, h + 1, 1 - par, 3)
                        m = merge_maximum(2, new, m)
                        run_maxima(h, 0)
                        m = merge_maximum(3, new, m)
                        run_maxima(h, 1)
                        top = new_top(m)
                        sums = scale_sums(h - 2, par, 2, old, sums)
                        rise(1 - par, top)
                        run_maxima(h, 2)
                        sums = add_part(h - 2, par, 2, old, sums)
                        sums = scale_sums(h - 2, par, 3, old, sums)
                    subtract_maxima(h)
                    if early == 2:
                        sums = add_part(h - 2, par, 3, old, sums)
                        sums_merged(sums)
                    weigh_values(h, par)
                    assert own.k == (FIRST, SECOND, PER)[min(early, 2)], own.k

                start = own.count()
                FIRST = 2 + 2 + 2
                SECOND = FIRST + (4 + 2 * H4 + 1)
                PER = SECOND + (2 * H4 if nh > 1 else H4)
                for k in range(H4):
                    hot(ph, 0, 0, k)
                skewed(dve, half)
                own.at(start + FIRST + SECOND + (HALVES_A - 2) * PER)
                both = registers(dve, blkA, HALVES_A - 2, NB, H4, 2)
                old, new = both[0:H4], both[H4:H8]
                sums = own.count()
                new_maxima(HALVES_A - 1)
                m = own.count()
                for k in range(H4):
                    m = merge_maximum(k, new, m)
                rise(1, new_top(m))
                for h, blks in ((HALVES_A - 2, old), (HALVES_A - 1, new)):
                    for k in range(H4):
                        sums = scale_sums(h, h % 2, k, blks, sums)
                        sums = add_part(h, h % 2, k, blks, sums)
                    sums_merged(sums)
                dve.wait_ge(dve_done, own.count())
                a4 = acc.rearrange("p (b a c) -> p b a c", b=NB, a=nh)
                den = small[:, 0:NB * nh].rearrange("p (b a) -> p b a", b=NB)
                v.tensor_scalar(den, a4[:, :, :, ch:ch + 1].rearrange("p b a c -> p b (a c)"), 1e-16, None, ALU.add).then_inc(dve_done, own.up())
                dve.wait_ge(dve_done, own.count())
                v.reciprocal(den, den).then_inc(dve_done, own.up())
                dve.wait_ge(dve_done, own.count())
                y4 = Y[:, :, :].rearrange("p b (a c) -> p b a c", a=nh)
                v.tensor_tensor(y4, a4[:, :, :, 0:ch], small[:, 0:NB * nh].rearrange("p (b a c) -> p b a c", b=NB, c=1).broadcast_to([P, NB, nh, ch]), ALU.mult).then_inc(dve_done, own.up())
                dve.wait_ge(dve_done, own.count())
                if l == 0:
                    v.tensor_tensor(Y[:, :, :], Y[:, :, :], skip, ALU.add).then_inc(dve_done, own.up())
                    dve.wait_ge(dve_done, own.count())
                    v.tensor_scalar(H[:, :, :], Y[:, :, :], 0.0, None, ALU.max).then_inc(ev("att0.over"), 1)
                else:
                    v.tensor_tensor(X[:, :, :], Y[:, :, :], skip, ALU.add).then_inc(ev("att1.over"), 1)


_INS = ["x", "src", "dst", "edge_attr_128", "edge_type_8", "L1_gnn_weight", "L1_gnn_root", "L1_gnn_bias", "L1_gnn_bn_gamma",
        "L1_gnn_bn_beta", "L2_gnn_W", "L2_gnn_b", "L2_gnn_gamma", "L2_gnn_beta",
        "L3_gnn_w1_q", "L3_gnn_b1_q", "L3_gnn_w1_k", "L3_gnn_b1_k", "L3_gnn_w1_v", "L3_gnn_b1_v", "L3_gnn_w1_s", "L3_gnn_b1_s",
        "L3_gnn_w2_q", "L3_gnn_b2_q", "L3_gnn_w2_k", "L3_gnn_b2_k", "L3_gnn_w2_v", "L3_gnn_b2_v", "L3_gnn_w2_s", "L3_gnn_b2_s"]


def kernel(**inputs):
    import numpy as _np
    import concourse.bacc as _bacc
    from concourse import mybir as _mybir
    from concourse.bass_utils import run_bass_kernel_spmd as _run

    nc = _bacc.Bacc("TRN2", target_bir_lowering=False, num_devices=1)
    arrays, args = {}, []
    pads = {"src": 0, "dst": PAD_DST, "edge_type_8": 0, "edge_attr_128": 0}
    for name in _INS:
        a = _np.ascontiguousarray(inputs[name])
        if name in pads:
            rest = _np.full((EP - E,) + a.shape[1:], pads[name], a.dtype)
            a = _np.concatenate([a, rest])
        arrays[f"in_{name}"] = a
        args.append(nc.dram_tensor(f"in_{name}", a.shape, _mybir.dt.from_np(a.dtype), kind="ExternalInput").ap())
    args.append(nc.dram_tensor("h_table", (NP, D), F32).ap())
    args.append(nc.dram_tensor("kv_table", (NP, 2 * D), F32).ap())
    args.append(nc.dram_tensor("out_0", (N, D), F32, kind="ExternalOutput").ap())
    gnn_kernel(nc, *args)
    r = _run(nc, [arrays], core_ids=[0])
    return r.results[0]["out_0"]
```
